# Optimizing a Trainium2 kernel written in Bass

```python
import numpy as np
import jax
import jax.numpy as jnp

def _softmax(x, axis=-1):
    return jax.nn.softmax(x, axis=axis)

def _gelu(x):
    return jax.nn.gelu(x, approximate=True)

def _silu(x):
    return jax.nn.silu(x)

def _sigmoid(x):
    return jax.nn.sigmoid(x)

def _layernorm(x, axis=-1, eps=1e-05):
    m = jnp.mean(x, axis=axis, keepdims=True)
    v = jnp.var(x, axis=axis, keepdims=True)
    return (x - m) / jnp.sqrt(v + eps)

def _scatter_add(tgt, idx, src, axis=0):
    return tgt.at[idx].add(src)

def _segment_sum(src, seg, n):
    return jax.ops.segment_sum(src, seg, n)
kernel_name = 'mk_xattn_ffn_d2_seqx_r8_599935'

def setup_inputs(seed: int=0):
    np.random.seed(seed)
    _w = jnp.asarray

    def _rec_inputs():
        import jax
        import jax.numpy as jnp
        _rk = jax.random.key(seed)
        x = -0.0002928 + 1 * jax.random.normal(jax.random.fold_in(_rk, 1), (2, 512, 128), jnp.float32)
        _lenS = 512 - jax.random.randint(jax.random.fold_in(_rk, 7), (2,), 0, max(1, 512 // 4) + 1, jnp.int32)
        _lenS2 = 154 - jax.random.randint(jax.random.fold_in(_rk, 8), (2,), 0, max(1, 154 // 4) + 1, jnp.int32)
        _ctx_1024P = jax.random.normal(jax.random.fold_in(_rk, 11), (2, 16, 128), jnp.float32)
        _ctx_1024c = jax.random.dirichlet(jax.random.fold_in(_rk, 511), 0.3 * jnp.ones((16,), jnp.float32), (2, 154))
        _ctx_1024t = jnp.einsum('bsk,bkd->bsd', _ctx_1024c, _ctx_1024P)
        _ctx_1024t = _ctx_1024t * jax.lax.rsqrt(jnp.mean(jnp.square(_ctx_1024t)) + 1e-12) * 0.953939
        ctx_1024 = -1.39393e-06 + 0.999914 * (_ctx_1024t + 0.3 * jax.random.normal(jax.random.fold_in(_rk, 611), (2, 154, 128), jnp.float32))
        _validS = jnp.arange(512)[None, :] < _lenS[:, None]
        _validS2 = jnp.arange(154)[None, :] < _lenS2[:, None]
        _causal = jnp.tril(jnp.ones((512, 512), dtype=bool))
        mask_Bx1x1xS2_ik0 = jnp.where(jnp.broadcast_to(_validS2[:, None, None, :], (2, 1, 1, 154)), 0, 1).astype(jnp.int32)
        mask_1x1xSxS2_ik0 = jnp.where(jnp.broadcast_to(_validS2[0:1, None, None, :], (1, 1, 512, 154)), 0, 1).astype(jnp.int32)
        return (x, ctx_1024, mask_Bx1x1xS2_ik0, mask_1x1xSxS2_ik0)
    x, ctx_1024, mask_Bx1x1xS2_ik0, mask_1x1xSxS2_ik0 = _rec_inputs()

    def _L0_xattn_setup():
        import jax, jax.numpy as jnp
        import numpy as np
        E, H = (128, 16)
        N, S, T = (2, 256, 256)
        key = jax.random.key(seed)
        ks = jax.random.split(key, 8)
        scale = 1.0 / np.sqrt(E)
        q = jax.random.normal(ks[0], (N, S, E), dtype=jnp.float32)
        k = jax.random.normal(ks[1], (N, T, E), dtype=jnp.float32)
        v = jax.random.normal(ks[2], (N, T, E), dtype=jnp.float32)
        pad_mask = jax.random.randint(ks[3], (N, 1, 1, T), 0, 2, dtype=jnp.int32)
        subsq_mask = jnp.tril(jnp.ones((S, T), dtype=jnp.int32))[None, None]
        Wq = jax.random.normal(ks[4], (E, E), dtype=jnp.float32) * scale
        Wk = jax.random.normal(ks[5], (E, E), dtype=jnp.float32) * scale
        Wv = jax.random.normal(ks[6], (E, E), dtype=jnp.float32) * scale
        bq = jnp.zeros((E,), dtype=jnp.float32)
        bk = jnp.zeros((E,), dtype=jnp.float32)
        bv = jnp.zeros((E,), dtype=jnp.float32)
        return {'query': q, 'key': k, 'value': v, 'pad_mask': pad_mask, 'subsq_mask': subsq_mask, 'Wq': Wq, 'bq': bq, 'Wk': Wk, 'bk': bk, 'Wv': Wv, 'bv': bv}
    _L0_xattn_all = _L0_xattn_setup()
    _L0_xattn_in = {k: v for k, v in _L0_xattn_all.items() if k in ('Wq', 'bq', 'Wk', 'bk', 'Wv', 'bv')}
    del _L0_xattn_all

    def _L0_ffn_setup():
        import jax, jax.numpy as jnp
        import numpy as np
        DIM = 128
        HEADS = 16
        HD = DIM // HEADS
        M = 32
        E = 4
        K = 2
        HID = 256
        MID = 256
        LB = 0.01
        EPS = 1.1920929e-07

        def _rms(x, w):
            return x * jax.lax.rsqrt(jnp.mean(x * x, axis=-1, keepdims=True) + EPS) * w

        def _gelu(x):
            return jax.nn.gelu(x, approximate=False)
        key = jax.random.key(seed)
        ks = jax.random.split(key, 20)
        d = DIM
        w = lambda k, s: jax.random.normal(k, s, jnp.float32) * 0.02
        return {'x': jax.random.normal(ks[0], (4, 128, d), jnp.float32), 'n1_w': jnp.ones((d,), jnp.float32), 'n2_w': jnp.ones((d,), jnp.float32), 'wq': w(ks[1], (d, d)), 'wk': w(ks[2], (d, d)), 'wv': w(ks[3], (d, d)), 'wo': w(ks[4], (d, d)), 'qn_w': jnp.ones((HD,), jnp.float32), 'kn_w': jnp.ones((HD,), jnp.float32), 'gate_w': w(ks[5], (E, d)), 'e0_up': w(ks[6], (HID, d)), 'e0_down': w(ks[7], (d, HID)), 'e1_w1': w(ks[8], (HID, d)), 'e1_w2': w(ks[9], (HID, d)), 'e1_down': w(ks[10], (d, HID)), 'e2_l1': w(ks[11], (MID, d)), 'e2_l2': w(ks[12], (HID, MID)), 'e2_l3': w(ks[13], (MID, HID)), 'e2_l4': w(ks[14], (d, MID)), 'e3_down': w(ks[15], (d, d)), 'e3_up': w(ks[16], (HID, d)), 'e3_out': w(ks[17], (d, HID))}
    _L0_ffn_all = _L0_ffn_setup()
    _L0_ffn_in = {k: v for k, v in _L0_ffn_all.items() if k in ('n1_w', 'n2_w', 'wq', 'wk', 'wv', 'wo', 'qn_w', 'kn_w', 'gate_w', 'e0_up', 'e0_down', 'e1_w1', 'e1_w2', 'e1_down', 'e2_l1', 'e2_l2', 'e2_l3', 'e2_l4', 'e3_down', 'e3_up', 'e3_out')}
    del _L0_ffn_all

    def _L1_xattn_setup():
        import jax, jax.numpy as jnp
        import numpy as np
        D_MODEL = 128
        N_HEAD = 16
        N_KV_HEAD = 4
        D_K = D_MODEL // N_HEAD
        N_REP = N_HEAD // N_KV_HEAD
        B, S = (2, 256)
        key = jax.random.key(seed)
        ks = jax.random.split(key, 7)
        scale = 1.0 / np.sqrt(D_MODEL)
        return {'q': jax.random.normal(ks[0], (B, S, D_MODEL), jnp.float32), 'k': jax.random.normal(ks[1], (B, S, D_MODEL), jnp.float32), 'v': jax.random.normal(ks[2], (B, S, D_MODEL), jnp.float32), 'W_q': jax.random.normal(ks[3], (D_MODEL, N_HEAD * D_K), jnp.float32) * scale, 'W_k': jax.random.normal(ks[4], (D_MODEL, N_KV_HEAD * D_K), jnp.float32) * scale, 'W_v': jax.random.normal(ks[5], (D_MODEL, N_KV_HEAD * D_K), jnp.float32) * scale, 'W_o': jax.random.normal(ks[6], (D_MODEL, D_MODEL), jnp.float32) * scale}
    _L1_xattn_all = _L1_xattn_setup()
    _L1_xattn_in = {k: v for k, v in _L1_xattn_all.items() if k in ('W_q', 'W_k', 'W_v', 'W_o')}
    del _L1_xattn_all

    def _L1_ffn_setup():
        import jax, jax.numpy as jnp
        import numpy as np
        B, S, D, E, H, K = (4, 256, 128, 8, 64, 2)
        key = jax.random.key(seed)
        ks = jax.random.split(key, 11)
        sc = 0.02
        return {'x': jax.random.normal(ks[0], (B, S, D), dtype=jnp.float32), 'gate_W': jax.random.normal(ks[1], (D, E), dtype=jnp.float32) * sc, 'W1': jax.random.normal(ks[2], (E, D, H), dtype=jnp.float32) * sc, 'b1': jnp.zeros((E, H), dtype=jnp.float32), 'W2': jax.random.normal(ks[3], (E, H, D), dtype=jnp.float32) * sc, 'b2': jnp.zeros((E, D), dtype=jnp.float32), 'Ws1': jax.random.normal(ks[4], (D, H), dtype=jnp.float32) * sc, 'bs1': jnp.zeros((H,), dtype=jnp.float32), 'Ws2': jax.random.normal(ks[5], (H, D), dtype=jnp.float32) * sc, 'bs2': jnp.zeros((D,), dtype=jnp.float32), 'route_scale': jnp.ones((), dtype=jnp.float32)}
    _L1_ffn_all = _L1_ffn_setup()
    _L1_ffn_in = {k: v for k, v in _L1_ffn_all.items() if k in ('gate_W', 'W1', 'b1', 'W2', 'b2', 'Ws1', 'bs1', 'Ws2', 'bs2', 'route_scale')}
    del _L1_ffn_all
    return {'x': x, 'ctx_1024': ctx_1024, 'mask_Bx1x1xS2_ik0': mask_Bx1x1xS2_ik0, 'mask_1x1xSxS2_ik0': mask_1x1xSxS2_ik0, 'L0_xattn_Wq': _L0_xattn_in['Wq'], 'L0_xattn_bq': _L0_xattn_in['bq'], 'L0_xattn_Wk': _L0_xattn_in['Wk'], 'L0_xattn_bk': _L0_xattn_in['bk'], 'L0_xattn_Wv': _L0_xattn_in['Wv'], 'L0_xattn_bv': _L0_xattn_in['bv'], 'L0_ffn_n1_w': _L0_ffn_in['n1_w'], 'L0_ffn_n2_w': _L0_ffn_in['n2_w'], 'L0_ffn_wq': _L0_ffn_in['wq'], 'L0_ffn_wk': _L0_ffn_in['wk'], 'L0_ffn_wv': _L0_ffn_in['wv'], 'L0_ffn_wo': _L0_ffn_in['wo'], 'L0_ffn_qn_w': _L0_ffn_in['qn_w'], 'L0_ffn_kn_w': _L0_ffn_in['kn_w'], 'L0_ffn_gate_w': _L0_ffn_in['gate_w'], 'L0_ffn_e0_up': _L0_ffn_in['e0_up'], 'L0_ffn_e0_down': _L0_ffn_in['e0_down'], 'L0_ffn_e1_w1': _L0_ffn_in['e1_w1'], 'L0_ffn_e1_w2': _L0_ffn_in['e1_w2'], 'L0_ffn_e1_down': _L0_ffn_in['e1_down'], 'L0_ffn_e2_l1': _L0_ffn_in['e2_l1'], 'L0_ffn_e2_l2': _L0_ffn_in['e2_l2'], 'L0_ffn_e2_l3': _L0_ffn_in['e2_l3'], 'L0_ffn_e2_l4': _L0_ffn_in['e2_l4'], 'L0_ffn_e3_down': _L0_ffn_in['e3_down'], 'L0_ffn_e3_up': _L0_ffn_in['e3_up'], 'L0_ffn_e3_out': _L0_ffn_in['e3_out'], 'L1_xattn_W_q': _L1_xattn_in['W_q'], 'L1_xattn_W_k': _L1_xattn_in['W_k'], 'L1_xattn_W_v': _L1_xattn_in['W_v'], 'L1_xattn_W_o': _L1_xattn_in['W_o'], 'L1_ffn_gate_W': _L1_ffn_in['gate_W'], 'L1_ffn_W1': _L1_ffn_in['W1'], 'L1_ffn_b1': _L1_ffn_in['b1'], 'L1_ffn_W2': _L1_ffn_in['W2'], 'L1_ffn_b2': _L1_ffn_in['b2'], 'L1_ffn_Ws1': _L1_ffn_in['Ws1'], 'L1_ffn_bs1': _L1_ffn_in['bs1'], 'L1_ffn_Ws2': _L1_ffn_in['Ws2'], 'L1_ffn_bs2': _L1_ffn_in['bs2'], 'L1_ffn_route_scale': _L1_ffn_in['route_scale']}

def reference(x, ctx_1024, mask_Bx1x1xS2_ik0, mask_1x1xSxS2_ik0, L0_xattn_Wq, L0_xattn_bq, L0_xattn_Wk, L0_xattn_bk, L0_xattn_Wv, L0_xattn_bv, L0_ffn_n1_w, L0_ffn_n2_w, L0_ffn_wq, L0_ffn_wk, L0_ffn_wv, L0_ffn_wo, L0_ffn_qn_w, L0_ffn_kn_w, L0_ffn_gate_w, L0_ffn_e0_up, L0_ffn_e0_down, L0_ffn_e1_w1, L0_ffn_e1_w2, L0_ffn_e1_down, L0_ffn_e2_l1, L0_ffn_e2_l2, L0_ffn_e2_l3, L0_ffn_e2_l4, L0_ffn_e3_down, L0_ffn_e3_up, L0_ffn_e3_out, L1_xattn_W_q, L1_xattn_W_k, L1_xattn_W_v, L1_xattn_W_o, L1_ffn_gate_W, L1_ffn_W1, L1_ffn_b1, L1_ffn_W2, L1_ffn_b2, L1_ffn_Ws1, L1_ffn_bs1, L1_ffn_Ws2, L1_ffn_bs2, L1_ffn_route_scale):
    import jax
    import jax.numpy as jnp

    def _L0_xattn_ref(query, key, value, pad_mask, subsq_mask, Wq, bq, Wk, bk, Wv, bv):
        import jax, jax.numpy as jnp
        import numpy as np
        E, H = (128, 16)
        N, S, T = (2, 256, 256)
        n, s, e = query.shape
        t = value.shape[1]
        d = e // H
        q = (query @ Wq.T + bq).reshape(n, s, H, d).transpose(0, 2, 1, 3)
        k = (key @ Wk.T + bk).reshape(n, t, H, d).transpose(0, 2, 1, 3)
        v = (value @ Wv.T + bv).reshape(n, t, H, d).transpose(0, 2, 1, 3)
        att = jnp.einsum('bhsd,bhtd->bhst', q, k) / jnp.sqrt(jnp.float32(d))
        att = jnp.where(pad_mask == 0, jnp.float32(-1000000000.0), att)
        att = jnp.where(subsq_mask == 0, jnp.float32(-1000000000.0), att)
        prob = jax.nn.softmax(att, axis=-1)
        out = jnp.einsum('bhst,bhtd->bhsd', prob, v)
        return out.transpose(0, 2, 1, 3).reshape(n, s, e)

    def _L0_ffn_ref(x, n1_w, n2_w, wq, wk, wv, wo, qn_w, kn_w, gate_w, e0_up, e0_down, e1_w1, e1_w2, e1_down, e2_l1, e2_l2, e2_l3, e2_l4, e3_down, e3_up, e3_out):
        import jax, jax.numpy as jnp
        import numpy as np
        DIM = 128
        HEADS = 16
        HD = DIM // HEADS
        M = 32
        E = 4
        K = 2
        HID = 256
        MID = 256
        LB = 0.01
        EPS = 1.1920929e-07

        def _rms(x, w):
            return x * jax.lax.rsqrt(jnp.mean(x * x, axis=-1, keepdims=True) + EPS) * w

        def _gelu(x):
            return jax.nn.gelu(x, approximate=False)
        B, T, C = x.shape
        h = _rms(x, n1_w)
        heads = lambda w_: (h @ w_.T).reshape(B, T, HEADS, HD).transpose(0, 2, 1, 3)
        q = _rms(heads(wq), qn_w)
        k = _rms(heads(wk), kn_w)
        v = heads(wv)
        scores = jnp.einsum('bhqd,bhkd->bhqk', q, k) * HD ** (-0.5)
        causal = jnp.tril(jnp.ones((T, T), bool))
        scores = jnp.where(causal[None, None], scores, -jnp.inf)
        attn = jax.nn.softmax(scores, axis=-1)
        ao = jnp.einsum('bhqk,bhkd->bhqd', attn, v).transpose(0, 2, 1, 3).reshape(B, T, C) @ wo.T
        ao = ao.at[:, :, :M].set(0.0)
        x = x + ao
        xf = _rms(x, n2_w).reshape(-1, C)
        N = xf.shape[0]
        logits = jnp.nan_to_num(xf @ gate_w.T)
        probs = jax.nn.softmax(logits, axis=-1)
        topv, topi = jax.lax.top_k(probs, K)
        topv = topv / (topv.sum(-1, keepdims=True) + 1e-08)
        wts = jnp.zeros((N, E), x.dtype).at[jnp.arange(N)[:, None], topi].add(topv)
        o0 = _gelu(xf @ e0_up.T) @ e0_down.T
        o1 = jax.nn.silu(xf @ e1_w1.T) * (xf @ e1_w2.T) @ e1_down.T
        o2 = _gelu(_gelu(_gelu(xf @ e2_l1.T) @ e2_l2.T) @ e2_l3.T) @ e2_l4.T
        o3 = _gelu(_gelu(xf @ e3_down.T) @ e3_up.T) @ e3_out.T
        moe = wts[:, 0:1] * o0 + wts[:, 1:2] * o1 + wts[:, 2:3] * o2 + wts[:, 3:4] * o3
        moe = moe.reshape(B, T, C).at[:, :, :M].set(0.0)
        return x + moe

    def _L1_xattn_ref(q, k, v, W_q, W_k, W_v, W_o):
        import jax, jax.numpy as jnp
        import numpy as np
        D_MODEL = 128
        N_HEAD = 16
        N_KV_HEAD = 4
        D_K = D_MODEL // N_HEAD
        N_REP = N_HEAD // N_KV_HEAD
        B, S = (2, 256)
        batch, seq_q, _ = q.shape
        seq_k = k.shape[1]
        Q = (q @ W_q).reshape(batch, seq_q, N_HEAD, D_K).transpose(0, 2, 1, 3)
        K = (k @ W_k).reshape(batch, seq_k, N_KV_HEAD, D_K).transpose(0, 2, 1, 3)
        V = (v @ W_v).reshape(batch, seq_k, N_KV_HEAD, D_K).transpose(0, 2, 1, 3)
        K = jnp.repeat(K, N_REP, axis=1)
        V = jnp.repeat(V, N_REP, axis=1)
        scores = jnp.einsum('bhqd,bhkd->bhqk', Q, K) / np.sqrt(D_K).astype(jnp.float32)
        attn = jax.nn.softmax(scores, axis=-1)
        out = jnp.einsum('bhqk,bhkd->bhqd', attn, V)
        out = out.transpose(0, 2, 1, 3).reshape(batch, seq_q, D_MODEL)
        return out @ W_o

    def _L1_ffn_ref(x, gate_W, W1, b1, W2, b2, Ws1, bs1, Ws2, bs2, route_scale):
        import jax, jax.numpy as jnp
        import numpy as np
        B, S, D, E, H, K = (4, 256, 128, 8, 64, 2)
        scores = jax.nn.sigmoid(x @ gate_W) * route_scale
        topk_scores, topk_idx = jax.lax.top_k(scores, K)
        topk_w = topk_scores / topk_scores.sum(-1, keepdims=True)
        onehot = jax.nn.one_hot(topk_idx, E, dtype=x.dtype)
        gate_full = jnp.einsum('bsk,bske->bse', topk_w, onehot)
        h = jax.nn.gelu(jnp.einsum('bsd,edh->bseh', x, W1) + b1, approximate=False)
        y = jnp.einsum('bseh,ehd->bsed', h, W2) + b2
        expert_out = jnp.einsum('bse,bsed->bsd', gate_full, y)
        shared = jax.nn.gelu(x @ Ws1 + bs1, approximate=False) @ Ws2 + bs2
        return expert_out + shared
    x = x + _L0_xattn_ref(_layernorm(x, axis=-1), ctx_1024, ctx_1024, mask_Bx1x1xS2_ik0, mask_1x1xSxS2_ik0, L0_xattn_Wq, L0_xattn_bq, L0_xattn_Wk, L0_xattn_bk, L0_xattn_Wv, L0_xattn_bv)
    x = x + _L0_ffn_ref(_layernorm(x, axis=-1), L0_ffn_n1_w, L0_ffn_n2_w, L0_ffn_wq, L0_ffn_wk, L0_ffn_wv, L0_ffn_wo, L0_ffn_qn_w, L0_ffn_kn_w, L0_ffn_gate_w, L0_ffn_e0_up, L0_ffn_e0_down, L0_ffn_e1_w1, L0_ffn_e1_w2, L0_ffn_e1_down, L0_ffn_e2_l1, L0_ffn_e2_l2, L0_ffn_e2_l3, L0_ffn_e2_l4, L0_ffn_e3_down, L0_ffn_e3_up, L0_ffn_e3_out)
    x = x + _L1_xattn_ref(_layernorm(x, axis=-1), ctx_1024, ctx_1024, L1_xattn_W_q, L1_xattn_W_k, L1_xattn_W_v, L1_xattn_W_o)
    x = x + _L1_ffn_ref(_layernorm(x, axis=-1), L1_ffn_gate_W, L1_ffn_W1, L1_ffn_b1, L1_ffn_W2, L1_ffn_b2, L1_ffn_Ws1, L1_ffn_bs1, L1_ffn_Ws2, L1_ffn_bs2, L1_ffn_route_scale)
    return x

_drawn_inputs = setup_inputs


def setup_inputs(seed=0):
    import zlib

    import numpy as np

    out = dict(_drawn_inputs(seed))
    spreads = {'L0_xattn_bq': (0.0, 0.1),
     'L0_xattn_bk': (0.0, 2.0),
     'L0_xattn_bv': (0.0, 0.1),
     'L0_ffn_n1_w': (1.0, 0.6),
     'L0_ffn_n2_w': (1.0, 0.6),
     'L0_ffn_qn_w': (1.0, 0.6),
     'L0_ffn_kn_w': (1.0, 0.6),
     'L1_ffn_b1': (0.0, 0.8),
     'L1_ffn_b2': (0.0, 0.754),
     'L1_ffn_bs1': (0.0, 0.8),
     'L1_ffn_bs2': (0.0, 0.617)}
    factors = {'L0_ffn_wq': 8.0,
     'L0_ffn_wk': 8.0,
     'L0_ffn_wv': 5.65,
     'L0_ffn_wo': 5.332,
     'L0_ffn_gate_w': 8.0,
     'L0_ffn_e0_up': 8.0,
     'L0_ffn_e0_down': 7.961,
     'L0_ffn_e1_w1': 8.0,
     'L0_ffn_e1_w2': 8.0,
     'L0_ffn_e1_down': 8.0,
     'L0_ffn_e2_l1': 8.0,
     'L0_ffn_e2_l2': 8.0,
     'L0_ffn_e2_l3': 8.0,
     'L0_ffn_e2_l4': 8.0,
     'L0_ffn_e3_down': 8.0,
     'L0_ffn_e3_up': 8.0,
     'L0_ffn_e3_out': 8.0,
     'L1_ffn_W1': 8.0,
     'L1_ffn_W2': 8.0,
     'L1_ffn_Ws1': 6.762,
     'L1_ffn_Ws2': 6.293}
    for name, (base, spread) in spreads.items():
        noise = np.random.default_rng([zlib.crc32(name.encode()), seed]).standard_normal(out[name].shape)
        drawn = base * np.exp(spread * noise) if base else spread * noise
        out[name] = jnp.asarray(drawn.astype(out[name].dtype))
    for name, factor in factors.items():
        out[name] = (out[name] * factor).astype(out[name].dtype)
    return out
```

```python
from contextlib import ExitStack

import numpy as np

import concourse.bass as bass
from concourse import mybir

F32 = mybir.dt.float32
BF16 = mybir.dt.bfloat16
I32 = mybir.dt.int32
ALU = mybir.AluOpType
ACT = mybir.ActivationFunctionType
AX = mybir.AxisListType

P = 128
B, S, D = 2, 512, 128
H, HD = 16, 8
KV = 4
SC = 154
KT = 96
CT = (0, SC - KT)
OVER = 2 * KT - SC
NT = B * S // P
TB = S // P
QUADS = H // 4
ITEMS = B * QUADS
STACK = 96
TOP = STACK + 3
NEG = -float(2 ** 100)
FLT_MAX = 3.4028234663852886e38
LN_EPS = 1e-5
RMS_EPS = 1.1920929e-07
KEEP = 32
OC = D - KEEP
E0, E1 = 4, 8
HE = 64

CROSS0, SELF, CROSS1 = range(3)
N_CROSS0, N_SELF, R_SELF, R_FFN0, N_CROSS1, N_FFN1 = range(6)
T_CROSS0, T_SELF, T_FFN0, T_CROSS1, T_FFN1 = range(5)
SP_K0, SP_K1, SP_Q0, SP_SELF, SP_Q1 = 0, 1, 2, 4, 8
N_SPLITS = 10


def columns(names):
    at, cols = 0, {}
    for name, n in names:
        cols[name] = (at, n)
        at += n
    return cols, at


EARLY, N_EARLY = columns([("ctx", B * SC), ("x0_k", D), ("x0_v", D), ("x1_k", KV * HD), ("x1_v", KV * HD), ("x0_q", D)])
LATE, N_LATE = columns([
    ("wq", D), ("wk", D), ("wv", D), ("wo", D), ("gate0", E0),
    ("e1_w1", 2 * D), ("e1_w2", 2 * D), ("e0_up", 2 * D), ("e3_down", D), ("e2_l1", 2 * D), ("e3_up", 2 * D),
    ("e2_l2", 4 * D), ("e2_l3", 4 * D), ("e0_down", 2 * D), ("e1_down", 2 * D), ("e2_l4", 2 * D), ("e3_out", 2 * D),
    ("x1_q", D), ("x1_o", D), ("gate1", E1), ("w1", 4 * D), ("w2", 4 * D), ("ws1", HE)])
CONST, N_CONST = columns([("ident", P), ("head_mean", P), ("causal", P), ("causal_t", P),
                          ("before0", E0 * E0), ("before1", E1 * E1), ("spread", 4 * P)])
VECS = ["x0_bq", "x0_bk", "n1", "n2", "qn", "kn", "b1_0", "b1_1", "b1_2", "b1_3"]

HIDDEN = [
    ("e1_w1", (0,), None, 0, ACT.Silu), ("e1_w1", (1,), None, 1, ACT.Silu),
    ("e1_w2", (0,), None, 0, "times"), ("e1_w2", (1,), None, 1, "times"),
    ("e3_down", (0,), None, 2, ACT.Gelu),
    ("e2_l1", (0,), None, 3, ACT.Gelu), ("e2_l1", (1,), None, 4, ACT.Gelu),
    ("e3_up", (0,), (2,), 5, ACT.Gelu), ("e3_up", (1,), (2,), 6, ACT.Gelu),
    ("e2_l2", (0, 2), (3, 4), 7, ACT.Gelu), ("e2_l2", (1, 3), (3, 4), 8, ACT.Gelu),
    ("e0_up", (0,), None, 9, ACT.Gelu), ("e0_up", (1,), None, 10, ACT.Gelu),
    ("e2_l3", (0, 2), (7, 8), 11, ACT.Gelu), ("e2_l3", (1, 3), (7, 8), 12, ACT.Gelu),
]
OUTPUTS = [("e0_down", (9, 10)), ("e1_down", (0, 1)), ("e2_l4", (11, 12)), ("e3_out", (5, 6))]
N_HIDDEN = len(HIDDEN)
N_TIMES = sum(h[4] == "times" for h in HIDDEN)
N_GELU = N_HIDDEN - N_TIMES
H_BANKS = 4


def gelus_to(k):
    return sum(h[4] != "times" for h in HIDDEN[:k + 1])


def build(nc, early, late, consts, vecs, bs1, ws2, b2, bs2, bv, rscale, pad_mask, sub_mask, x, out):
    with ExitStack() as ctx:
        def sb(name, shape, dt=F32):
            return ctx.enter_context(nc.sbuf_tensor(name, shape, dt))

        def sem(name):
            return ctx.enter_context(nc.semaphore(name))

        def sems(name, n):
            return [sem(f"{name}_{i}") for i in range(n)]

        we = sb("we", [P, N_EARLY])
        wl = sb("wl", [P, N_LATE])
        cst = sb("cst", [P, N_CONST])
        vec = sb("vec", [P, len(VECS)])
        bs1_c = sb("bs1_c", [HE, 1])
        w_tail = sb("w_tail", [P, D])
        bv_b = sb("bv_b", [P, D])
        rs_b = sb("rs_b", [P, 1])
        eps_ln = sb("eps_ln", [P, 1])
        eps_rms = sb("eps_rms", [P, 1])
        msk = sb("msk", [P, B, TB, SC], BF16)
        msk_t = sb("msk_t", [KT, B, 2 * S], BF16)
        ident_b = sb("ident_b", [P, P], BF16)
        causal_b = sb("causal_b", [P, P], BF16)
        causal_tb = sb("causal_tb", [P, P], BF16)
        spread_b = sb("spread_b", [3 * E1, 4 * P], BF16)
        zeros_b = sb("zeros_b", [P, 512], BF16)
        ones_b = sb("ones_b", [P, 512], BF16)
        X = sb("X", [P, NT, D])
        Y = sb("Y", [P, NT, D])
        U = sb("U", [P, NT, D])
        yT = sb("yT", [P, B * S])
        parts = sb("parts", [P, 4, 3, S], BF16)
        QA = sb("QA", [P, B * H * S], BF16)
        KS = sb("KS", [P, B * H * S], BF16)
        K1 = sb("K1", [P, KV, B * SC], BF16)
        VS = sb("VS", [P, NT, H, HD + 1])
        V0 = sb("V0", [KT, B, 2, H, HD + 1])
        V1 = sb("V1", [KT, B, 2, KV, HD + 1])
        PR = sb("PR", [P, 2 * 4 * 1280])
        O = sb("O", [P, ITEMS, S])
        tail = sb("tail", [P, S])
        stats = sb("stats", [P, NT, 6])
        mv = sb("mv", [P, NT, 2])
        sm = sb("sm", [P, 6, NT])
        RSTD, VAR2, RMS, LOGV, GSUM, GINV = range(6)
        rden = sb("rden", [P, 2, H])
        nmax = sb("nmax", [P, 2, 16])
        nres = sb("nres", [P, 2, 16])
        nparts = sb("nparts", [P, 2, 48], BF16)
        nrows = sb("nrows", [48, 2, P], BF16)
        G = sb("G", [P, 6, TB, E1])
        GL = sb("GL", [P, B, TB, E1])
        gnum = sb("gnum", [P, TB, E1], I32)
        GG = sb("GG", [P, 2, TB, E1, E1])
        gparts = sb("gparts", [P, TB, 3, E1], BF16)
        gT = sb("gT", [3 * E1, S], BF16)
        PS = ctx.enter_context(nc.psum_tensor("PS", [P, 8, 512], F32))

        QAv = QA[:, :].rearrange("p (b h s) -> p b h s", b=B, h=H)
        KSv = KS[:, :].rearrange("p (b h s) -> p b h s", b=B, h=H)
        K0 = KS[:, 0:H * B * SC].rearrange("p (h s) -> p h s", h=H)
        PRv = PR[:, :].rearrange("p (i h s) -> p i h s", i=2, h=4)
        HB = PR[:, 0:16 * S].rearrange("p (c s) -> p c s", s=S)
        f32T = PR[:, 0:4 * S].rearrange("p (c s) -> p c s", s=S)
        res = PR[:, 4 * S:6 * S].rearrange("p (c s) -> p c s", s=S)
        sub_f = PR[:, 6 * S:6 * S + TB * SC].rearrange("p (t k) -> p t k", t=TB)
        sub_i = PR[:, 8 * S:8 * S + TB * SC].bitcast(I32).rearrange("p (t k) -> p t k", t=TB)
        pad_i = PR[:, 10 * S:10 * S + B * SC].bitcast(I32).rearrange("p (b k) -> p b k", b=B)
        pad_z = PR[:, 11 * S:11 * S + B * SC].rearrange("p (b k) -> p b k", b=B)
        sq = O[:, 0:2, :]

        def bank(b, rows=P, n=512, at=0):
            return PS[0:rows, b, at:at + n]

        def bank16(b):
            return PS[:, b, :].bitcast(BF16)

        def W(name, chunk=0, n=D):
            src, (at, size) = (we, EARLY[name]) if name in EARLY else (wl, LATE[name])
            n = min(n, size)
            return src[:, at + chunk * n:at + chunk * n + n]

        def C(name):
            at, n = CONST[name]
            return cst[:, at:at + n]

        def V(name):
            i = VECS.index(name)
            return vec[:, i:i + 1]

        ident = C("ident")
        ctxT = we[:, 0:B * SC]

        in_x, in_early, in_const, in_vec = sem("in_x"), sem("in_early"), sem("in_const"), sem("in_vec")
        in_mask, in_late, in_tail = sem("in_mask"), sem("in_late"), sem("in_tail")
        eps_set, consts_cast, pv_cleared = sem("eps_set"), sem("consts_cast"), sem("pv_cleared")
        pool_fills = sem("pool_fills")
        stack_fill = sem("stack_fill")
        ctx_mm, ctx_v = sem("ctx_mm"), sem("ctx_v")
        mask_ready, maskt_mm, maskt_ready = sem("mask_ready"), sem("maskt_mm"), sem("maskt_ready")
        k0_stack, k1_stack = sem("k0_stack"), sem("k1_stack")
        q_stack = [sems(f"q_stack{l}", B) for l in range(3)]
        k_stack = sems("k_stack", B)
        var_ready = sems("var_ready", 6)
        rstd_ready = sems("rstd_ready", 6)
        rows_ready = sems("rows_ready", 5)
        rowsT_mm = sems("rowsT_mm", 5)
        rowsT_ready = sems("rowsT_ready", 5)
        proj_mm = sem("proj_mm")
        f32_ready = sem("f32_ready")
        hi_ready = sem("hi_ready")
        split_ready = sem("split_ready")
        sq_ready, ms_mm, rms_ready = sem("sq_ready"), sem("ms_mm"), sem("rms_ready")
        v_mm, v_ready = sem("v_mm"), sem("v_ready")
        s_mm, s_max = sem("s_mm"), sem("s_max")
        nparts_ready, nrows_mm, nrows_ready = sem("nparts_ready"), sem("nrows_mm"), sem("nrows_ready")
        max_rows = sems("max_rows", 2)
        t_mm, probs = sem("t_mm"), sem("probs")
        pv_mm, o_ready = sem("pv_mm"), sem("o_ready")
        oT_mm, ao_ready = sem("oT_mm"), sem("ao_ready")
        aoT_mm, aoT_ready, wo_mm, wo_used = sem("aoT_mm"), sem("aoT_ready"), sem("wo_mm"), sem("wo_used")
        gate_mm, gate_in, gate_exp, gates = sem("gate_mm"), sem("gate_in"), sem("gate_exp"), sem("gates")
        base_ready = sem("base_ready")
        h_mm, h_act, h_times = sem("h_mm"), sem("h_act"), sem("h_times")
        y_mm, y_used = sem("y_mm"), sem("y_used")
        h1_mm, h1_act, h1_gated = sem("h1_mm"), sem("h1_act"), sem("h1_gated")
        gT_mm, gT_ready, spread_mm = sem("gT_mm"), sem("gT_ready"), sem("spread_mm")
        tail_mm, tail_ready = sem("tail_mm"), sem("tail_ready")
        y1_mm, x_final = sem("y1_mm"), sem("x_final")
        dve_step, act_step = sem("dve_step"), sem("act_step")
        written = sem("written")

        block = ctx.enter_context(nc.Block())

        def s_jobs(layer):
            if layer == SELF:
                return [((t,), P * (t + 1)) for t in range(TB)]
            return [((0, 1), SC), ((2, 3), SC)]

        def t_jobs(layer):
            if layer == SELF:
                return [(j, P, P * j, sum(S - P * i for i in range(j))) for j in range(TB)]
            return [(j, KT, 0, S * j) for j in range(2)]

        S_PER = [4 * len(s_jobs(l)) for l in range(3)]
        T_PER = [4 * len(t_jobs(l)) for l in range(3)]
        S_BEFORE = [ITEMS * sum(S_PER[:l]) for l in range(4)]
        T_BEFORE = [ITEMS * sum(T_PER[:l]) for l in range(4)]
        T_BANKS, S_BANKS, PV_BANKS, N_BANK = (0, 1, 2), (3, 4), (5, 6), 7

        def s_index(layer, n, hh, k):
            return S_BEFORE[layer] + n * S_PER[layer] + hh * len(s_jobs(layer)) + k

        def t_index(layer, n, hh, k):
            return T_BEFORE[layer] + n * T_PER[layer] + hh * len(t_jobs(layer)) + k

        @block.sync
        def _(sp):
            sp.dma_start(X[:, :, :], x.rearrange("b (t p) d -> p (b t) d", p=P)).then_inc(in_x, 16)
            sp.dma_start(we[:, :], early).then_inc(in_early, 16)
            sp.dma_start(vec[:, :], vecs).then_inc(in_vec, 16)
            sp.dma_start(bv_b[:, :], bv.partition_broadcast(P)).then_inc(in_vec, 16)
            sp.dma_start(cst[:, :], consts).then_inc(in_const, 16)
            sp.dma_start(sub_i, sub_mask.rearrange("(t p) k -> p t k", p=P)).then_inc(in_mask, 16)
            sp.dma_start(PR[:, 10 * S:10 * S + B * SC].bitcast(I32), pad_mask.partition_broadcast(P)).then_inc(in_mask, 16)

            sp.wait_ge(pool_fills, 2)
            k1 = K1[:, :, :].rearrange("p h s -> p (h s)")
            for stack, n, w in ((QA, B * H * S, S), (KS, B * H * S, S), (k1, KV * B * SC, B * SC)):
                for rows, fill in ((slice(72, STACK), zeros_b), (slice(STACK, TOP), ones_b)):
                    if stack is QA and fill is ones_b:
                        continue
                    count = rows.stop - rows.start
                    sp.dma_start(stack[rows, :].rearrange("p (a w) -> p a w", w=w),
                                 fill[rows, 0:w].unsqueeze(1).to_broadcast([count, n // w, w])).then_inc(stack_fill, 16)

            def stack_rows(dst, src, done):
                for i in range(3):
                    for j in range(3):
                        at = i * 24 + j * HD
                        sp.dma_start(dst(at), src(i, j)).then_inc(done, 16)

            def queries(layer, b, slot):
                stack_rows(lambda at: QAv[at:at + HD, b, :, :], lambda i, j: parts[:, slot, i, :], q_stack[layer][b])

            sp.wait_ge(split_ready, SP_K0 + 1)
            stack_rows(lambda at: K0[at:at + HD, :, :], lambda i, j: parts[:, 0, j, 0:B * SC], k0_stack)
            for b in range(B):
                sp.wait_ge(split_ready, SP_Q0 + b + 1)
                queries(CROSS0, b, 2 + b)
            stack_rows(lambda at: K1[at:at + HD, :, :], lambda i, j: parts[0:KV * HD, 1, j, 0:B * SC], k1_stack)

            sp.dma_start(wl[:, :], late).then_inc(in_late, 16)
            sp.wait_ge(pool_fills, 5)
            sp.dma_start(w_tail[0:HE, :], ws2).then_inc(in_tail, 16)
            sp.dma_start(w_tail[HE:HE + E1, :], b2).then_inc(in_tail, 16)
            sp.dma_start(w_tail[96:97, :], bs2).then_inc(in_tail, 16)
            sp.dma_start(bs1_c[:, :], bs1).then_inc(in_tail, 16)
            sp.dma_start(rs_b[:, :], rscale.partition_broadcast(P)).then_inc(in_tail, 16)

            def maxima(layer):
                for n in range(ITEMS):
                    N = layer * ITEMS + n
                    b, g = divmod(n, QUADS)
                    sp.wait_ge(nrows_ready, N + 1)
                    sp.dma_start(QAv[STACK:TOP, b, 4 * g:4 * g + 4, :].rearrange("p h (t c) -> p (h t) c", c=P),
                                 nrows[:, N % 2, :]).then_inc(max_rows[N % 2], 16)

            maxima(CROSS0)
            sp.wait_ge(t_mm, T_BEFORE[SELF])
            for b in range(B):
                sp.wait_ge(split_ready, SP_SELF + 2 * b + 1)
                queries(SELF, b, 2 * b)
                sp.wait_ge(split_ready, SP_SELF + 2 * b + 2)
                stack_rows(lambda at: KSv[at:at + HD, b, :, :], lambda i, j: parts[:, 2 * b + 1, j, :], k_stack[b])
            maxima(SELF)
            sp.wait_ge(t_mm, T_BEFORE[CROSS1])
            for b in range(B):
                sp.wait_ge(split_ready, SP_Q1 + b + 1)
                queries(CROSS1, b, b)
            maxima(CROSS1)
            out_v = out.rearrange("b (t p) d -> b p t d", p=P)
            for b in range(B):
                sp.wait_ge(x_final, b + 1)
                sp.dma_start(out_v[b], X[:, TB * b:TB * b + TB, :]).then_inc(written, 16)
            sp.wait_ge(written, 16 * B)

        @block.gpsimd
        def _(pool):
            nc.gpsimd.memset(zeros_b[:, :], 0.0).then_inc(pool_fills, 1)
            nc.gpsimd.memset(ones_b[:, :], 1.0).then_inc(pool_fills, 1)
            nc.gpsimd.memset(V0[:, :, :, :, HD], 1.0).then_inc(pool_fills, 1)
            nc.gpsimd.memset(V1[:, :, :, :, HD], 1.0).then_inc(pool_fills, 1)
            nc.gpsimd.memset(w_tail[:, :], 0.0).then_inc(pool_fills, 1)
            pool.wait_ge(pool_fills, 5)
            nc.gpsimd.memset(tail[64:P, :], 0.0).then_inc(pool_fills, 1)
            pool.wait_ge(pool_fills, 6)
            nc.gpsimd.memset(VS[:, :, :, HD], 1.0).then_inc(pool_fills, 1)
            pool.wait_ge(pool_fills, 7)
            nc.gpsimd.memset(tail[96:97, :], 1.0).then_inc(pool_fills, 1)
            for b in range(B):
                pool.wait_ge(wo_used, TB * (b + 1))
                ts = slice(TB * b, TB * b + TB)
                nc.gpsimd.tensor_tensor(X[:, ts, :], X[:, ts, :], Y[:, ts, :], ALU.add).then_inc(base_ready, 1)

        @block.scalar
        def _(act):
            steps = [0]

            def link(ins):
                steps[0] += 1
                ins.then_inc(act_step, 1)
                act.wait_ge(act_step, steps[0])

            def exp_table():
                nc.scalar.preload_act_table_set("natural_log_exp_and_others")

            def inv_sqrt(stage, b, src, to, eps):
                ts = slice(TB * b, TB * b + TB)
                act.wait_ge(var_ready[stage], b + 1)
                link(nc.scalar.activation(sm[:, LOGV, ts], src[:, ts], ACT.Ln, bias=eps[:, 0:1]))
                nc.scalar.activation(sm[:, to, ts], sm[:, LOGV, ts], ACT.Exp, scale=-0.5).then_inc(rstd_ready[stage], 1)

            def rows_t(stage, b, scale=None):
                act.wait_ge(rowsT_mm[stage], b + 1)
                if scale is None:
                    ins = nc.scalar.activation(yT[:, S * b:S * b + S], bank(6 + b), ACT.Copy)
                else:
                    ins = nc.scalar.activation(yT[:, S * b:S * b + S], bank(6 + b), ACT.Identity, scale=scale)
                ins.then_inc(rowsT_ready[stage], 1)

            def hi_part(slot, rows=P, n=S):
                nc.scalar.activation(parts[0:rows, slot, 0, 0:n], f32T[0:rows, slot, 0:n], ACT.Copy).then_inc(hi_ready, 1)

            def exps(layer):
                for n in range(ITEMS):
                    N = layer * ITEMS + n
                    if N >= 2:
                        act.wait_ge(pv_mm, N - 1)
                    for hh in range(4):
                        for k, (j, rows, q0, at) in enumerate(t_jobs(layer)):
                            tj = t_index(layer, n, hh, k)
                            act.wait_ge(t_mm, tj + 1)
                            nc.scalar.activation(PRv[0:rows, N % 2, hh, at:at + S - q0],
                                                 bank(T_BANKS[tj % 3], rows, S - q0, q0), ACT.Exp).then_inc(probs, 1)

            def ao_t(k, b):
                act.wait_ge(aoT_mm, k + b + 1)
                nc.scalar.activation(yT[:, S * b:S * b + S], bank(4 + b), ACT.Copy).then_inc(aoT_ready, 1)

            exp_table()
            act.wait_ge(in_vec, 32)
            act.wait_ge(eps_set, 1)
            act.wait_ge(ctx_mm, 1)
            nc.scalar.activation(f32T[:, 0, 0:B * SC], bank(0, P, B * SC), ACT.Identity, bias=V("x0_bk")).then_inc(f32_ready, 1)
            act.wait_ge(f32_ready, 1)
            hi_part(0, P, B * SC)
            for b in range(B):
                inv_sqrt(N_CROSS0, b, mv[:, :, 1], RSTD, eps_ln)
            act.wait_ge(ctx_mm, 2)
            nc.scalar.activation(f32T[0:KV * HD, 1, 0:B * SC], bank(1, KV * HD, B * SC), ACT.Copy).then_inc(f32_ready, 1)
            act.wait_ge(f32_ready, 2)
            hi_part(1, KV * HD, B * SC)
            for b in range(B):
                rows_t(T_CROSS0, b)
            for b in range(B):
                act.wait_ge(proj_mm, b + 1)
                link(nc.scalar.activation(f32T[:, 2 + b, :], bank(b), ACT.Identity, bias=V("x0_bq")))
                nc.scalar.activation(f32T[:, 2 + b, :], f32T[:, 2 + b, :], ACT.Copy, scale=HD ** -0.5).then_inc(f32_ready, 1)
                act.wait_ge(f32_ready, 3 + b)
                hi_part(2 + b)
            act.wait_ge(split_ready, SP_Q0 + B)
            act.wait_ge(mask_ready, B)
            exps(CROSS0)

            for b in range(B):
                inv_sqrt(N_SELF, b, mv[:, :, 1], RSTD, eps_ln)
            for b in range(B):
                inv_sqrt(R_SELF, b, sm[:, VAR2, :], RMS, eps_rms)
            for b in range(B):
                rows_t(T_SELF, b, V("n1"))
            for k in range(2 * B):
                r = k % 2
                act.wait_ge(proj_mm, 3 + k)
                if k >= 2:
                    act.wait_ge(f32_ready, SP_SELF + k - 1)
                nc.scalar.activation(sq[:, r, :], bank(k), ACT.Square).then_inc(sq_ready, 1)
                act.wait_ge(ms_mm, k + 1)
                link(nc.scalar.activation(sq[:, r, :], bank(4 + r), ACT.Ln, bias=eps_rms[:, 0:1]))
                nc.scalar.activation(sq[:, r, :], sq[:, r, :], ACT.Exp, scale=-0.5).then_inc(rms_ready, 1)
                act.wait_ge(f32_ready, SP_SELF + k + 1)
                if k == 0:
                    act.wait_ge(k0_stack, 16 * 9)
                if k == 1:
                    act.wait_ge(k1_stack, 16 * 9)
                if k >= 2:
                    act.wait_ge(q_stack[CROSS0][k - 2], 16 * 9)
                hi_part(k)
            act.wait_ge(split_ready, SP_SELF + 2 * B)
            exps(SELF)

            for b in range(B):
                ao_t(0, b)
            for b in range(B):
                inv_sqrt(R_FFN0, b, sm[:, VAR2, :], RMS, eps_rms)
            for b in range(B):
                rows_t(T_FFN0, b, V("n2"))
            for b in range(B):
                act.wait_ge(gate_in, b + 1)
                nc.scalar.activation(G[:, 1, :, 0:E0], G[:, 0, :, 0:E0], ACT.Exp).then_inc(gate_exp, 1)
                for k, (_, _, _, dst, func) in enumerate(HIDDEN):
                    if func == "times":
                        continue
                    if k == 0:
                        act.wait_ge(pv_mm, 2 * ITEMS)
                        if b:
                            act.wait_ge(y_mm, TB * b)
                    act.wait_ge(h_mm, b * N_HIDDEN + k + 1)
                    nc.scalar.activation(HB[:, dst, :], bank(k % H_BANKS), func).then_inc(h_act, 1)
                exp_table()

            for b in range(B):
                inv_sqrt(N_CROSS1, b, mv[:, :, 1], RSTD, eps_ln)
            for b in range(B):
                rows_t(T_CROSS1, b)
            for b in range(B):
                act.wait_ge(proj_mm, 7 + b)
                nc.scalar.activation(f32T[:, b, :], bank(b), ACT.Copy, scale=HD ** -0.5).then_inc(f32_ready, 1)
                act.wait_ge(f32_ready, SP_Q1 + b + 1)
                act.wait_ge([q_stack[SELF][0], k_stack[0]][b], 16 * 9)
                hi_part(b)
            act.wait_ge(split_ready, SP_Q1 + B)
            exps(CROSS1)

            for b in range(B):
                ao_t(B, b)
            for b in range(B):
                inv_sqrt(N_FFN1, b, mv[:, :, 1], RSTD, eps_ln)
            for b in range(B):
                rows_t(T_FFN1, b)
            act.wait_ge(in_tail, 16 * 5)
            act.wait_ge(pool_fills, 8)
            act.wait_ge(pv_mm, 3 * ITEMS)
            for b in range(B):
                act.wait_ge(gate_in, B + b + 1)
                nc.scalar.activation(GL[:, b, :, :], GL[:, b, :, :], ACT.Exp, scale=-1.0).then_inc(gate_exp, 1)
            for b in range(B):
                for c in range(4):
                    act.wait_ge(h1_mm, 4 * b + c + 1)
                    nc.scalar.activation(HB[:, 4 * b + c, :], bank(c), ACT.Gelu, bias=V(f"b1_{c}")).then_inc(h1_act, 1)
                act.wait_ge(tail_mm, b + 1)
                if b:
                    act.wait_ge(y1_mm, b)
                nc.scalar.activation(tail[0:HE, :], bank(7, HE), ACT.Gelu, bias=bs1_c[:, 0:1]).then_inc(tail_ready, 1)

        @block.tensor
        def _(pe):
            mm, tr = nc.tensor.matmul, nc.tensor.transpose

            def rows_t(stage, b, src):
                pe.wait_ge(rows_ready[stage], b + 1)
                for t in range(TB):
                    last = tr(bank(6 + b, P, P, P * t), src[:, TB * b + t, :], ident)
                last.then_inc(rowsT_mm[stage], 1)

            def attention(layer):
                def pass_s(n, hh):
                    b, g = divmod(n, QUADS)
                    h = 4 * g + hh
                    if hh == 0 and g == 0:
                        pe.wait_ge(q_stack[layer][b], 16 * 9)
                        if layer == SELF:
                            pe.wait_ge(k_stack[b], 16 * 9)
                    for k, (tiles, w) in enumerate(s_jobs(layer)):
                        sj = s_index(layer, n, hh, k)
                        bk = S_BANKS[sj % 2]
                        if sj >= 2:
                            pe.wait_ge(s_max, sj - 1)
                        for i, t in enumerate(tiles):
                            q = QAv[0:STACK, b, h, P * t:P * t + P]
                            if layer == SELF:
                                keys = KSv[0:STACK, b, h, 0:w]
                            elif layer == CROSS0:
                                keys = K0[0:STACK, h, SC * b:SC * b + SC]
                            else:
                                keys = K1[0:STACK, g, SC * b:SC * b + SC]
                            last = mm(bank(bk, P, w, w * i), q, keys, start=True, stop=layer == CROSS1)
                            if layer == CROSS0:
                                last = mm(bank(bk, P, w, w * i), ident_b[:, :], msk[:, b, t, :], start=False, stop=True)
                            if layer == SELF:
                                last = mm(bank(bk, P, P, P * t), ident_b[:, :], causal_b[:, :], start=False, stop=True)
                        last.then_inc(s_mm, 1)

                def maxima(n):
                    N = layer * ITEMS + n
                    pe.wait_ge(nparts_ready, N + 1)
                    if N >= 1:
                        pe.wait_ge(nrows_ready, N)
                    tr(bank16(N_BANK)[0:48, 0:P], nparts[:, N % 2, :], ident_b[:, :]).then_inc(nrows_mm, 1)

                def pass_t(n, hh):
                    N = layer * ITEMS + n
                    b, g = divmod(n, QUADS)
                    h = 4 * g + hh
                    if hh == 0:
                        pe.wait_ge(max_rows[N % 2], 16 * (N // 2 + 1))
                    for k, (j, rows, q0, _) in enumerate(t_jobs(layer)):
                        tj = t_index(layer, n, hh, k)
                        bk = T_BANKS[tj % 3]
                        if tj >= 3:
                            pe.wait_ge(probs, tj - 2)
                        if layer == SELF:
                            keys = KSv[0:TOP, b, h, P * j:P * j + P]
                        elif layer == CROSS0:
                            keys = K0[0:TOP, h, SC * b + CT[j]:SC * b + CT[j] + KT]
                        else:
                            keys = K1[0:TOP, g, SC * b + CT[j]:SC * b + CT[j] + KT]
                        last = mm(bank(bk, rows, S - q0, q0), keys, QAv[0:TOP, b, h, q0:S], start=True, stop=layer == CROSS1)
                        if layer == CROSS0:
                            last = mm(bank(bk, rows), ident_b[0:KT, 0:KT], msk_t[:, b, S * j:S * j + S], start=False, stop=True)
                        if layer == SELF:
                            last = mm(bank(bk, rows, P, q0), ident_b[:, :], causal_tb[:, :], start=False, stop=True)
                        last.then_inc(t_mm, 1)

                def pass_v(n, slot):
                    N = layer * ITEMS + n
                    b, g = divmod(n, QUADS)
                    jobs = t_jobs(layer)
                    if slot * len(jobs) % 4:
                        return
                    j, rows, q0, at = jobs[slot * len(jobs) // 4]
                    if slot == 0:
                        pe.wait_ge(probs, T_BEFORE[layer] + (n + 1) * T_PER[layer])
                        if N >= 2:
                            pe.wait_ge(o_ready, N - 1)
                    for hh in range(4):
                        if layer == SELF:
                            v = VS[:, TB * b + j, 4 * g + hh, :]
                        elif layer == CROSS0:
                            v = V0[:, b, j, 4 * g + hh, :]
                        else:
                            v = V1[:, b, j, g, :]
                        last = mm(PS[32 * hh:32 * hh + HD + 1, PV_BANKS[N % 2], q0:S], v,
                                  PRv[0:rows, N % 2, hh, at:at + S - q0], start=j == 0, stop=j == len(jobs) - 1)
                    if j == len(jobs) - 1:
                        last.then_inc(pv_mm, 1)

                for w in range(-2, ITEMS + 1):
                    for hh in range(4):
                        if w + 2 < ITEMS:
                            pass_s(w + 2, hh)
                        if hh == 1 and 0 <= w + 1 < ITEMS:
                            maxima(w + 1)
                        if 0 <= w < ITEMS:
                            pass_t(w, hh)
                        if w >= 1:
                            pass_v(w - 1, hh)

            def heads_to_rows(layer):
                for t in range(NT):
                    b, k = t // TB, layer * NT + t
                    pe.wait_ge(o_ready, layer * ITEMS + QUADS * (b + 1))
                    if t >= 4:
                        pe.wait_ge(ao_ready, k - 3)
                    for g in range(QUADS):
                        last = tr(bank(t % 4, P, P, P * g), O[:, QUADS * b + g, P * (t % TB):P * (t % TB) + P], ident)
                    last.then_inc(oT_mm, 1)

            def out_projection(layer, k, w, n):
                for b in range(B):
                    pe.wait_ge(ao_ready, layer * NT + TB * (b + 1))
                    for t in range(TB):
                        last = tr(bank(4 + b, P, P, P * t), U[:, TB * b + t, :], ident)
                    last.then_inc(aoT_mm, 1)
                for b in range(B):
                    pe.wait_ge(aoT_ready, k + b + 1)
                    if b == 0:
                        pe.wait_ge(o_ready, (layer + 1) * ITEMS)
                    for t in range(TB):
                        last = mm(bank(6 + b, P, n, n * t), yT[:, S * b + P * t:S * b + P * t + P], w, start=True, stop=True)
                    last.then_inc(wo_mm, 1)

            def gate(stage, b, w, E):
                pe.wait_ge(rowsT_ready[stage], b + 1)
                for t in range(TB):
                    last = mm(bank(4 + b, P, E, E * t), yT[:, S * b + P * t:S * b + P * t + P], w, start=True, stop=True)
                last.then_inc(gate_mm, 1)

            pe.wait_ge(in_early, 16)
            mm(bank(0, P, B * SC), W("x0_k"), ctxT, start=True, stop=True).then_inc(ctx_mm, 1)
            mm(bank(1, KV * HD, B * SC), W("x1_k"), ctxT, start=True, stop=True).then_inc(ctx_mm, 1)
            for b in range(B):
                for j in range(2):
                    keys = ctxT[:, SC * b + CT[j]:SC * b + CT[j] + KT]
                    mm(bank(2, KT, D, D * (2 * b + j)), keys, W("x0_v"), start=True, stop=True)
                    last = mm(bank(3, KT, KV * HD, KV * HD * (2 * b + j)), keys, W("x1_v"), start=True, stop=True)
            last.then_inc(ctx_mm, 1)
            pe.wait_ge(in_const, 16)
            for b in range(B):
                rows_t(T_CROSS0, b, Y)
            for b in range(B):
                pe.wait_ge(rowsT_ready[T_CROSS0], b + 1)
                pe.wait_ge(f32_ready, b + 1)
                mm(bank(b), W("x0_q"), yT[:, S * b:S * b + S], start=True, stop=True).then_inc(proj_mm, 1)
            pe.wait_ge(consts_cast, 1)
            for b in range(B):
                pe.wait_ge(mask_ready, b + 1)
                for j in range(2):
                    for t in range(TB):
                        last = tr(bank16(4 if b == 0 else 7)[0:KT, S * j + P * t:S * j + P * t + P],
                                  msk[:, b, t, CT[j]:CT[j] + KT], ident_b[:, :])
                last.then_inc(maskt_mm, 1)
            pe.wait_ge(rowsT_ready[T_CROSS0], 2)
            pe.wait_ge(k0_stack, 16 * 9)
            pe.wait_ge(stack_fill, 16 * 5)
            pe.wait_ge(f32_ready, SP_Q0 + B)
            pe.wait_ge(ctx_v, 5)
            pe.wait_ge(maskt_ready, 2)
            pe.wait_ge(pv_cleared, 1)
            attention(CROSS0)

            pe.wait_ge(probs, T_BEFORE[SELF])
            pe.wait_ge(s_max, S_BEFORE[SELF])
            heads_to_rows(CROSS0)
            for b in range(B):
                rows_t(T_SELF, b, U)
            pe.wait_ge(in_late, 16)
            pe.wait_ge(ao_ready, NT)
            pe.wait_ge(nrows_ready, ITEMS)
            for b in range(B):
                pe.wait_ge(rowsT_ready[T_SELF], b + 1)
                for r, w in enumerate(("wq", "wk")):
                    mm(bank(2 * b + r), W(w), yT[:, S * b:S * b + S], start=True, stop=True).then_inc(proj_mm, 1)
            for b in range(B):
                for t in range(TB):
                    last = mm(bank(6 + b, P, P, P * t), yT[:, S * b + P * t:S * b + P * t + P], W("wv"), start=True, stop=True)
                last.then_inc(v_mm, 1)
                for r in range(2):
                    k = 2 * b + r
                    pe.wait_ge(sq_ready, k + 1)
                    mm(bank(4 + r), C("head_mean"), sq[:, r, :], start=True, stop=True).then_inc(ms_mm, 1)
            pe.wait_ge(f32_ready, SP_SELF + 2 * B)
            pe.wait_ge(rms_ready, 2 * B)
            pe.wait_ge(v_ready, B)
            pe.wait_ge(pool_fills, 8)
            attention(SELF)

            pe.wait_ge(probs, T_BEFORE[CROSS1])
            pe.wait_ge(s_max, S_BEFORE[CROSS1])
            heads_to_rows(SELF)
            pe.wait_ge(nrows_ready, 2 * ITEMS)
            out_projection(SELF, 0, wl[:, LATE["wo"][0] + KEEP:LATE["wo"][0] + D], OC)
            pe.wait_ge(wo_used, NT)
            for b in range(B):
                rows_t(T_FFN0, b, U)
            for b in range(B):
                gate(T_FFN0, b, W("gate0"), E0)
            for b in range(B):
                for k, (w, chunks, srcs, _, _) in enumerate(HIDDEN):
                    free = b * N_HIDDEN + k - H_BANKS
                    if free >= 0:
                        fb, fk = divmod(free, N_HIDDEN)
                        if HIDDEN[fk][4] == "times":
                            pe.wait_ge(h_times, fb * N_TIMES + fk + 1 - gelus_to(fk))
                        else:
                            pe.wait_ge(h_act, fb * N_GELU + gelus_to(fk))
                    if srcs is None:
                        last = mm(bank(k % H_BANKS), W(w, chunks[0]), yT[:, S * b:S * b + S], start=True, stop=True)
                    else:
                        writer = max(i for i, h in enumerate(HIDDEN) if h[3] in srcs)
                        pe.wait_ge(h_act, b * N_GELU + gelus_to(writer))
                        for i, s in enumerate(srcs):
                            last = mm(bank(k % H_BANKS), W(w, chunks[i]), HB[:, s, :], start=i == 0, stop=i == len(srcs) - 1)
                    last.then_inc(h_mm, 1)
                pe.wait_ge(h_act, (b + 1) * N_GELU)
                pe.wait_ge(h_times, (b + 1) * N_TIMES)
                for t in range(TB):
                    k = TB * b + t
                    if k >= 2:
                        pe.wait_ge(y_used, k - 1)
                    for e, (w, srcs) in enumerate(OUTPUTS):
                        at = LATE[w][0]
                        for i, s in enumerate(srcs):
                            last = mm(bank(6 + k % 2, P, OC, OC * e), HB[:, s, P * t:P * t + P],
                                      wl[:, at + D * i + KEEP:at + D * i + D], start=i == 0, stop=i == 1)
                    last.then_inc(y_mm, 1)

            pe.wait_ge(y_used, NT)
            for b in range(B):
                rows_t(T_CROSS1, b, Y)
            for b in range(B):
                pe.wait_ge(rowsT_ready[T_CROSS1], b + 1)
                mm(bank(b), W("x1_q"), yT[:, S * b:S * b + S], start=True, stop=True).then_inc(proj_mm, 1)
            pe.wait_ge(k1_stack, 16 * 9)
            pe.wait_ge(f32_ready, SP_Q1 + B)
            attention(CROSS1)

            pe.wait_ge(probs, T_BEFORE[3])
            pe.wait_ge(s_max, S_BEFORE[3])
            heads_to_rows(CROSS1)
            pe.wait_ge(nrows_ready, 3 * ITEMS)
            out_projection(CROSS1, B, W("x1_o"), D)
            pe.wait_ge(wo_used, 2 * NT)
            for b in range(B):
                rows_t(T_FFN1, b, Y)
            for b in range(B):
                gate(T_FFN1, b, W("gate1"), E1)
            pe.wait_ge(in_tail, 16 * 5)
            for b in range(B):
                xT = yT[:, S * b:S * b + S]
                for c in range(4):
                    if b:
                        pe.wait_ge(h1_act, 4 * (b - 1) + c + 1)
                    mm(bank(c), W("w1", c), xT, start=True, stop=True).then_inc(h1_mm, 1)
                if b:
                    pe.wait_ge(tail_ready, b)
                mm(bank(7, HE), W("ws1"), xT, start=True, stop=True).then_inc(tail_mm, 1)
                pe.wait_ge(gates, b + 1)
                pe.wait_ge(gate_in, 2 * B)
                if b:
                    pe.wait_ge(h1_gated, 4 * b)
                for t in range(TB):
                    tr(bank16(4)[0:3 * E1, P * t:P * t + P], gparts[:, t, :, :].rearrange("p a e -> p (a e)"), ident_b[:, :])
                for t in range(TB):
                    last = tr(bank(5, E1, P, P * t), G[:, 5, t, :], ident)
                last.then_inc(gT_mm, 1)
                pe.wait_ge(gT_ready, 2 * b + 2)
                for c in range(4):
                    if c >= 2:
                        pe.wait_ge(h1_gated, 4 * b + c - 1)
                    mm(bank(4 + c % 2), spread_b[:, P * c:P * c + P], gT[:, :], start=True, stop=True).then_inc(spread_mm, 1)
                pe.wait_ge(h1_gated, 4 * (b + 1))
                pe.wait_ge(tail_ready, b + 1)
                if b:
                    pe.wait_ge(x_final, b)
                for t in range(TB):
                    cols = slice(P * t, P * t + P)
                    for c in range(4):
                        mm(bank(6, P, D, D * t), HB[:, 4 * b + c, cols], W("w2", c), start=c == 0, stop=False)
                    last = mm(bank(6, P, D, D * t), tail[0:97, cols], w_tail[0:97, :], start=False, stop=True)
                last.then_inc(y1_mm, 1)

        @block.vector
        def _(dve):
            steps = [0]

            def link(ins):
                steps[0] += 1
                ins.then_inc(dve_step, 1)
                dve.wait_ge(dve_step, steps[0])

            def tiles(b):
                return range(TB * b, TB * b + TB)

            def statistics(src, b):
                for t in tiles(b):
                    last = nc.vector.bn_stats(stats[:, t, :], src[:, t, :])
                link(last)
                for t in tiles(b):
                    last = nc.vector.bn_aggr(mv[:, t, :], stats[:, t, :])
                return last

            def normalise(stage, b):
                dve.wait_ge(rstd_ready[stage], b + 1)
                for t in tiles(b):
                    last = nc.vector.tensor_scalar(Y[:, t, :], X[:, t, :], mv[:, t, 0:1], sm[:, RSTD, t:t + 1],
                                                   ALU.subtract, ALU.mult)
                return last

            def rms_scale(stage, b):
                dve.wait_ge(rstd_ready[stage], b + 1)
                for t in tiles(b):
                    last = nc.vector.tensor_scalar(U[:, t, :], Y[:, t, :], sm[:, RMS, t:t + 1], None, ALU.mult)
                return last

            def split(k, slot, rows=P, n=S):
                p = [parts[0:rows, slot, i, 0:n] for i in range(3)]
                r = res[0:rows, k % 2, 0:n]
                dve.wait_ge(hi_ready, k + 1)
                link(nc.vector.tensor_tensor(r, f32T[0:rows, slot, 0:n], p[0], ALU.subtract))
                link(nc.vector.tensor_copy(p[1], r))
                nc.vector.tensor_tensor(p[2], r, p[1], ALU.subtract).then_inc(split_ready, 1)

            def attention(layer):
                def reduce(n, hh):
                    N = layer * ITEMS + n
                    for k, (ts, w) in enumerate(s_jobs(layer)):
                        sj = s_index(layer, n, hh, k)
                        dve.wait_ge(s_mm, sj + 1)
                        at = 4 * hh + ts[0]
                        nc.vector.tensor_reduce(nmax[:, N % 2, at:at + len(ts)],
                                                PS[:, S_BANKS[sj % 2], 0:w * len(ts)].rearrange("p (t k) -> p t k", k=w),
                                                AX.X, ALU.max, negate=True).then_inc(s_max, 1)

                def split_max(n):
                    N = layer * ITEMS + n
                    src, r = nmax[:, N % 2, :], nres[:, N % 2, :]
                    p = [nparts[:, N % 2, 16 * i:16 * i + 16] for i in range(3)]
                    dve.wait_ge(s_max, S_BEFORE[layer] + (n + 1) * S_PER[layer])
                    if N >= 2:
                        dve.wait_ge(nrows_mm, N - 1)
                    link(nc.vector.tensor_copy(p[0], src))
                    link(nc.vector.tensor_tensor(r, src, p[0], ALU.subtract))
                    link(nc.vector.tensor_copy(p[1], r))
                    nc.vector.tensor_tensor(p[2], r, p[1], ALU.subtract).then_inc(nparts_ready, 1)

                def copy_rows(n):
                    N = layer * ITEMS + n
                    dve.wait_ge(nrows_mm, N + 1)
                    if N >= 2:
                        dve.wait_ge(max_rows[N % 2], 16 * (N // 2))
                    nc.vector.tensor_copy(nrows[:, N % 2, :], bank16(N_BANK)[0:48, 0:P]).then_inc(nrows_ready, 1)

                def evacuate(n):
                    N = layer * ITEMS + n
                    dve.wait_ge(pv_mm, N + 1)
                    nc.vector.tensor_copy(O[:, n, :], bank(PV_BANKS[N % 2])).then_inc(o_ready, 1)

                for w in range(-2, ITEMS + 2):
                    for hh in range(4):
                        if w + 2 < ITEMS:
                            reduce(w + 2, hh)
                        if hh == 0 and w >= 2:
                            evacuate(w - 2)
                        if hh == 1 and 0 <= w + 1 < ITEMS:
                            copy_rows(w + 1)
                    if w + 2 < ITEMS:
                        split_max(w + 2)

            def rows_of_heads(layer, t):
                dve.wait_ge(oT_mm, layer * NT + t + 1)
                v = PS[:, t % 4, :].rearrange("p (h c) -> p h c", c=32)
                link(nc.vector.reciprocal(rden[:, t % 2, :], v[:, :, HD]))
                nc.vector.tensor_tensor(U[:, t, :].rearrange("p (h d) -> p h d", d=HD), v[:, :, 0:HD],
                                        rden[:, t % 2, :].unsqueeze(2).to_broadcast([P, H, HD]), ALU.mult)\
                    .then_inc(ao_ready, 1)

            def top2(prob, E, before, guard):
                g, q = GG[:, 0, :, 0:E, 0:E], GG[:, 1, :, 0:E, 0:E]
                pj = prob.unsqueeze(2).to_broadcast([P, TB, E, E])
                pi = prob.unsqueeze(3).to_broadcast([P, TB, E, E])
                lt = before.rearrange("p (i j) -> p i j", j=E).unsqueeze(1).to_broadcast([P, TB, E, E])
                nc.vector.tensor_tensor(g, pj, pi, ALU.is_gt)
                link(nc.vector.tensor_tensor(q, pj, pi, ALU.is_equal))
                link(nc.vector.tensor_tensor(q, q, lt, ALU.mult))
                link(nc.vector.tensor_tensor(g, g, q, ALU.add))
                link(nc.vector.tensor_reduce(G[:, 2, :, 0:E], g, AX.X, ALU.add))
                link(nc.vector.scalar_tensor_tensor(out=G[:, 3, :, 0:E], in0=G[:, 2, :, 0:E], scalar=2.0, in1=prob,
                                                    op0=ALU.is_lt, op1=ALU.mult))
                link(nc.vector.tensor_reduce(sm[:, GSUM, 0:TB], G[:, 3, :, 0:E], AX.X, ALU.add))
                if guard:
                    link(nc.vector.tensor_scalar(sm[:, GSUM, 0:TB], sm[:, GSUM, 0:TB], guard, None, ALU.add))
                link(nc.vector.reciprocal(sm[:, GINV, 0:TB], sm[:, GSUM, 0:TB]))
                link(nc.vector.tensor_tensor(G[:, 5, :, 0:E], G[:, 3, :, 0:E],
                                             sm[:, GINV, 0:TB].unsqueeze(2).to_broadcast([P, TB, E]), ALU.mult))

            nc.vector.memset(eps_ln[:, :], LN_EPS)
            nc.vector.memset(eps_rms[:, :], RMS_EPS).then_inc(eps_set, 1)
            nc.vector.memset(PS[:, PV_BANKS[0]:PV_BANKS[0] + 1, :], 0.0)
            dve.wait_ge(in_x, 16)
            for b in range(B):
                statistics(X, b).then_inc(var_ready[N_CROSS0], 1)
            dve.wait_ge(in_vec, 32)
            nc.vector.tensor_scalar(V("qn"), V("qn"), HD ** -0.5, None, ALU.mult).then_inc(eps_set, 1)
            for b in range(B):
                normalise(N_CROSS0, b).then_inc(rows_ready[T_CROSS0], 1)
            split(SP_K0, 0, P, B * SC)
            dve.wait_ge(in_const, 16)
            nc.vector.tensor_copy(causal_b[:, :], C("causal"))
            nc.vector.tensor_copy(causal_tb[:, :], C("causal_t"))
            nc.vector.tensor_copy(spread_b[:, :], C("spread")[0:3 * E1, :])
            nc.vector.tensor_copy(ident_b[:, :], ident).then_inc(consts_cast, 1)
            split(SP_K1, 1, KV * HD, B * SC)
            for b in range(B):
                split(SP_Q0 + b, 2 + b)
            dve.wait_ge(in_mask, 32)
            link(nc.vector.tensor_scalar(pad_z, pad_i, 0.0, None, ALU.is_equal))
            for b in range(B):
                for t in range(TB):
                    last = nc.vector.scalar_tensor_tensor(out=sub_f[:, t, :], in0=sub_i[:, t, :], scalar=0.0,
                                                          in1=pad_z[:, b, :], op0=ALU.is_equal, op1=ALU.max)
                link(last)
                nc.vector.tensor_scalar(msk[:, b, :, :], sub_f, NEG, None, ALU.mult).then_inc(mask_ready, 1)
                dve.wait_ge(mask_ready, b + 1)
            dve.wait_ge(ctx_mm, 3)
            dve.wait_ge(pool_fills, 4)
            bias = bv_b[0:KT, :].rearrange("p (h d) -> p h d", d=HD)
            for b in range(B):
                for j in range(2):
                    nc.vector.tensor_copy(V1[:, b, j, :, 0:HD],
                                          bank(3, KT, KV * HD, KV * HD * (2 * b + j)).rearrange("p (h d) -> p h d", d=HD))
                    nc.vector.tensor_tensor(V0[:, b, j, :, 0:HD],
                                            bank(2, KT, D, D * (2 * b + j)).rearrange("p (h d) -> p h d", d=HD), bias, ALU.add)\
                        .then_inc(ctx_v, 1)
            dve.wait_ge(ctx_v, 4)
            for b in range(B):
                nc.vector.memset(V0[0:OVER, b, 1, :, :], 0.0)
                last = nc.vector.memset(V1[0:OVER, b, 1, :, :], 0.0)
            last.then_inc(ctx_v, 1)
            for b in range(B):
                dve.wait_ge(maskt_mm, b + 1)
                nc.vector.tensor_copy(msk_t[:, b, :], bank16(4 if b == 0 else 7)[0:KT, 0:2 * S]).then_inc(maskt_ready, 1)
            dve.wait_ge(rowsT_ready[T_CROSS0], 2)
            nc.vector.memset(PS[:, PV_BANKS[1]:PV_BANKS[1] + 1, :], 0.0).then_inc(pv_cleared, 1)
            attention(CROSS0)

            for b in range(B):
                ts = slice(TB * b, TB * b + TB)
                for t in tiles(b):
                    rows_of_heads(CROSS0, t)
                dve.wait_ge(ao_ready, TB * (b + 1))
                link(nc.vector.tensor_tensor(X[:, ts, :], X[:, ts, :], U[:, ts, :], ALU.add))
                statistics(X, b).then_inc(var_ready[N_SELF], 1)
            for b in range(B):
                ts = slice(TB * b, TB * b + TB)
                dve.wait_ge(rstd_ready[N_SELF], b + 1)
                link(nc.vector.tensor_tensor(sm[:, VAR2, ts], mv[:, ts, 1], sm[:, RSTD, ts], ALU.mult))
                nc.vector.tensor_tensor(sm[:, VAR2, ts], sm[:, VAR2, ts], sm[:, RSTD, ts], ALU.mult)\
                    .then_inc(var_ready[R_SELF], 1)
                link(normalise(N_SELF, b))
            for b in range(B):
                rms_scale(R_SELF, b).then_inc(rows_ready[T_SELF], 1)
            for b in range(B):
                for r, w in enumerate(("qn", "kn")):
                    k = 2 * b + r
                    dve.wait_ge(rms_ready, k + 1)
                    if k == 0:
                        dve.wait_ge(pv_mm, ITEMS)
                    if k >= 2:
                        dve.wait_ge(split_ready, SP_SELF + k - 1)
                    nc.vector.scalar_tensor_tensor(out=f32T[:, k, :], in0=bank(k), scalar=V(w), in1=sq[:, r, :],
                                                   op0=ALU.mult, op1=ALU.mult).then_inc(f32_ready, 1)
                    if r == 0:
                        dve.wait_ge(v_mm, b + 1)
                        nc.vector.tensor_copy(VS[:, TB * b:TB * b + TB, :, 0:HD],
                                              bank(6 + b).rearrange("p (t h d) -> p t h d", t=TB, h=H)).then_inc(v_ready, 1)
                    split(SP_SELF + k, k)
            attention(SELF)

            for t in range(NT):
                rows_of_heads(SELF, t)
            for b in range(B):
                ts = slice(TB * b, TB * b + TB)
                dve.wait_ge(wo_mm, b + 1)
                for t in tiles(b):
                    last = nc.vector.tensor_tensor(Y[:, t, KEEP:D], Y[:, t, KEEP:D], bank(6 + b, P, OC, OC * (t % TB)), ALU.add)
                    last.then_inc(wo_used, 1)
                dve.wait_ge(wo_used, TB * (b + 1))
                link(statistics(Y, b))
                link(nc.vector.tensor_tensor(sm[:, VAR2, ts], mv[:, ts, 0], mv[:, ts, 0], ALU.mult))
                nc.vector.tensor_tensor(sm[:, VAR2, ts], sm[:, VAR2, ts], mv[:, ts, 1], ALU.add).then_inc(var_ready[R_FFN0], 1)
            dve.wait_ge(aoT_mm, 2)
            for b in range(B):
                rms_scale(R_FFN0, b).then_inc(rows_ready[T_FFN0], 1)
            nc.vector.memset(G[:, 0, :, :], 0.0)
            for b in range(B):
                dve.wait_ge(gate_mm, b + 1)
                logits = bank(4 + b, P, TB * E0).rearrange("p (t e) -> p t e", e=E0)
                z, num = G[:, 0, :, 0:E0], gnum[:, :, 0:E0]
                link(nc.vector.tensor_copy(G[:, 4, :, 0:E0], logits))
                nc.vector.memset(z, 0.0)
                link(nc.vector.tensor_tensor(num, G[:, 4, :, 0:E0], G[:, 4, :, 0:E0], ALU.is_equal))
                link(nc.vector.copy_predicated(z, num, G[:, 4, :, 0:E0]))
                link(nc.vector.tensor_scalar(z, z, -FLT_MAX, FLT_MAX, ALU.max, ALU.min))
                link(nc.vector.tensor_reduce(sm[:, GSUM, 0:TB], z, AX.X, ALU.max))
                nc.vector.tensor_tensor(z, z, sm[:, GSUM, 0:TB].unsqueeze(2).to_broadcast([P, TB, E0]), ALU.subtract)\
                    .then_inc(gate_in, 1)
                dve.wait_ge(gate_exp, b + 1)
                link(nc.vector.tensor_reduce(sm[:, GSUM, 0:TB], G[:, 1, :, 0:E0], AX.X, ALU.add))
                link(nc.vector.reciprocal(sm[:, GINV, 0:TB], sm[:, GSUM, 0:TB]))
                link(nc.vector.tensor_tensor(G[:, 4, :, 0:E0], G[:, 1, :, 0:E0],
                                             sm[:, GINV, 0:TB].unsqueeze(2).to_broadcast([P, TB, E0]), ALU.mult))
                top2(G[:, 4, :, 0:E0], E0, C("before0"), 1e-8)
                for k, (_, _, _, dst, func) in enumerate(HIDDEN):
                    if func == "times":
                        dve.wait_ge(h_act, b * N_GELU + gelus_to(k))
                        dve.wait_ge(h_mm, b * N_HIDDEN + k + 1)
                        nc.vector.tensor_tensor(HB[:, dst, :], HB[:, dst, :], bank(k % H_BANKS), ALU.mult).then_inc(h_times, 1)
                dve.wait_ge(base_ready, b + 1)
                for t in tiles(b):
                    dve.wait_ge(y_mm, t + 1)
                    xt = X[:, t, KEEP:D]
                    for e in range(E0):
                        ins = nc.vector.scalar_tensor_tensor(out=xt, in0=bank(6 + t % 2, P, OC, OC * e),
                                                             scalar=G[:, 5, t % TB, e:e + 1], in1=xt,
                                                             op0=ALU.mult, op1=ALU.add)
                        if e < E0 - 1:
                            link(ins)
                        else:
                            ins.then_inc(y_used, 1)
                dve.wait_ge(y_used, TB * (b + 1))
                statistics(X, b).then_inc(var_ready[N_CROSS1], 1)
            for b in range(B):
                normalise(N_CROSS1, b).then_inc(rows_ready[T_CROSS1], 1)
            for b in range(B):
                split(SP_Q1 + b, b)
            attention(CROSS1)

            for t in range(NT):
                rows_of_heads(CROSS1, t)
            for b in range(B):
                ts = slice(TB * b, TB * b + TB)
                dve.wait_ge(wo_mm, B + b + 1)
                nc.vector.tensor_tensor(X[:, ts, :], X[:, ts, :], bank(6 + b).rearrange("p (t d) -> p t d", t=TB), ALU.add)\
                    .then_inc(wo_used, TB)
                dve.wait_ge(wo_used, NT + TB * (b + 1))
                statistics(X, b).then_inc(var_ready[N_FFN1], 1)
            for b in range(B):
                normalise(N_FFN1, b).then_inc(rows_ready[T_FFN1], 1)
            for b in range(B):
                dve.wait_ge(gate_mm, B + b + 1)
                nc.vector.tensor_copy(GL[:, b, :, :], bank(4 + b, P, TB * E1).rearrange("p (t e) -> p t e", e=E1))\
                    .then_inc(gate_in, 1)
            dve.wait_ge(in_tail, 16 * 5)
            for b in range(B):
                if b:
                    dve.wait_ge(gT_mm, b)
                dve.wait_ge(gate_exp, B + b + 1)
                link(nc.vector.tensor_scalar(G[:, 1, :, :], GL[:, b, :, :], 1.0, None, ALU.add))
                link(nc.vector.reciprocal(G[:, 4, :, :], G[:, 1, :, :]))
                link(nc.vector.tensor_scalar(G[:, 4, :, :], G[:, 4, :, :], rs_b[:, 0:1], None, ALU.mult))
                top2(G[:, 4, :, :], E1, C("before1"), None)
                g5, g4 = G[:, 5, :, :], G[:, 4, :, :]
                link(nc.vector.tensor_copy(gparts[:, :, 0, :], g5))
                link(nc.vector.tensor_tensor(g4, g5, gparts[:, :, 0, :], ALU.subtract))
                link(nc.vector.tensor_copy(gparts[:, :, 1, :], g4))
                nc.vector.tensor_tensor(gparts[:, :, 2, :], g4, gparts[:, :, 1, :], ALU.subtract).then_inc(gates, 1)
                dve.wait_ge(gT_mm, b + 1)
                if b:
                    dve.wait_ge(spread_mm, 4 * b)
                    dve.wait_ge(y1_mm, b)
                nc.vector.tensor_copy(gT[:, :], bank16(4)[0:3 * E1, 0:S]).then_inc(gT_ready, 1)
                nc.vector.tensor_copy(tail[HE:HE + E1, :], bank(5, E1)).then_inc(gT_ready, 1)
                for c in range(4):
                    dve.wait_ge(h1_act, 4 * b + c + 1)
                    dve.wait_ge(spread_mm, 4 * b + c + 1)
                    hc = HB[:, 4 * b + c, :]
                    nc.vector.tensor_tensor(hc, hc, bank(4 + c % 2), ALU.mult).then_inc(h1_gated, 1)
                dve.wait_ge(y1_mm, b + 1)
                ts = slice(TB * b, TB * b + TB)
                nc.vector.tensor_tensor(X[:, ts, :], X[:, ts, :], bank(6).rearrange("p (t d) -> p t d", t=TB), ALU.add)\
                    .then_inc(x_final, 1)


def shape_constants():
    c = np.zeros((P, N_CONST), np.float32)

    def put(name, a):
        at, n = CONST[name]
        c[:a.shape[0], at:at + n] = a

    i = np.arange(P)
    put("ident", np.eye(P))
    put("head_mean", (i[:, None] % H == i[None, :] % H) / HD)
    put("causal", np.where(i[None, :] > i[:, None], NEG, 0.0))
    put("causal_t", np.where(i[:, None] > i[None, :], NEG, 0.0))
    for name, E in (("before0", E0), ("before1", E1)):
        e = np.arange(E)
        put(name, np.tile((e[None, :] < e[:, None]).reshape(1, -1), (P, 1)))
    r, col = np.arange(3 * E1), np.arange(4 * P)
    put("spread", r[:, None] % E1 == col[None, :] // HE)
    return c


def kernel(**inputs):
    import concourse.bacc as bacc
    from concourse.bass_utils import run_bass_kernel_spmd

    a = {k: np.asarray(v) for k, v in inputs.items()}

    def chunks(w):
        return np.concatenate([w[P * i:P * i + P] for i in range(w.shape[0] // P)], axis=1)

    def by_feature(w, heads=H):
        return w.reshape(w.shape[0], heads, HD).transpose(0, 2, 1).reshape(w.shape[0], heads * HD)

    def vector_by_feature(v):
        return v.reshape(H, HD).T.reshape(-1)

    f0, f1 = "L0_ffn_", "L1_ffn_"
    packed = {
        "ctx": a["ctx_1024"].transpose(2, 0, 1).reshape(D, B * SC),
        "x0_k": by_feature(a["L0_xattn_Wk"].T), "x0_v": a["L0_xattn_Wv"].T, "x0_q": by_feature(a["L0_xattn_Wq"].T),
        "x1_k": by_feature(a["L1_xattn_W_k"], KV), "x1_v": a["L1_xattn_W_v"],
        "wq": by_feature(a[f0 + "wq"].T), "wk": by_feature(a[f0 + "wk"].T), "wv": a[f0 + "wv"].T, "wo": a[f0 + "wo"].T,
        "gate0": a[f0 + "gate_w"].T,
        "e1_w1": a[f0 + "e1_w1"].T, "e1_w2": a[f0 + "e1_w2"].T, "e0_up": a[f0 + "e0_up"].T,
        "e3_down": a[f0 + "e3_down"].T, "e2_l1": a[f0 + "e2_l1"].T, "e3_up": a[f0 + "e3_up"].T,
        "e2_l2": chunks(a[f0 + "e2_l2"].T), "e2_l3": chunks(a[f0 + "e2_l3"].T),
        "e0_down": chunks(a[f0 + "e0_down"].T), "e1_down": chunks(a[f0 + "e1_down"].T),
        "e2_l4": chunks(a[f0 + "e2_l4"].T), "e3_out": chunks(a[f0 + "e3_out"].T),
        "x1_q": by_feature(a["L1_xattn_W_q"]), "x1_o": a["L1_xattn_W_o"],
        "gate1": a[f1 + "gate_W"],
        "w1": a[f1 + "W1"].transpose(1, 0, 2).reshape(D, E1 * HE),
        "w2": chunks(a[f1 + "W2"].reshape(E1 * HE, D)),
        "ws1": a[f1 + "Ws1"],
    }
    vectors = {
        "x0_bq": vector_by_feature(a["L0_xattn_bq"]), "x0_bk": vector_by_feature(a["L0_xattn_bk"]),
        "n1": a[f0 + "n1_w"], "n2": a[f0 + "n2_w"],
        "qn": np.repeat(a[f0 + "qn_w"], H), "kn": np.repeat(a[f0 + "kn_w"], H),
        **{f"b1_{c}": a[f1 + "b1"].reshape(-1)[P * c:P * c + P] for c in range(4)},
    }
    arrays = {
        "early": np.concatenate([packed[n] for n in EARLY], axis=1),
        "late": np.concatenate([packed[n] for n in LATE], axis=1),
        "consts": shape_constants(),
        "vecs": np.stack([vectors[n] for n in VECS], axis=1),
        "bs1": a[f1 + "bs1"].reshape(HE, 1), "ws2": a[f1 + "Ws2"], "b2": a[f1 + "b2"],
        "bs2": a[f1 + "bs2"].reshape(1, D), "bv": a["L0_xattn_bv"],
        "rscale": a[f1 + "route_scale"].reshape(1),
        "pad_mask": a["mask_Bx1x1xS2_ik0"].reshape(B * SC),
        "sub_mask": a["mask_1x1xSxS2_ik0"].reshape(S, SC),
        "x": a["x"],
    }
    nc = bacc.Bacc("TRN2", target_bir_lowering=False, num_devices=1)
    arrays = {f"in_{k}": np.ascontiguousarray(v) for k, v in arrays.items()}
    args = [nc.dram_tensor(k, v.shape, mybir.dt.from_np(v.dtype), kind="ExternalInput").ap() for k, v in arrays.items()]
    out = nc.dram_tensor("out_x", (B, S, D), F32, kind="ExternalOutput").ap()
    build(nc, *args, out)
    r = run_bass_kernel_spmd(nc, [arrays], core_ids=[0])
    return r.results[0]["out_x"]
```

```python
from contextlib import ExitStack

import numpy as np

import concourse.bass as bass
from concourse import mybir

F32 = mybir.dt.float32
BF16 = mybir.dt.bfloat16
I32 = mybir.dt.int32
ALU = mybir.AluOpType
ACT = mybir.ActivationFunctionType
AX = mybir.AxisListType

P = 128
B, S, D = 2, 512, 128
H, HD = 16, 8
KV = 4
SC = 154
KT = 96
CT = (0, SC - KT)
OVER = 2 * KT - SC
NT = B * S // P
TB = S // P
QUADS = H // 4
ITEMS = B * QUADS
STACK = 96
TOP = STACK + 3
NEG = -float(2 ** 100)
FLT_MAX = 3.4028234663852886e38
LN_EPS = 1e-5
RMS_EPS = 1.1920929e-07
KEEP = 32
OC = D - KEEP
E0, E1 = 4, 8
HE = 64

CROSS0, SELF, CROSS1 = range(3)
N_CROSS0, N_SELF, R_SELF, R_FFN0, N_CROSS1, N_FFN1 = range(6)
T_CROSS0, T_SELF, T_FFN0, T_CROSS1, T_FFN1 = range(5)
SP_K0, SP_Q0, SP_K1, SP_SELF, SP_Q1 = 0, (1, 3), 2, 4, 8
N_SPLITS = 10
LATE_PIECES = 4


def columns(names):
    at, cols = 0, {}
    for name, n in names:
        cols[name] = (at, n)
        at += n
    return cols, at


EARLY, N_EARLY = columns([("ctx", B * SC), ("x0_k", D), ("x0_v", D), ("x1_k", KV * HD), ("x1_v", KV * HD), ("x0_q", D)])
LATE, N_LATE = columns([
    ("wq", D), ("wk", D), ("wv", D), ("wo", D), ("gate0", E0),
    ("e1_w1", 2 * D), ("e1_w2", 2 * D), ("e0_up", 2 * D), ("e3_down", D), ("e2_l1", 2 * D), ("e3_up", 2 * D),
    ("e2_l2", 4 * D), ("e2_l3", 4 * D), ("e0_down", 2 * D), ("e1_down", 2 * D), ("e2_l4", 2 * D), ("e3_out", 2 * D),
    ("x1_q", D), ("x1_o", D), ("gate1", E1), ("w1", 4 * D), ("w2", 4 * D), ("ws1", HE)])
CONST, N_CONST = columns([("ident", P), ("head_mean", P), ("causal", P), ("causal_t", P),
                          ("before0", E0 * E0), ("before1", E1 * E1), ("spread", 4 * P)])
VECS = ["x0_bq", "x0_bk", "n1", "n2", "qn", "kn", "b1_0", "b1_1", "b1_2", "b1_3"]

E1_JOBS = [
    ("e1_w1", (0,), None, 0, ACT.Silu), ("e1_w1", (1,), None, 1, ACT.Silu),
    ("e1_w2", (0,), None, 0, "times"), ("e1_w2", (1,), None, 1, "times")]
GELU_JOBS = [
    ("e3_down", (0,), None, 2, ACT.Gelu),
    ("e2_l1", (0,), None, 3, ACT.Gelu), ("e2_l1", (1,), None, 4, ACT.Gelu),
    ("e3_up", (0,), (2,), 5, ACT.Gelu), ("e3_up", (1,), (2,), 6, ACT.Gelu),
    ("e2_l2", (0, 2), (3, 4), 7, ACT.Gelu), ("e2_l2", (1, 3), (3, 4), 8, ACT.Gelu)]
MORE_JOBS = [
    ("e0_up", (0,), None, 9, ACT.Gelu), ("e0_up", (1,), None, 10, ACT.Gelu),
    ("e2_l3", (0, 2), (7, 8), 11, ACT.Gelu), ("e2_l3", (1, 3), (7, 8), 12, ACT.Gelu)]
HIDDEN = [E1_JOBS + GELU_JOBS + MORE_JOBS, GELU_JOBS + E1_JOBS + MORE_JOBS]
OUTPUTS = [("e0_down", (9, 10)), ("e1_down", (0, 1)), ("e2_l4", (11, 12)), ("e3_out", (5, 6))]
N_HIDDEN = len(HIDDEN[0])
N_TIMES = sum(h[4] == "times" for h in HIDDEN[0])
H_BANKS = (0, 1, 3, 4)
OUT_BANKS = (5, 7)


def by_act(b, k):
    return b * (N_HIDDEN - N_TIMES) + sum(h[4] != "times" for h in HIDDEN[b][:k + 1])


def by_dve(b, k):
    return b * N_HIDDEN + k + 1 - by_act(b, k)


SELF_START, CROSS1_START = 7, 1000
START_WEIGHTS = (2, 0)
START_SELF = [(19, 22), (34, 35)]
START_FFN0 = (52 + SELF_START, 0)
START_HIDDEN = (4 * 2 * ITEMS + SELF_START, 0)
START_CROSS1, START_FFN1 = (CROSS1_START - 7, 0), (CROSS1_START + 19, 0)

LEAD = (7, 6, 7)

T_SLOT = {}
for _n in range(ITEMS):
    T_SLOT[_n] = 4 * _n
    T_SLOT[_n + ITEMS] = 4 * (_n + ITEMS) + SELF_START
    T_SLOT[_n + 2 * ITEMS] = CROSS1_START + 4 * _n


def lead(N):
    return LEAD[N // ITEMS]


def v_slots(N):
    after = range(4) if N // ITEMS == SELF else (0, 1) if N % ITEMS == ITEMS - 1 else (1, 2)
    return [T_SLOT[N] + 4 + i for i in after]


T_IN = {T_SLOT[n] + hh: (n, hh) for n in T_SLOT for hh in range(4)}
S_IN = {T_SLOT[n] - lead(n) + hh: (n, hh) for n in T_SLOT for hh in range(4)}
MAX_IN = {T_SLOT[n] - lead(n) + 4: n for n in T_SLOT}
V_IN = {slot: (n, j) for n in T_SLOT for j, slot in enumerate(v_slots(n))}
OUT_IN = {v_slots(n)[-1] + 1: n for n in T_SLOT}
FIRST_SLOTS = range(-LEAD[CROSS0], max(k for k in OUT_IN if k < CROSS1_START) + 1)
LAST_SLOTS = range(CROSS1_START - LEAD[CROSS1], max(OUT_IN) + 1)


def run_slots(slots, attention_slot, between):
    for slot in slots:
        attention_slot(slot)
        for (first, twice), work in between:
            if slot >= first:
                next(work, None)
                if slot < twice:
                    next(work, None)


def run_all(work):
    for _ in work:
        pass


def build(nc, early, late, consts, vecs, bs1, ws2, b2, bs2, bv, rscale, pad_mask, sub_mask, x, out):
    with ExitStack() as ctx:
        def sb(name, shape, dt=F32):
            return ctx.enter_context(nc.sbuf_tensor(name, shape, dt))

        def sem(name):
            return ctx.enter_context(nc.semaphore(name))

        def sems(name, n):
            return [sem(f"{name}_{i}") for i in range(n)]

        we = sb("we", [P, N_EARLY])
        wl = sb("wl", [P, N_LATE])
        cst = sb("cst", [P, N_CONST])
        vec = sb("vec", [P, len(VECS)])
        bs1_c = sb("bs1_c", [HE, 1])
        w_tail = sb("w_tail", [P, D])
        bv_b = sb("bv_b", [P, D])
        rs_b = sb("rs_b", [P, 1])
        eps_ln = sb("eps_ln", [P, 1])
        eps_rms = sb("eps_rms", [P, 1])
        msk = sb("msk", [P, B, TB, SC], BF16)
        msk_t = sb("msk_t", [KT, B, 2 * S], BF16)
        ident_b = sb("ident_b", [P, P], BF16)
        causal_b = sb("causal_b", [P, P], BF16)
        causal_tb = sb("causal_tb", [P, P], BF16)
        spread_b = sb("spread_b", [3 * E1, 4 * P], BF16)
        ones_b = sb("ones_b", [P, 512], BF16)
        X = sb("X", [P, NT, D])
        Y = sb("Y", [P, NT, D])
        U = sb("U", [P, NT, D])
        yT = sb("yT", [P, B * S])
        f32T = sb("f32T", [P, 2, S])
        sq = sb("sq", [P, 2, S])
        res = sb("res", [P, S])
        parts = sb("parts", [P, 4, 3, S], BF16)
        QA = sb("QA", [P, B * H * S], BF16)
        KS = sb("KS", [P, B * H * S], BF16)
        K1 = sb("K1", [P, KV, B * SC], BF16)
        VS = sb("VS", [P, NT, H, HD + 1])
        V0 = sb("V0", [KT, B, 2, H, HD + 1])
        V1 = sb("V1", [KT, B, 2, KV, HD + 1])
        PR = sb("PR", [P, 2 * 4 * 1280])
        O = sb("O", [P, 2, S])
        tail = sb("tail", [P, S])
        stats = sb("stats", [P, NT, 6])
        mv = sb("mv", [P, NT, 2])
        sm = sb("sm", [P, 6, NT])
        RSTD, VAR2, RMS, LOGV, GSUM, GINV = range(6)
        rden = sb("rden", [P, 2, TB, 4])
        nmax = sb("nmax", [P, 2, 16])
        nres = sb("nres", [P, 2, 16])
        nparts = sb("nparts", [P, 2, 48], BF16)
        nrows = sb("nrows", [48, 2, P], BF16)
        G = sb("G", [P, B, 6, TB, E1])
        gnum = sb("gnum", [P, TB, E1], I32)
        GG = sb("GG", [P, 2, TB, E1, E1])
        gparts = sb("gparts", [P, B, TB, 3, E1], BF16)
        gT = sb("gT", [3 * E1, S], BF16)
        PS = ctx.enter_context(nc.psum_tensor("PS", [P, 8, 512], F32))

        QAv = QA[:, :].rearrange("p (b h s) -> p b h s", b=B, h=H)
        KSv = KS[:, :].rearrange("p (b h s) -> p b h s", b=B, h=H)
        K0_AT, K0_N = H * S, H * B * SC
        K0 = KS[:, K0_AT:K0_AT + K0_N].rearrange("p (h s) -> p h s", h=H)
        K1f = K1[:, :, :].rearrange("p h s -> p (h s)")
        PRv = PR[:, :].rearrange("p (i h s) -> p i h s", i=2, h=4)
        HB = PR[:, 0:16 * S].rearrange("p (c s) -> p c s", s=S)
        sub_z = PR[:, 0:TB * SC].rearrange("p (t k) -> p t k", t=TB)
        sub_i = PR[:, 2 * S:2 * S + TB * SC].bitcast(I32).rearrange("p (t k) -> p t k", t=TB)
        pad_i = PR[:, 4 * S:4 * S + B * SC].bitcast(I32)
        pad_z = PR[:, 5 * S:5 * S + B * SC].rearrange("p (b k) -> p b k", b=B)

        def bank(b, rows=P, n=512, at=0):
            return PS[0:rows, b, at:at + n]

        def bank16(b):
            return PS[:, b, :].bitcast(BF16)

        def W(name, chunk=0, n=D):
            src, (at, size) = (we, EARLY[name]) if name in EARLY else (wl, LATE[name])
            n = min(n, size)
            return src[:, at + chunk * n:at + chunk * n + n]

        def C(name):
            at, n = CONST[name]
            return cst[:, at:at + n]

        def V(name):
            i = VECS.index(name)
            return vec[:, i:i + 1]

        def tokens(b):
            return slice(S * b, S * b + S)

        def tiles(b):
            return slice(TB * b, TB * b + TB)

        ident = C("ident")
        ctxT = we[:, 0:B * SC]
        T_BANKS, S_BANKS, PV_BANK, N_BANK = (0, 1), (3, 4), 5, 7
        SIDE = (2, 6)

        in_x, in_early, in_const, in_vec, in_bv = sems("in_x", B), sem("in_early"), sem("in_const"), sem("in_vec"), sem("in_bv")
        in_mask, in_late, in_tail = sem("in_mask"), sem("in_late"), sem("in_tail")
        eps_set, consts_cast, pv_cleared = sem("eps_set"), sem("consts_cast"), sem("pv_cleared")
        vec_scaled = sem("vec_scaled")
        pool_fills = sem("pool_fills")
        ones_ready = sem("ones_ready")
        stack_fill = sem("stack_fill")
        ctx_mm, ctx_v = sem("ctx_mm"), sem("ctx_v")
        mask_ready, maskt_mm, maskt_ready = sem("mask_ready"), sem("maskt_mm"), sem("maskt_ready")
        stacked = sems("stacked", N_SPLITS)
        stacked3 = sems("stacked3", N_SPLITS)
        var_ready = sems("var_ready", 6)
        rstd_ready = sems("rstd_ready", 6)
        rows_ready = sems("rows_ready", 5)
        rowsT_mm = sems("rowsT_mm", 5)
        rowsT_ready = sems("rowsT_ready", 5)
        proj_mm = sem("proj_mm")
        f32_ready = sem("f32_ready")
        hi_ready = sem("hi_ready")
        split_ready = sem("split_ready")
        sq_ready, ms_mm, rms_ready = sem("sq_ready"), sem("ms_mm"), sem("rms_ready")
        v_mm, v_ready = sem("v_mm"), sem("v_ready")
        s_mm, s_max = sem("s_mm"), sem("s_max")
        nparts_ready, nrows_mm, nrows_ready = sem("nparts_ready"), sem("nrows_mm"), sem("nrows_ready")
        max_rows = sems("max_rows", 2)
        t_mm, probs = sem("t_mm"), sem("probs")
        pv_mm, o_ready = sem("pv_mm"), sem("o_ready")
        oT_mm, ao_ready = sem("oT_mm"), sem("ao_ready")
        aoT_mm, aoT_ready, wo_mm, wo_used = sem("aoT_mm"), sem("aoT_ready"), sem("wo_mm"), sem("wo_used")
        gate_mm, gate_in, gate_exp, gates = sem("gate_mm"), sem("gate_in"), sem("gate_exp"), sem("gates")
        base_ready = sem("base_ready")
        h_mm, h_act, h_times = sem("h_mm"), sem("h_act"), sem("h_times")
        y_mm, y_used = sem("y_mm"), sem("y_used")
        h1_mm, h1_act, h1_gated = sem("h1_mm"), sem("h1_act"), sem("h1_gated")
        gT_mm, gT_ready, spread_mm = sem("gT_mm"), sem("gT_ready"), sem("spread_mm")
        tail_mm, tail_ready = sem("tail_mm"), sem("tail_ready")
        y1_mm, x_final = sem("y1_mm"), sem("x_final")
        dve_step, act_step = sem("dve_step"), sem("act_step")
        written = sem("written")

        block = ctx.enter_context(nc.Block())

        def s_jobs(layer):
            if layer == SELF:
                return [((t,), P * (t + 1)) for t in range(TB)]
            return [((0, 1), SC), ((2, 3), SC)]

        def t_jobs(layer):
            if layer == SELF:
                return [(j, P, P * j, sum(S - P * i for i in range(j))) for j in range(TB)]
            return [(j, KT, 0, S * j) for j in range(2)]

        S_PER = [4 * len(s_jobs(l)) for l in range(3)]
        T_PER = [4 * len(t_jobs(l)) for l in range(3)]
        S_BEFORE = [ITEMS * sum(S_PER[:l]) for l in range(4)]
        T_BEFORE = [ITEMS * sum(T_PER[:l]) for l in range(4)]

        def place(N):
            layer, n = divmod(N, ITEMS)
            return (layer,) + divmod(n, QUADS)

        def s_index(N, hh=0, k=0):
            layer, n = divmod(N, ITEMS)
            return S_BEFORE[layer] + n * S_PER[layer] + hh * S_PER[layer] // 4 + k

        def t_index(N, hh=0, k=0):
            layer, n = divmod(N, ITEMS)
            return T_BEFORE[layer] + n * T_PER[layer] + hh * T_PER[layer] // 4 + k

        def q_split(layer, b):
            return (SP_Q0[b], SP_SELF + 2 * b, SP_Q1 + b)[layer]

        def wait_stacked(e, k):
            e.wait_ge(stacked[k], 16 * 6)
            e.wait_ge(stacked3[k], 16 * 3)

        def stack_dmas(e, k, which):
            if k == SP_K0:
                dst, src, q_side = lambda at: K0[at:at + HD, :, :], lambda i: parts[:, k % 4, i, 0:B * SC], False
            elif k == SP_K1:
                dst, src, q_side = lambda at: K1[at:at + HD, :, :], lambda i: parts[0:KV * HD, k % 4, i, 0:B * SC], False
            else:
                q_side = k < SP_SELF or k >= SP_Q1 or k % 2 == 0
                b = SP_Q0.index(k) if k < SP_SELF else k - SP_Q1 if k >= SP_Q1 else (k - SP_SELF) // 2
                stack = QAv if q_side else KSv
                dst, src = lambda at: stack[at:at + HD, b, :, :], lambda i: parts[:, k % 4, i, :]
            for part in which:
                e.wait_ge(hi_ready if part == 0 else split_ready, k + 1)
                for other in range(3):
                    at = part * 24 + other * HD if q_side else other * 24 + part * HD
                    e.dma_start(dst(at), src(part)).then_inc((stacked if part < 2 else stacked3)[k], 16)

        def run_ffn0(hidden, outputs, gate_work, query_work, ahead=0):
            next(gate_work)
            next(gate_work)
            for k in range(2):
                if k >= ahead:
                    hidden(0, k)
            next(gate_work)
            for k in range(2, N_HIDDEN):
                if k >= ahead:
                    hidden(0, k)
                if k in GATE_STAGES:
                    next(gate_work)
            if outputs:
                outputs(0)
            for k in range(N_HIDDEN):
                if k == len(GELU_JOBS):
                    next(query_work)
                    next(gate_work)
                    next(query_work)
                    run_all(gate_work)
                hidden(1, k)
                if k in QUERY_STAGES:
                    next(query_work)
            if outputs:
                outputs(1)
            run_all(query_work)

        GATE_STAGES, QUERY_STAGES = (5, 8, 10), (8, 11, 13, 14)

        def run_ffn1(hidden, gate_rows, spread, outputs, gate_work):
            def do(part, b):
                if part:
                    part(b)

            next(gate_work)
            do(hidden, 0)
            next(gate_work)
            next(gate_work)
            do(gate_rows, 0)
            next(gate_work)
            do(spread, 0)
            next(gate_work)
            next(gate_work)
            do(outputs, 0)
            next(gate_work)
            do(hidden, 1)
            next(gate_work)
            for part in (gate_rows, spread, outputs):
                do(part, 1)

        TAIL_BANK, GT_BANK = 5, 7

        FILL_K0, FILL_QA0, FILL_QA1, FILL_V, FILL_K1, FILL_KS0, FILL_KS1, FILL_W_TAIL, FILL_TAIL, FILL_VS, FILL_ALL = range(1, 12)

        @block.sync
        def _(sp):
            x_v = x.rearrange("b (t p) d -> b p t d", p=P)
            sp.dma_start(X[:, tiles(0), :], x_v[0]).then_inc(in_x[0], 16)
            sp.dma_start(we[:, :], early).then_inc(in_early, 16)
            sp.dma_start(vec[:, :], vecs).then_inc(in_vec, 16)
            sp.dma_start(cst[:, :], consts).then_inc(in_const, 16)
            sp.dma_start(sub_i, sub_mask.rearrange("(t p) k -> p t k", p=P)).then_inc(in_mask, 16)
            sp.dma_start(pad_i, pad_mask.partition_broadcast(P)).then_inc(in_mask, 16)
            sp.dma_start(X[:, tiles(1), :], x_v[1]).then_inc(in_x[1], 16)
            sp.dma_start(bv_b[:, :], bv.partition_broadcast(P)).then_inc(in_bv, 16)

            sp.wait_ge(pool_fills, FILL_K0)
            stack_dmas(sp, SP_K0, (0, 1))
            sp.wait_ge(ones_ready, 1)
            rest = (B * H * S - K0_AT - K0_N) // 8
            for stack, n, w in ((KS[STACK:TOP, K0_AT:K0_AT + K0_N], H, B * SC), (KS[STACK:TOP, 0:K0_AT], H, S),
                                (KS[STACK:TOP, K0_AT + K0_N:], 8, rest), (K1f[STACK:TOP, :], KV, B * SC)):
                sp.dma_start(stack.rearrange("p (a w) -> p a w", w=w),
                             ones_b[STACK:TOP, 0:w].unsqueeze(1).to_broadcast([3, n, w])).then_inc(stack_fill, 16)
            sp.wait_ge(pool_fills, FILL_QA0)
            stack_dmas(sp, SP_Q0[0], (0, 1))
            sp.wait_ge(pool_fills, FILL_K1)
            stack_dmas(sp, SP_K1, (0, 1))
            stack_dmas(sp, SP_Q0[1], (0, 1))

            def load_weights():
                for piece in range(LATE_PIECES):
                    lo, hi = (N_LATE * (piece + i) // LATE_PIECES for i in range(2))
                    sp.dma_start(wl[:, lo:hi], late[:, lo:hi]).then_inc(in_late, 16)
                    for _ in range(4):
                        yield
                sp.wait_ge(pool_fills, FILL_W_TAIL)
                sp.dma_start(w_tail[0:HE, :], ws2).then_inc(in_tail, 16)
                sp.dma_start(w_tail[HE:HE + E1, :], b2).then_inc(in_tail, 16)
                sp.dma_start(w_tail[96:97, :], bs2).then_inc(in_tail, 16)
                sp.dma_start(bs1_c[:, :], bs1).then_inc(in_tail, 16)
                sp.dma_start(rs_b[:, :], rscale.partition_broadcast(P)).then_inc(in_tail, 16)
                yield

            def prep_self(b):
                for _ in range(9):
                    yield
                sp.wait_ge(pool_fills, FILL_KS1)
                stack_dmas(sp, SP_SELF + 2 * b, (0,))
                yield
                stack_dmas(sp, SP_SELF + 2 * b, (1,))
                stack_dmas(sp, SP_SELF + 2 * b + 1, (0,))
                yield
                stack_dmas(sp, SP_SELF + 2 * b + 1, (1,))
                yield

            def prep_cross1(b):
                for _ in range(5):
                    yield
                stack_dmas(sp, SP_Q1 + b, (0, 1))
                yield

            def attention_slot(slot):
                if slot not in MAX_IN:
                    return
                N = MAX_IN[slot]
                _, b, g = place(N)
                sp.wait_ge(nrows_ready, N + 1)
                sp.dma_start(QAv[STACK:TOP, b, 4 * g:4 * g + 4, :].rearrange("p h (t c) -> p (h t) c", c=P),
                             nrows[:, N % 2, :]).then_inc(max_rows[N % 2], 16)

            run_slots(FIRST_SLOTS, attention_slot, [(START_WEIGHTS, load_weights()), (START_SELF[0], prep_self(0)),
                                              (START_SELF[1], prep_self(1))])
            run_all(prep_cross1(0))
            run_slots(LAST_SLOTS, attention_slot, [(START_CROSS1, prep_cross1(1))])
            out_v = out.rearrange("b (t p) d -> b p t d", p=P)
            for b in range(B):
                sp.wait_ge(x_final, b + 1)
                sp.dma_start(out_v[b], X[:, tiles(b), :]).then_inc(written, 16)
            sp.wait_ge(written, 16 * B)

        @block.gpsimd
        def _(pool):
            fills = [0]

            def fill(view, value, last=True):
                ins = nc.gpsimd.memset(view, value)
                if last:
                    fills[0] += 1
                    ins.then_inc(pool_fills, 1)

            def zero_rows(stack):
                fill(stack.bitcast(F32), 0.0)

            zero_rows(KS[64:STACK, K0_AT:K0_AT + K0_N])
            zero_rows(QA[64:STACK, 0:H * S])
            pool.wait_ge(pool_fills, fills[0])
            stack_dmas(pool, SP_K0, (2,))
            zero_rows(QA[64:STACK, H * S:])
            pool.wait_ge(pool_fills, fills[0])
            stack_dmas(pool, SP_Q0[0], (2,))
            pool.wait_ge(pool_fills, fills[0])
            fill(V0[:, :, :, :, HD], 1.0, last=False)
            fill(V1[:, :, :, :, HD], 1.0)
            pool.wait_ge(pool_fills, fills[0])
            zero_rows(K1f[64:STACK, :])
            pool.wait_ge(pool_fills, fills[0])
            stack_dmas(pool, SP_K1, (2,))
            stack_dmas(pool, SP_Q0[1], (2,))
            zero_rows(KS[64:STACK, 0:K0_AT])
            zero_rows(KS[64:STACK, K0_AT + K0_N:])
            pool.wait_ge(pool_fills, fills[0])
            fill(w_tail[:, :], 0.0)
            pool.wait_ge(pool_fills, fills[0])
            fill(tail[64:P, :], 0.0)
            pool.wait_ge(pool_fills, fills[0])
            fill(VS[:, :, :, HD], 1.0)
            pool.wait_ge(pool_fills, fills[0])
            fill(tail[96:97, :], 1.0)
            for k in range(SP_SELF, SP_SELF + 2 * B):
                stack_dmas(pool, k, (2,))
            for b in range(B):
                pool.wait_ge(wo_used, b + 1)
                nc.gpsimd.tensor_tensor(X[:, tiles(b), :], X[:, tiles(b), :], Y[:, tiles(b), :], ALU.add)\
                    .then_inc(base_ready, 1)
            for b in range(B):
                stack_dmas(pool, SP_Q1 + b, (2,))

        @block.scalar
        def _(act):
            steps = [0]

            def link(ins):
                steps[0] += 1
                ins.then_inc(act_step, 1)
                act.wait_ge(act_step, steps[0])

            def exp_table():
                nc.scalar.preload_act_table_set("natural_log_exp_and_others")

            def inv_sqrt(stage, b, src, to, eps):
                ts = tiles(b)
                act.wait_ge(var_ready[stage], b + 1)
                link(nc.scalar.activation(sm[:, LOGV, ts], src[:, ts], ACT.Ln, bias=eps[:, 0:1]))
                nc.scalar.activation(sm[:, to, ts], sm[:, LOGV, ts], ACT.Exp, scale=-0.5).then_inc(rstd_ready[stage], 1)

            def rows_t(stage, b, scale=None):
                act.wait_ge(rowsT_mm[stage], b + 1)
                if scale is None:
                    ins = nc.scalar.activation(yT[:, tokens(b)], bank(SIDE[0]), ACT.Copy)
                else:
                    ins = nc.scalar.activation(yT[:, tokens(b)], bank(SIDE[0]), ACT.Identity, scale=scale)
                ins.then_inc(rowsT_ready[stage], 1)

            def f32_slot(k):
                if k >= 2:
                    act.wait_ge(split_ready, k - 1)
                return k % 2

            def hi_part(k, rows=P, n=S):
                act.wait_ge(f32_ready, k + 1)
                if k >= 4:
                    wait_stacked(act, k - 4)
                nc.scalar.activation(parts[0:rows, k % 4, 0, 0:n], f32T[0:rows, k % 2, 0:n], ACT.Copy).then_inc(hi_ready, 1)

            def ao_t(k):
                act.wait_ge(aoT_mm, k + 1)
                nc.scalar.activation(yT[:, tokens(k % B)], bank(SIDE[0]), ACT.Copy).then_inc(aoT_ready, 1)

            def attention_slot(slot):
                if slot in OUT_IN:
                    E = OUT_IN[slot]
                    act.wait_ge(pv_mm, E + 1)
                    if E >= 2:
                        act.wait_ge(oT_mm, E - 1)
                    nc.scalar.activation(O[:, E % 2, :], bank(PV_BANK), ACT.Copy).then_inc(o_ready, 1)
                if slot in T_IN:
                    N, hh = T_IN[slot]
                    if N >= 2 and hh == 0:
                        act.wait_ge(pv_mm, N - 1)
                    if N == 2 * ITEMS and hh == 0:
                        act.wait_ge(y_mm, NT)
                    for k, (j, rows, q0, at) in enumerate(t_jobs(N // ITEMS)):
                        tj = t_index(N, hh, k)
                        act.wait_ge(t_mm, tj + 1)
                        nc.scalar.activation(PRv[0:rows, N % 2, hh, at:at + S - q0],
                                             bank(T_BANKS[tj % 2], rows, S - q0, q0), ACT.Exp).then_inc(probs, 1)
                if slot in MAX_IN:
                    M = MAX_IN[slot]
                    act.wait_ge(nrows_mm, M + 1)
                    if M >= 2:
                        act.wait_ge(max_rows[M % 2], 16 * (M // 2))
                    nc.scalar.activation(nrows[:, M % 2, :], bank16(N_BANK)[0:48, 0:P], ACT.Copy).then_inc(nrows_ready, 1)

            def keys_of_context(k, done, at, rows, bias):
                act.wait_ge(ctx_mm, done)
                dst = f32T[0:rows, f32_slot(k), 0:B * SC]
                if bias is None:
                    nc.scalar.activation(dst, bank(at, rows, B * SC), ACT.Copy).then_inc(f32_ready, 1)
                else:
                    nc.scalar.activation(dst, bank(at, rows, B * SC), ACT.Identity, bias=bias).then_inc(f32_ready, 1)
                hi_part(k, rows, B * SC)

            def prep_cross0(b):
                yield
                inv_sqrt(N_CROSS0, b, mv[:, :, 1], RSTD, eps_ln)
                yield
                yield
                rows_t(T_CROSS0, b)
                yield
                act.wait_ge(proj_mm, b + 1)
                nc.scalar.activation(f32T[:, f32_slot(SP_Q0[b]), :], bank(SIDE[1]), ACT.Identity, bias=V("x0_bq"),
                                     scale=HD ** -0.5).then_inc(f32_ready, 1)
                hi_part(SP_Q0[b])
                yield
                yield

            def prep_self(b):
                def raw(r):
                    k = 2 * b + r
                    act.wait_ge(proj_mm, 3 + k)
                    nc.scalar.activation(f32T[:, f32_slot(SP_SELF + k), :], bank(SIDE[1 - r]), ACT.Copy)
                    nc.scalar.activation(sq[:, r, :], bank(SIDE[1 - r]), ACT.Square).then_inc(sq_ready, 1)

                def inv_rms(r):
                    act.wait_ge(ms_mm, 2 * b + r + 1)
                    link(nc.scalar.activation(sq[:, r, :], bank(SIDE[1 - r]), ACT.Ln, bias=eps_rms[:, 0:1]))
                    nc.scalar.activation(sq[:, r, :], sq[:, r, :], ACT.Exp, scale=-0.5).then_inc(rms_ready, 1)

                yield
                inv_sqrt(N_SELF, b, mv[:, :, 1], RSTD, eps_ln)
                yield
                yield
                inv_sqrt(R_SELF, b, sm[:, VAR2, :], RMS, eps_rms)
                yield
                yield
                rows_t(T_SELF, b, V("n1"))
                yield
                raw(0)
                yield
                raw(1)
                inv_rms(0)
                yield
                inv_rms(1)
                yield
                hi_part(SP_SELF + 2 * b)
                yield
                hi_part(SP_SELF + 2 * b + 1)
                yield
                yield

            def ffn0_in(b):
                ao_t(b)
                yield
                yield
                inv_sqrt(R_FFN0, b, sm[:, VAR2, :], RMS, eps_rms)
                yield
                yield
                rows_t(T_FFN0, b, V("n2"))
                yield
                yield
                if b:
                    exp_table()
                act.wait_ge(gate_in, b + 1)
                nc.scalar.activation(G[:, b, 1, :, 0:E0], G[:, b, 0, :, 0:E0], ACT.Exp).then_inc(gate_exp, 1)
                yield
                yield

            def prep_cross1(b):
                yield
                inv_sqrt(N_CROSS1, b, mv[:, :, 1], RSTD, eps_ln)
                yield
                yield
                rows_t(T_CROSS1, b)
                yield
                act.wait_ge(proj_mm, 7 + b)
                k = SP_Q1 + b
                nc.scalar.activation(f32T[:, f32_slot(k), :], bank(SIDE[1]), ACT.Copy, scale=HD ** -0.5).then_inc(f32_ready, 1)
                hi_part(k)
                yield
                yield

            def ffn1_in(b):
                ao_t(B + b)
                yield
                yield
                if b:
                    exp_table()
                inv_sqrt(N_FFN1, b, mv[:, :, 1], RSTD, eps_ln)
                yield
                yield
                rows_t(T_FFN1, b)
                yield
                yield
                act.wait_ge(gate_in, B + b + 1)
                nc.scalar.activation(G[:, b, 1, :, :], G[:, b, 0, :, :], ACT.Exp, scale=-1.0).then_inc(gate_exp, 1)
                yield
                yield

            def hidden(b, k):
                _, _, _, dst, func = HIDDEN[b][k]
                if func == "times":
                    return
                if k == 0 and b == 0:
                    act.wait_ge(pv_mm, 2 * ITEMS)
                if k == 0 and b == 1:
                    act.wait_ge(y_mm, TB * b)
                act.wait_ge(h_mm, b * N_HIDDEN + k + 1)
                nc.scalar.activation(HB[:, dst, :], bank(H_BANKS[(b * N_HIDDEN + k) % 4]), func).then_inc(h_act, 1)

            def hidden1(b):
                for c in range(4):
                    if b == 0 and c == 0:
                        act.wait_ge(pv_mm, 3 * ITEMS)
                    act.wait_ge(h1_mm, 4 * b + c + 1)
                    nc.scalar.activation(HB[:, 4 * b + c, :], bank(H_BANKS[c]), ACT.Gelu, bias=V(f"b1_{c}")).then_inc(h1_act, 1)
                act.wait_ge(tail_mm, b + 1)
                if b:
                    act.wait_ge(y1_mm, b)
                nc.scalar.activation(tail[0:HE, :], bank(TAIL_BANK, HE), ACT.Gelu, bias=bs1_c[:, 0:1]).then_inc(tail_ready, 1)

            exp_table()
            act.wait_ge(in_vec, 16)
            act.wait_ge(eps_set, 1)
            keys_of_context(SP_K0, 1, 0, P, V("x0_bk"))
            act.wait_ge(vec_scaled, 1)
            first, second = prep_cross0(0), prep_cross0(1)
            for _ in range(5):
                next(first)
            for _ in range(4):
                next(second)
            keys_of_context(SP_K1, 2, N_BANK, KV * HD, None)
            run_all(second)
            for b in range(B):
                act.wait_ge(maskt_mm, b + 1)
                nc.scalar.activation(msk_t[:, b, :], bank16(T_BANKS[b])[0:KT, 0:2 * S], ACT.Copy).then_inc(maskt_ready, 1)

            run_slots(FIRST_SLOTS, attention_slot, [(START_SELF[0], prep_self(0)), (START_SELF[1], prep_self(1)),
                                              (START_FFN0, ffn0_in(0))])
            run_ffn0(hidden, None, ffn0_in(1), prep_cross1(0))
            exp_table()
            run_slots(LAST_SLOTS, attention_slot, [(START_CROSS1, prep_cross1(1)), (START_FFN1, ffn1_in(0))])
            act.wait_ge(in_tail, 16 * 5)
            act.wait_ge(pool_fills, FILL_ALL)
            run_ffn1(hidden1, None, None, None, ffn1_in(1))

        @block.tensor
        def _(pe):
            mm, tr = nc.tensor.matmul, nc.tensor.transpose
            reader = {}

            def side(i, sem, value):
                if i in reader:
                    pe.wait_ge(*reader[i])
                reader[i] = (sem, value)
                return SIDE[i]

            def transposes(src, bk, b, done):
                for t in range(TB):
                    last = tr(bank(bk, P, P, P * t), src[:, TB * b + t, :], ident)
                last.then_inc(done, 1)

            def rows_t(stage, b, src):
                pe.wait_ge(rows_ready[stage], b + 1)
                transposes(src, side(0, rowsT_ready[stage], b + 1), b, rowsT_mm[stage])

            def by_tile(bk, b, w, n):
                for t in range(TB):
                    last = mm(bank(bk, P, n, n * t), yT[:, S * b + P * t:S * b + P * t + P], w, start=True, stop=True)
                return last

            def s_job(N, hh, k):
                layer, b, g = place(N)
                h = 4 * g + hh
                if g == hh == k == 0:
                    wait_stacked(pe, q_split(layer, b))
                    if layer == SELF:
                        wait_stacked(pe, SP_SELF + 2 * b + 1)
                        pe.wait_ge(pool_fills, FILL_ALL)
                        pe.wait_ge(consts_cast, 2)
                    if layer == CROSS1:
                        wait_stacked(pe, SP_K1)
                ts, w = s_jobs(layer)[k]
                sj = s_index(N, hh, k)
                bk = S_BANKS[sj % 2]
                if sj >= 2:
                    pe.wait_ge(s_max, sj - 1)
                for i, t in enumerate(ts):
                    q = QAv[0:STACK, b, h, P * t:P * t + P]
                    if layer == SELF:
                        keys = KSv[0:STACK, b, h, 0:w]
                    elif layer == CROSS0:
                        keys = K0[0:STACK, h, SC * b:SC * b + SC]
                    else:
                        keys = K1[0:STACK, g, SC * b:SC * b + SC]
                    last = mm(bank(bk, P, w, w * i), q, keys, start=True, stop=layer == CROSS1)
                    if layer == CROSS0:
                        last = mm(bank(bk, P, w, w * i), ident_b[:, :], msk[:, b, t, :], start=False, stop=True)
                    if layer == SELF:
                        last = mm(bank(bk, P, P, P * t), ident_b[:, :], causal_b[:, :], start=False, stop=True)
                last.then_inc(s_mm, 1)

            def maxima(N):
                pe.wait_ge(nparts_ready, N + 1)
                if N == 0:
                    pe.wait_ge(f32_ready, SP_K1 + 1)
                else:
                    pe.wait_ge(nrows_ready, N)
                tr(bank16(N_BANK)[0:48, 0:P], nparts[:, N % 2, :], ident_b[:, :]).then_inc(nrows_mm, 1)

            def t_job(N, hh, k):
                layer, b, g = place(N)
                h = 4 * g + hh
                if hh == k == 0:
                    pe.wait_ge(max_rows[N % 2], 16 * (N // 2 + 1))
                j, rows, q0, _ = t_jobs(layer)[k]
                tj = t_index(N, hh, k)
                bk = T_BANKS[tj % 2]
                if tj >= 2:
                    pe.wait_ge(probs, tj - 1)
                if layer == SELF:
                    keys = KSv[0:TOP, b, h, P * j:P * j + P]
                elif layer == CROSS0:
                    keys = K0[0:TOP, h, SC * b + CT[j]:SC * b + CT[j] + KT]
                else:
                    keys = K1[0:TOP, g, SC * b + CT[j]:SC * b + CT[j] + KT]
                last = mm(bank(bk, rows, S - q0, q0), keys, QAv[0:TOP, b, h, q0:S], start=True, stop=layer == CROSS1)
                if layer == CROSS0:
                    last = mm(bank(bk, rows), ident_b[0:KT, 0:KT], msk_t[:, b, S * j:S * j + S], start=False, stop=True)
                if layer == SELF:
                    last = mm(bank(bk, rows, P, q0), ident_b[:, :], causal_tb[:, :], start=False, stop=True)
                last.then_inc(t_mm, 1)

            def pass_v(N, tile):
                layer, b, g = place(N)
                jobs = t_jobs(layer)
                j, rows, q0, at = jobs[tile]
                if tile == 0:
                    pe.wait_ge(probs, t_index(N) + T_PER[layer])
                    if N >= 1:
                        pe.wait_ge(o_ready, N)
                for head in range(4):
                    if layer == SELF:
                        v = VS[:, TB * b + j, 4 * g + head, :]
                    elif layer == CROSS0:
                        v = V0[:, b, j, 4 * g + head, :]
                    else:
                        v = V1[:, b, j, g, :]
                    last = mm(PS[32 * head:32 * head + HD + 1, PV_BANK, q0:S], v,
                              PRv[0:rows, N % 2, head, at:at + S - q0], start=j == 0, stop=j == len(jobs) - 1)
                if j == len(jobs) - 1:
                    last.then_inc(pv_mm, 1)

            def heads_to_rows(N):
                pe.wait_ge(o_ready, N + 1)
                bk = side(0, ao_ready, N + 1)
                for t in range(TB):
                    last = tr(bank(bk, P, P, P * t), O[:, N % 2, P * t:P * t + P], ident)
                last.then_inc(oT_mm, 1)

            def attention_slot(slot):
                n_s = len(s_jobs(S_IN[slot][0] // ITEMS)) if slot in S_IN else 0
                n_t = len(t_jobs(T_IN[slot][0] // ITEMS)) if slot in T_IN else 0
                for k in range(max(n_s, n_t, 2)):
                    if k < n_s:
                        s_job(*S_IN[slot], k)
                    if k < n_t:
                        t_job(*T_IN[slot], k)
                    if k == 1 and slot in V_IN:
                        pass_v(*V_IN[slot])
                if slot in MAX_IN:
                    maxima(MAX_IN[slot])
                if slot in OUT_IN:
                    heads_to_rows(OUT_IN[slot])

            def prep_cross0(b):
                yield
                yield
                yield
                rows_t(T_CROSS0, b, Y)
                yield
                pe.wait_ge(rowsT_ready[T_CROSS0], b + 1)
                bk = side(1, f32_ready, SP_Q0[b] + 1)
                mm(bank(bk), W("x0_q"), yT[:, tokens(b)], start=True, stop=True).then_inc(proj_mm, 1)
                yield
                yield

            def prep_self(b):
                for _ in range(5):
                    yield
                rows_t(T_SELF, b, U)
                yield
                pe.wait_ge(in_late, 16 * LATE_PIECES)
                pe.wait_ge(rowsT_ready[T_SELF], b + 1)
                for r, w in enumerate(("wq", "wk")):
                    bk = side(1 - r, sq_ready, 2 * b + r + 1)
                    mm(bank(bk), W(w), yT[:, tokens(b)], start=True, stop=True).then_inc(proj_mm, 1)
                yield
                for r in range(2):
                    k = 2 * b + r
                    bk = side(1 - r, rms_ready, k + 1)
                    pe.wait_ge(sq_ready, k + 1)
                    mm(bank(bk), C("head_mean"), sq[:, r, :], start=True, stop=True).then_inc(ms_mm, 1)
                    yield
                by_tile(side(1, v_ready, b + 1), b, W("wv"), D).then_inc(v_mm, 1)
                yield
                yield
                yield

            def ffn0_in(b):
                pe.wait_ge(ao_ready, ITEMS + QUADS * (b + 1))
                transposes(U, side(0, aoT_ready, b + 1), b, aoT_mm)
                yield
                pe.wait_ge(aoT_ready, b + 1)
                at = LATE["wo"][0]
                by_tile(side(1, wo_used, b + 1), b, wl[:, at + KEEP:at + D], OC).then_inc(wo_mm, 1)
                yield
                yield
                yield
                rows_t(T_FFN0, b, U)
                yield
                pe.wait_ge(rowsT_ready[T_FFN0], b + 1)
                by_tile(side(1, gate_in, b + 1), b, W("gate0"), E0).then_inc(gate_mm, 1)
                yield
                yield
                yield

            def prep_cross1(b):
                yield
                yield
                yield
                rows_t(T_CROSS1, b, Y)
                yield
                pe.wait_ge(rowsT_ready[T_CROSS1], b + 1)
                bk = side(1, f32_ready, SP_Q1 + b + 1)
                mm(bank(bk), W("x1_q"), yT[:, tokens(b)], start=True, stop=True).then_inc(proj_mm, 1)
                yield
                yield

            def ffn1_in(b):
                pe.wait_ge(ao_ready, 2 * ITEMS + QUADS * (b + 1))
                transposes(U, side(0, aoT_ready, B + b + 1), b, aoT_mm)
                yield
                pe.wait_ge(aoT_ready, B + b + 1)
                by_tile(side(1, wo_used, B + b + 1), b, W("x1_o"), D).then_inc(wo_mm, 1)
                yield
                yield
                yield
                rows_t(T_FFN1, b, Y)
                yield
                pe.wait_ge(rowsT_ready[T_FFN1], b + 1)
                by_tile(side(1, gate_in, B + b + 1), b, W("gate1"), E1).then_inc(gate_mm, 1)
                yield
                yield
                yield

            def hidden(b, k):
                w, chunks, srcs, _, _ = HIDDEN[b][k]
                job = b * N_HIDDEN + k
                if job == 0:
                    pe.wait_ge(probs, T_BEFORE[CROSS1])
                    pe.wait_ge(s_max, S_BEFORE[CROSS1])
                if job >= 4:
                    fb, fk = divmod(job - 4, N_HIDDEN)
                    if HIDDEN[fb][fk][4] == "times":
                        pe.wait_ge(h_times, by_dve(fb, fk))
                    else:
                        pe.wait_ge(h_act, by_act(fb, fk))
                bk = H_BANKS[job % 4]
                if srcs is None:
                    last = mm(bank(bk), W(w, chunks[0]), yT[:, tokens(b)], start=True, stop=True)
                else:
                    pe.wait_ge(h_act, by_act(b, max(i for i, h in enumerate(HIDDEN[b]) if h[3] in srcs)))
                    for i, s in enumerate(srcs):
                        last = mm(bank(bk), W(w, chunks[i]), HB[:, s, :], start=i == 0, stop=i == len(srcs) - 1)
                last.then_inc(h_mm, 1)

            def outputs(b):
                pe.wait_ge(h_act, by_act(b, N_HIDDEN - 1))
                pe.wait_ge(h_times, by_dve(b, N_HIDDEN - 1))
                if b == 0:
                    pe.wait_ge(o_ready, 2 * ITEMS)
                    pe.wait_ge(nrows_ready, 2 * ITEMS)
                for t in range(TB):
                    k = TB * b + t
                    if k >= 2:
                        pe.wait_ge(y_used, k - 1)
                    for e, (w, srcs) in enumerate(OUTPUTS):
                        at = LATE[w][0]
                        for i, s in enumerate(srcs):
                            last = mm(bank(OUT_BANKS[k % 2], P, OC, OC * e), HB[:, s, P * t:P * t + P],
                                      wl[:, at + D * i + KEEP:at + D * i + D], start=i == 0, stop=i == 1)
                    last.then_inc(y_mm, 1)

            def hidden1(b):
                if b == 0:
                    pe.wait_ge(in_tail, 16 * 5)
                    pe.wait_ge(probs, T_BEFORE[3])
                    pe.wait_ge(s_max, S_BEFORE[3])
                    pe.wait_ge(o_ready, 3 * ITEMS)
                for c in range(4):
                    if b:
                        pe.wait_ge(h1_act, 4 * (b - 1) + c + 1)
                    mm(bank(H_BANKS[c]), W("w1", c), yT[:, tokens(b)], start=True, stop=True).then_inc(h1_mm, 1)
                if b:
                    pe.wait_ge(x_final, b)
                mm(bank(TAIL_BANK, HE), W("ws1"), yT[:, tokens(b)], start=True, stop=True).then_inc(tail_mm, 1)

            def gate_rows(b):
                pe.wait_ge(gates, b + 1)
                if b == 0:
                    pe.wait_ge(nrows_ready, 3 * ITEMS)
                else:
                    pe.wait_ge(h1_gated, 4 * b)
                for t in range(TB):
                    tr(bank16(GT_BANK)[0:3 * E1, P * t:P * t + P], gparts[:, b, t, :, :].rearrange("p a e -> p (a e)"), ident_b[:, :])
                bk = side(1, gT_ready, 2 * b + 2)
                for t in range(TB):
                    last = tr(bank(bk, E1, P, P * t), G[:, b, 5, t, :], ident)
                last.then_inc(gT_mm, 1)

            def spread(b):
                pe.wait_ge(gT_ready, 2 * b + 1)
                for c in range(4):
                    if c % 2:
                        bk = side(0, h1_gated, 4 * b + c + 1)
                    else:
                        bk = GT_BANK
                        if c:
                            pe.wait_ge(h1_gated, 4 * b + c - 1)
                    mm(bank(bk), spread_b[:, P * c:P * c + P], gT[:, :], start=True, stop=True).then_inc(spread_mm, 1)

            def outputs1(b):
                pe.wait_ge(gT_ready, 2 * b + 2)
                pe.wait_ge(h1_gated, 4 * (b + 1))
                pe.wait_ge(tail_ready, b + 1)
                for t in range(TB):
                    cols = slice(P * t, P * t + P)
                    for c in range(4):
                        mm(bank(TAIL_BANK, P, D, D * t), HB[:, 4 * b + c, cols], W("w2", c), start=c == 0, stop=False)
                    last = mm(bank(TAIL_BANK, P, D, D * t), tail[0:97, cols], w_tail[0:97, :], start=False, stop=True)
                last.then_inc(y1_mm, 1)

            pe.wait_ge(in_early, 16)
            mm(bank(0, P, B * SC), W("x0_k"), ctxT, start=True, stop=True).then_inc(ctx_mm, 1)
            mm(bank(N_BANK, KV * HD, B * SC), W("x1_k"), ctxT, start=True, stop=True).then_inc(ctx_mm, 1)
            pe.wait_ge(in_const, 16)
            first, second = prep_cross0(0), prep_cross0(1)
            for _ in range(5):
                next(first)
            for _ in range(4):
                next(second)
            for b in range(B):
                for j in range(2):
                    keys = ctxT[:, SC * b + CT[j]:SC * b + CT[j] + KT]
                    mm(bank(3, KT, D, D * (2 * b + j)), keys, W("x0_v"), start=True, stop=True)
                    last = mm(bank(4, KT, KV * HD, KV * HD * (2 * b + j)), keys, W("x1_v"), start=True, stop=True)
            last.then_inc(ctx_mm, 1)
            run_all(second)
            pe.wait_ge(consts_cast, 1)
            pe.wait_ge(f32_ready, SP_K0 + 1)
            for b in range(B):
                pe.wait_ge(mask_ready, b + 1)
                for j in range(2):
                    for t in range(TB):
                        last = tr(bank16(T_BANKS[b])[0:KT, S * j + P * t:S * j + P * t + P],
                                  msk[:, b, t, CT[j]:CT[j] + KT], ident_b[:, :])
                last.then_inc(maskt_mm, 1)
            wait_stacked(pe, SP_K0)
            pe.wait_ge(stack_fill, 16 * 4)
            pe.wait_ge(ctx_v, 1)
            pe.wait_ge(maskt_ready, 2)
            pe.wait_ge(pv_cleared, 1)

            def first_hidden():
                for k in range(len(H_BANKS)):
                    hidden(0, k)
                    yield

            run_slots(FIRST_SLOTS, attention_slot, [(START_SELF[0], prep_self(0)), (START_SELF[1], prep_self(1)),
                                                    (START_FFN0, ffn0_in(0)), (START_HIDDEN, first_hidden())])
            run_ffn0(hidden, outputs, ffn0_in(1), prep_cross1(0), ahead=len(H_BANKS))
            pe.wait_ge(h_act, by_act(1, N_HIDDEN - 1))
            pe.wait_ge(h_times, by_dve(1, N_HIDDEN - 1))
            pe.wait_ge(y_used, NT)
            run_slots(LAST_SLOTS, attention_slot, [(START_CROSS1, prep_cross1(1)), (START_FFN1, ffn1_in(0))])
            run_ffn1(hidden1, gate_rows, spread, outputs1, ffn1_in(1))

        @block.vector
        def _(dve):
            steps = [0]

            def link(ins):
                steps[0] += 1
                ins.then_inc(dve_step, 1)
                dve.wait_ge(dve_step, steps[0])

            def statistics(src, b):
                for t in range(TB * b, TB * b + TB):
                    last = nc.vector.bn_stats(stats[:, t, :], src[:, t, :])
                link(last)
                for t in range(TB * b, TB * b + TB):
                    last = nc.vector.bn_aggr(mv[:, t, :], stats[:, t, :])
                return last

            def normalise(stage, b):
                dve.wait_ge(rstd_ready[stage], b + 1)
                for t in range(TB * b, TB * b + TB):
                    last = nc.vector.tensor_scalar(Y[:, t, :], X[:, t, :], mv[:, t, 0:1], sm[:, RSTD, t:t + 1],
                                                   ALU.subtract, ALU.mult)
                return last

            def rms_scale(stage, b):
                dve.wait_ge(rstd_ready[stage], b + 1)
                for t in range(TB * b, TB * b + TB):
                    last = nc.vector.tensor_scalar(U[:, t, :], Y[:, t, :], sm[:, RMS, t:t + 1], None, ALU.mult)
                return last

            def split(k, rows=P, n=S):
                p = [parts[0:rows, k % 4, i, 0:n] for i in range(3)]
                r = res[0:rows, 0:n]
                dve.wait_ge(hi_ready, k + 1)
                dve.wait_ge(split_ready, k)
                link(nc.vector.tensor_tensor(r, f32T[0:rows, k % 2, 0:n], p[0], ALU.subtract))
                link(nc.vector.tensor_copy(p[1], r))
                nc.vector.tensor_tensor(p[2], r, p[1], ALU.subtract).then_inc(split_ready, 1)

            def reduce(N, hh):
                for k, (ts, w) in enumerate(s_jobs(N // ITEMS)):
                    sj = s_index(N, hh, k)
                    dve.wait_ge(s_mm, sj + 1)
                    at = 4 * hh + ts[0]
                    nc.vector.tensor_reduce(nmax[:, N % 2, at:at + len(ts)],
                                            PS[:, S_BANKS[sj % 2], 0:w * len(ts)].rearrange("p (t k) -> p t k", k=w),
                                            AX.X, ALU.max, negate=True).then_inc(s_max, 1)

            def split_max(N):
                src, r = nmax[:, N % 2, :], nres[:, N % 2, :]
                p = [nparts[:, N % 2, 16 * i:16 * i + 16] for i in range(3)]
                dve.wait_ge(s_max, s_index(N) + S_PER[N // ITEMS])
                if N >= 2:
                    dve.wait_ge(nrows_mm, N - 1)
                link(nc.vector.tensor_copy(p[0], src))
                link(nc.vector.tensor_tensor(r, src, p[0], ALU.subtract))
                link(nc.vector.tensor_copy(p[1], r))
                nc.vector.tensor_tensor(p[2], r, p[1], ALU.subtract).then_inc(nparts_ready, 1)

            def rows_of_heads(N):
                _, b, g = place(N)
                dve.wait_ge(oT_mm, N + 1)
                v = PS[:, SIDE[0], :].rearrange("p (t h c) -> p t h c", t=TB, c=32)
                r = rden[:, N % 2, :, :]
                link(nc.vector.reciprocal(r, v[:, :, :, HD]))
                nc.vector.tensor_tensor(U[:, tiles(b), 4 * HD * g:4 * HD * g + 4 * HD].rearrange("p t (h d) -> p t h d", d=HD),
                                        v[:, :, :, 0:HD], r.unsqueeze(3).to_broadcast([P, TB, 4, HD]), ALU.mult)\
                    .then_inc(ao_ready, 1)

            def attention_slot(slot):
                if slot in S_IN:
                    N, hh = S_IN[slot]
                    reduce(N, hh)
                    if hh == 3:
                        split_max(N)
                if slot in OUT_IN:
                    rows_of_heads(OUT_IN[slot])

            def top2(b, prob, E, before, guard):
                g, q = GG[:, 0, :, 0:E, 0:E], GG[:, 1, :, 0:E, 0:E]
                pj = prob.unsqueeze(2).to_broadcast([P, TB, E, E])
                pi = prob.unsqueeze(3).to_broadcast([P, TB, E, E])
                lt = before.rearrange("p (i j) -> p i j", j=E).unsqueeze(1).to_broadcast([P, TB, E, E])
                nc.vector.tensor_tensor(g, pj, pi, ALU.is_gt)
                link(nc.vector.tensor_tensor(q, pj, pi, ALU.is_equal))
                link(nc.vector.tensor_tensor(q, q, lt, ALU.mult))
                link(nc.vector.tensor_tensor(g, g, q, ALU.add))
                link(nc.vector.tensor_reduce(G[:, b, 2, :, 0:E], g, AX.X, ALU.add))
                link(nc.vector.scalar_tensor_tensor(out=G[:, b, 3, :, 0:E], in0=G[:, b, 2, :, 0:E], scalar=2.0, in1=prob,
                                                    op0=ALU.is_lt, op1=ALU.mult))
                link(nc.vector.tensor_reduce(sm[:, GSUM, 0:TB], G[:, b, 3, :, 0:E], AX.X, ALU.add))
                if guard:
                    link(nc.vector.tensor_scalar(sm[:, GSUM, 0:TB], sm[:, GSUM, 0:TB], guard, None, ALU.add))
                link(nc.vector.reciprocal(sm[:, GINV, 0:TB], sm[:, GSUM, 0:TB]))
                link(nc.vector.tensor_tensor(G[:, b, 5, :, 0:E], G[:, b, 3, :, 0:E],
                                             sm[:, GINV, 0:TB].unsqueeze(2).to_broadcast([P, TB, E]), ALU.mult))

            def prep_cross0(b):
                dve.wait_ge(in_x[b], 16)
                statistics(X, b).then_inc(var_ready[N_CROSS0], 1)
                yield
                yield
                normalise(N_CROSS0, b).then_inc(rows_ready[T_CROSS0], 1)
                yield
                yield
                yield
                split(SP_Q0[b])
                yield

            def prep_self(b):
                ts = tiles(b)
                dve.wait_ge(ao_ready, QUADS * (b + 1))
                link(nc.vector.tensor_tensor(X[:, ts, :], X[:, ts, :], U[:, ts, :], ALU.add))
                statistics(X, b).then_inc(var_ready[N_SELF], 1)
                yield
                yield
                dve.wait_ge(rstd_ready[N_SELF], b + 1)
                link(nc.vector.tensor_tensor(sm[:, VAR2, ts], mv[:, ts, 1], sm[:, RSTD, ts], ALU.mult))
                nc.vector.tensor_tensor(sm[:, VAR2, ts], sm[:, VAR2, ts], sm[:, RSTD, ts], ALU.mult)\
                    .then_inc(var_ready[R_SELF], 1)
                link(normalise(N_SELF, b))
                yield
                yield
                rms_scale(R_SELF, b).then_inc(rows_ready[T_SELF], 1)
                yield
                yield
                yield
                yield

                def norm(r, w):
                    k = 2 * b + r
                    dve.wait_ge(rms_ready, k + 1)
                    f = f32T[:, (SP_SELF + k) % 2, :]
                    nc.vector.scalar_tensor_tensor(out=f, in0=f, scalar=V(w), in1=sq[:, r, :],
                                                   op0=ALU.mult, op1=ALU.mult).then_inc(f32_ready, 1)

                norm(0, "qn")
                yield
                norm(1, "kn")
                yield
                split(SP_SELF + 2 * b)
                dve.wait_ge(v_mm, b + 1)
                nc.vector.tensor_copy(VS[:, ts, :, 0:HD],
                                      bank(SIDE[1]).rearrange("p (t h d) -> p t h d", t=TB, h=H)).then_inc(v_ready, 1)
                yield
                split(SP_SELF + 2 * b + 1)
                yield

            def ffn0_in(b):
                ts = tiles(b)
                yield
                dve.wait_ge(wo_mm, b + 1)
                nc.vector.tensor_tensor(Y[:, ts, KEEP:D], Y[:, ts, KEEP:D],
                                        bank(SIDE[1], P, TB * OC).rearrange("p (t d) -> p t d", t=TB), ALU.add)\
                    .then_inc(wo_used, 1)
                dve.wait_ge(wo_used, b + 1)
                link(statistics(Y, b))
                link(nc.vector.tensor_tensor(sm[:, VAR2, ts], mv[:, ts, 0], mv[:, ts, 0], ALU.mult))
                nc.vector.tensor_tensor(sm[:, VAR2, ts], sm[:, VAR2, ts], mv[:, ts, 1], ALU.add).then_inc(var_ready[R_FFN0], 1)
                yield
                yield
                rms_scale(R_FFN0, b).then_inc(rows_ready[T_FFN0], 1)
                yield
                yield
                dve.wait_ge(gate_mm, b + 1)
                logits = bank(SIDE[1], P, TB * E0).rearrange("p (t e) -> p t e", e=E0)
                z, raw, num = G[:, b, 0, :, 0:E0], G[:, b, 4, :, 0:E0], gnum[:, :, 0:E0]
                nc.vector.memset(z, 0.0)
                link(nc.vector.tensor_copy(raw, logits))
                link(nc.vector.tensor_tensor(num, raw, raw, ALU.is_equal))
                link(nc.vector.copy_predicated(z, num, raw))
                link(nc.vector.tensor_scalar(z, z, -FLT_MAX, FLT_MAX, ALU.max, ALU.min))
                link(nc.vector.tensor_reduce(sm[:, GSUM, 0:TB], z, AX.X, ALU.max))
                nc.vector.tensor_tensor(z, z, sm[:, GSUM, 0:TB].unsqueeze(2).to_broadcast([P, TB, E0]), ALU.subtract)\
                    .then_inc(gate_in, 1)
                yield
                yield
                dve.wait_ge(gate_exp, b + 1)
                e = G[:, b, 1, :, 0:E0]
                link(nc.vector.tensor_reduce(sm[:, GSUM, 0:TB], e, AX.X, ALU.add))
                link(nc.vector.reciprocal(sm[:, GINV, 0:TB], sm[:, GSUM, 0:TB]))
                link(nc.vector.tensor_tensor(raw, e, sm[:, GINV, 0:TB].unsqueeze(2).to_broadcast([P, TB, E0]), ALU.mult))
                top2(b, raw, E0, C("before0"), 1e-8)
                yield

            def prep_cross1(b):
                dve.wait_ge(y_used, TB * (b + 1))
                statistics(X, b).then_inc(var_ready[N_CROSS1], 1)
                yield
                yield
                normalise(N_CROSS1, b).then_inc(rows_ready[T_CROSS1], 1)
                yield
                yield
                yield
                split(SP_Q1 + b)
                yield

            def ffn1_in(b):
                ts = tiles(b)
                yield
                dve.wait_ge(wo_mm, B + b + 1)
                nc.vector.tensor_tensor(X[:, ts, :], X[:, ts, :], bank(SIDE[1]).rearrange("p (t d) -> p t d", t=TB), ALU.add)\
                    .then_inc(wo_used, 1)
                dve.wait_ge(wo_used, B + b + 1)
                statistics(X, b).then_inc(var_ready[N_FFN1], 1)
                yield
                yield
                normalise(N_FFN1, b).then_inc(rows_ready[T_FFN1], 1)
                yield
                yield
                dve.wait_ge(gate_mm, B + b + 1)
                nc.vector.tensor_copy(G[:, b, 0, :, :], bank(SIDE[1], P, TB * E1).rearrange("p (t e) -> p t e", e=E1))\
                    .then_inc(gate_in, 1)
                yield
                yield
                dve.wait_ge(in_tail, 16 * 5)
                dve.wait_ge(gate_exp, B + b + 1)
                g4, g5, gp = G[:, b, 4, :, :], G[:, b, 5, :, :], gparts[:, b]
                link(nc.vector.tensor_scalar(G[:, b, 1, :, :], G[:, b, 1, :, :], 1.0, None, ALU.add))
                link(nc.vector.reciprocal(g4, G[:, b, 1, :, :]))
                link(nc.vector.tensor_scalar(g4, g4, rs_b[:, 0:1], None, ALU.mult))
                top2(b, g4, E1, C("before1"), None)
                link(nc.vector.tensor_copy(gp[:, :, 0, :], g5))
                link(nc.vector.tensor_tensor(g4, g5, gp[:, :, 0, :], ALU.subtract))
                link(nc.vector.tensor_copy(gp[:, :, 1, :], g4))
                nc.vector.tensor_tensor(gp[:, :, 2, :], g4, gp[:, :, 1, :], ALU.subtract).then_inc(gates, 1)
                yield

            def hidden(b, k):
                _, _, _, dst, func = HIDDEN[b][k]
                if func == "times":
                    dve.wait_ge(h_act, by_act(b, k))
                    dve.wait_ge(h_mm, b * N_HIDDEN + k + 1)
                    nc.vector.tensor_tensor(HB[:, dst, :], HB[:, dst, :], bank(H_BANKS[(b * N_HIDDEN + k) % 4]), ALU.mult)\
                        .then_inc(h_times, 1)

            def outputs(b):
                dve.wait_ge(base_ready, b + 1)
                for t in range(TB * b, TB * b + TB):
                    dve.wait_ge(y_mm, t + 1)
                    xt = X[:, t, KEEP:D]
                    for e in range(E0):
                        ins = nc.vector.scalar_tensor_tensor(out=xt, in0=bank(OUT_BANKS[t % 2], P, OC, OC * e),
                                                             scalar=G[:, b, 5, t % TB, e:e + 1], in1=xt,
                                                             op0=ALU.mult, op1=ALU.add)
                        if e < E0 - 1:
                            link(ins)
                        else:
                            ins.then_inc(y_used, 1)

            def gate_rows(b):
                dve.wait_ge(gT_mm, b + 1)
                if b:
                    dve.wait_ge(spread_mm, 4 * b)
                    dve.wait_ge(y1_mm, b)
                nc.vector.tensor_copy(gT[:, :], bank16(GT_BANK)[0:3 * E1, 0:S]).then_inc(gT_ready, 1)
                nc.vector.tensor_copy(tail[HE:HE + E1, :], bank(SIDE[1], E1)).then_inc(gT_ready, 1)

            def spread(b):
                for c in range(4):
                    dve.wait_ge(h1_act, 4 * b + c + 1)
                    dve.wait_ge(spread_mm, 4 * b + c + 1)
                    hc = HB[:, 4 * b + c, :]
                    nc.vector.tensor_tensor(hc, hc, bank(SIDE[0] if c % 2 else GT_BANK), ALU.mult).then_inc(h1_gated, 1)

            def outputs1(b):
                dve.wait_ge(y1_mm, b + 1)
                ts = tiles(b)
                nc.vector.tensor_tensor(X[:, ts, :], X[:, ts, :], bank(TAIL_BANK).rearrange("p (t d) -> p t d", t=TB), ALU.add)\
                    .then_inc(x_final, 1)

            nc.vector.memset(eps_ln[:, :], LN_EPS)
            nc.vector.memset(eps_rms[:, :], RMS_EPS).then_inc(eps_set, 1)
            nc.vector.memset(ones_b[:, :], 1.0).then_inc(ones_ready, 1)
            nc.vector.memset(PS[:, PV_BANK:PV_BANK + 1, :], 0.0).then_inc(pv_cleared, 1)
            first, second = prep_cross0(0), prep_cross0(1)
            next(first)
            dve.wait_ge(in_vec, 16)
            nc.vector.tensor_scalar(V("x0_bq"), V("x0_bq"), HD ** -0.5, None, ALU.mult)
            nc.vector.tensor_scalar(V("qn"), V("qn"), HD ** -0.5, None, ALU.mult).then_inc(vec_scaled, 1)
            for _ in range(2):
                next(first)
            split(SP_K0, P, B * SC)
            dve.wait_ge(in_const, 16)
            nc.vector.tensor_copy(ident_b[:, :], ident).then_inc(consts_cast, 1)
            dve.wait_ge(in_mask, 32)
            nc.vector.tensor_scalar(sub_z, sub_i, 0.0, NEG, ALU.is_equal, ALU.mult)
            link(nc.vector.tensor_scalar(pad_z, pad_i.rearrange("p (b k) -> p b k", b=B), 0.0, NEG, ALU.is_equal, ALU.mult))
            for b in range(B):
                nc.vector.tensor_tensor(msk[:, b, :, :], sub_z, pad_z[:, b, :].unsqueeze(1).to_broadcast([P, TB, SC]), ALU.min)\
                    .then_inc(mask_ready, 1)
            next(second)
            run_all(first)
            for _ in range(2):
                next(second)
            dve.wait_ge(ctx_mm, 3)
            dve.wait_ge(in_bv, 16)
            dve.wait_ge(pool_fills, FILL_V)
            bias = bv_b[0:KT, :].rearrange("p (h d) -> p h d", d=HD)
            for b in range(B):
                for j in range(2):
                    nc.vector.tensor_copy(V1[:, b, j, :, 0:HD],
                                          bank(4, KT, KV * HD, KV * HD * (2 * b + j)).rearrange("p (h d) -> p h d", d=HD))
                    last = nc.vector.tensor_tensor(V0[:, b, j, :, 0:HD],
                                                   bank(3, KT, D, D * (2 * b + j)).rearrange("p (h d) -> p h d", d=HD), bias, ALU.add)
            link(last)
            for b in range(B):
                nc.vector.memset(V0[0:OVER, b, 1, :, :], 0.0)
                last = nc.vector.memset(V1[0:OVER, b, 1, :, :], 0.0)
            last.then_inc(ctx_v, 1)
            split(SP_K1, KV * HD, B * SC)
            run_all(second)
            nc.vector.tensor_copy(causal_b[:, :], C("causal"))
            nc.vector.tensor_copy(causal_tb[:, :], C("causal_t"))
            nc.vector.tensor_copy(spread_b[:, :], C("spread")[0:3 * E1, :]).then_inc(consts_cast, 1)
            run_slots(FIRST_SLOTS, attention_slot, [(START_SELF[0], prep_self(0)), (START_SELF[1], prep_self(1)),
                                              (START_FFN0, ffn0_in(0))])
            run_ffn0(hidden, outputs, ffn0_in(1), prep_cross1(0))
            run_slots(LAST_SLOTS, attention_slot, [(START_CROSS1, prep_cross1(1)), (START_FFN1, ffn1_in(0))])
            run_ffn1(None, gate_rows, spread, outputs1, ffn1_in(1))


def shape_constants():
    c = np.zeros((P, N_CONST), np.float32)

    def put(name, a):
        at, n = CONST[name]
        c[:a.shape[0], at:at + n] = a

    i = np.arange(P)
    put("ident", np.eye(P))
    put("head_mean", (i[:, None] % H == i[None, :] % H) / HD)
    put("causal", np.where(i[None, :] > i[:, None], NEG, 0.0))
    put("causal_t", np.where(i[:, None] > i[None, :], NEG, 0.0))
    for name, E in (("before0", E0), ("before1", E1)):
        e = np.arange(E)
        put(name, np.tile((e[None, :] < e[:, None]).reshape(1, -1), (P, 1)))
    r, col = np.arange(3 * E1), np.arange(4 * P)
    put("spread", r[:, None] % E1 == col[None, :] // HE)
    return c


def kernel(**inputs):
    import concourse.bacc as bacc
    from concourse.bass_utils import run_bass_kernel_spmd

    a = {k: np.asarray(v) for k, v in inputs.items()}

    def chunks(w):
        return np.concatenate([w[P * i:P * i + P] for i in range(w.shape[0] // P)], axis=1)

    def by_feature(w, heads=H):
        return w.reshape(w.shape[0], heads, HD).transpose(0, 2, 1).reshape(w.shape[0], heads * HD)

    def vector_by_feature(v):
        return v.reshape(H, HD).T.reshape(-1)

    f0, f1 = "L0_ffn_", "L1_ffn_"
    packed = {
        "ctx": a["ctx_1024"].transpose(2, 0, 1).reshape(D, B * SC),
        "x0_k": by_feature(a["L0_xattn_Wk"].T), "x0_v": a["L0_xattn_Wv"].T, "x0_q": by_feature(a["L0_xattn_Wq"].T),
        "x1_k": by_feature(a["L1_xattn_W_k"], KV), "x1_v": a["L1_xattn_W_v"],
        "wq": by_feature(a[f0 + "wq"].T), "wk": by_feature(a[f0 + "wk"].T), "wv": a[f0 + "wv"].T, "wo": a[f0 + "wo"].T,
        "gate0": a[f0 + "gate_w"].T,
        "e1_w1": a[f0 + "e1_w1"].T, "e1_w2": a[f0 + "e1_w2"].T, "e0_up": a[f0 + "e0_up"].T,
        "e3_down": a[f0 + "e3_down"].T, "e2_l1": a[f0 + "e2_l1"].T, "e3_up": a[f0 + "e3_up"].T,
        "e2_l2": chunks(a[f0 + "e2_l2"].T), "e2_l3": chunks(a[f0 + "e2_l3"].T),
        "e0_down": chunks(a[f0 + "e0_down"].T), "e1_down": chunks(a[f0 + "e1_down"].T),
        "e2_l4": chunks(a[f0 + "e2_l4"].T), "e3_out": chunks(a[f0 + "e3_out"].T),
        "x1_q": by_feature(a["L1_xattn_W_q"]), "x1_o": a["L1_xattn_W_o"],
        "gate1": a[f1 + "gate_W"],
        "w1": a[f1 + "W1"].transpose(1, 0, 2).reshape(D, E1 * HE),
        "w2": chunks(a[f1 + "W2"].reshape(E1 * HE, D)),
        "ws1": a[f1 + "Ws1"],
    }
    vectors = {
        "x0_bq": vector_by_feature(a["L0_xattn_bq"]), "x0_bk": vector_by_feature(a["L0_xattn_bk"]),
        "n1": a[f0 + "n1_w"], "n2": a[f0 + "n2_w"],
        "qn": np.repeat(a[f0 + "qn_w"], H), "kn": np.repeat(a[f0 + "kn_w"], H),
        **{f"b1_{c}": a[f1 + "b1"].reshape(-1)[P * c:P * c + P] for c in range(4)},
    }
    arrays = {
        "early": np.concatenate([packed[n] for n in EARLY], axis=1),
        "late": np.concatenate([packed[n] for n in LATE], axis=1),
        "consts": shape_constants(),
        "vecs": np.stack([vectors[n] for n in VECS], axis=1),
        "bs1": a[f1 + "bs1"].reshape(HE, 1), "ws2": a[f1 + "Ws2"], "b2": a[f1 + "b2"],
        "bs2": a[f1 + "bs2"].reshape(1, D), "bv": a["L0_xattn_bv"],
        "rscale": a[f1 + "route_scale"].reshape(1),
        "pad_mask": a["mask_Bx1x1xS2_ik0"].reshape(B * SC),
        "sub_mask": a["mask_1x1xSxS2_ik0"].reshape(S, SC),
        "x": a["x"],
    }
    nc = bacc.Bacc("TRN2", target_bir_lowering=False, num_devices=1)
    arrays = {f"in_{k}": np.ascontiguousarray(v) for k, v in arrays.items()}
    args = [nc.dram_tensor(k, v.shape, mybir.dt.from_np(v.dtype), kind="ExternalInput").ap() for k, v in arrays.items()]
    out = nc.dram_tensor("out_x", (B, S, D), F32, kind="ExternalOutput").ap()
    build(nc, *args, out)
    r = run_bass_kernel_spmd(nc, [arrays], core_ids=[0])
    return r.results[0]["out_x"]
```

```python
from contextlib import ExitStack

import numpy as np

import concourse.bass as bass
from concourse import mybir

F32 = mybir.dt.float32
BF16 = mybir.dt.bfloat16
I32 = mybir.dt.int32
ALU = mybir.AluOpType
ACT = mybir.ActivationFunctionType
AX = mybir.AxisListType

P = 128
B, S, D = 2, 512, 128
H, HD = 16, 8
KV = 4
SC = 154
KT = 96
CT = (0, SC - KT)
OVER = 2 * KT - SC
NT = B * S // P
TB = S // P
QUADS = H // 4
ITEMS = B * QUADS
STACK = 96
TOP = STACK + 3
NEG = -float(2 ** 100)
FLT_MAX = 3.4028234663852886e38
LN_EPS = 1e-5
RMS_EPS = 1.1920929e-07
KEEP = 32
OC = D - KEEP
E0, E1 = 4, 8
HE = 64

CROSS0, SELF, CROSS1 = range(3)
N_CROSS0, N_SELF, R_SELF, R_FFN0, N_CROSS1, N_FFN1 = range(6)
T_CROSS0, T_SELF, T_FFN0, T_CROSS1, T_FFN1 = range(5)
SP_K0, SP_Q0, SP_K1, SP_SELF, SP_Q1 = 0, (1, 2), 3, 4, 8
N_SPLITS = 10
LATE_PIECES = 4


def columns(names):
    at, cols = 0, {}
    for name, n in names:
        cols[name] = (at, n)
        at += n
    return cols, at


EARLY, N_EARLY = columns([("ctx", B * SC), ("x0_k", D), ("x0_v", D), ("x1_k", KV * HD), ("x1_v", KV * HD), ("x0_q", D)])
LATE, N_LATE = columns([
    ("wq", D), ("wk", D), ("wv", D), ("wo", D), ("gate0", E0),
    ("e1_w1", 2 * D), ("e1_w2", 2 * D), ("e0_up", 2 * D), ("e3_down", D), ("e2_l1", 2 * D), ("e3_up", 2 * D),
    ("e2_l2", 4 * D), ("e2_l3", 4 * D), ("e0_down", 2 * D), ("e1_down", 2 * D), ("e2_l4", 2 * D), ("e3_out", 2 * D),
    ("x1_q", D), ("x1_o", D), ("gate1", E1), ("w1", 4 * D), ("w2", 4 * D), ("ws1", HE)])
CONST, N_CONST = columns([("ident", P), ("head_mean", P), ("causal", P), ("causal_t", P),
                          ("before0", E0 * E0), ("before1", E1 * E1), ("spread", 4 * P)])
VECS = ["x0_bq", "x0_bk", "n1", "n2", "qn", "kn", "b1_0", "b1_1", "b1_2", "b1_3"]

E1_JOBS = [
    ("e1_w1", (0,), None, 0, ACT.Silu), ("e1_w1", (1,), None, 1, ACT.Silu),
    ("e1_w2", (0,), None, 0, "times"), ("e1_w2", (1,), None, 1, "times")]
GELU_JOBS = [
    ("e3_down", (0,), None, 2, ACT.Gelu),
    ("e2_l1", (0,), None, 3, ACT.Gelu), ("e2_l1", (1,), None, 4, ACT.Gelu),
    ("e3_up", (0,), (2,), 5, ACT.Gelu), ("e3_up", (1,), (2,), 6, ACT.Gelu),
    ("e2_l2", (0, 2), (3, 4), 7, ACT.Gelu), ("e2_l2", (1, 3), (3, 4), 8, ACT.Gelu)]
MORE_JOBS = [
    ("e0_up", (0,), None, 9, ACT.Gelu), ("e0_up", (1,), None, 10, ACT.Gelu),
    ("e2_l3", (0, 2), (7, 8), 11, ACT.Gelu), ("e2_l3", (1, 3), (7, 8), 12, ACT.Gelu)]
SWITCH = 2
HIDDEN = [E1_JOBS + GELU_JOBS + MORE_JOBS, GELU_JOBS[:SWITCH] + E1_JOBS + GELU_JOBS[SWITCH:] + MORE_JOBS]
OUTPUTS = [("e0_down", (9, 10)), ("e1_down", (0, 1)), ("e2_l4", (11, 12)), ("e3_out", (5, 6))]
N_HIDDEN = len(HIDDEN[0])
N_TIMES = sum(h[4] == "times" for h in HIDDEN[0])
H_BANKS = (0, 1, 3, 4)


def by_act(b, k):
    return b * (N_HIDDEN - N_TIMES) + sum(h[4] != "times" for h in HIDDEN[b][:k + 1])


def by_dve(b, k):
    return b * N_HIDDEN + k + 1 - by_act(b, k)


SELF_START, CROSS1_START = 7, 1000
START_QUERIES1, START_KEYS1, START_WEIGHTS = (-6, 0), (-1, 0), (2, 0)
START_SELF = [(20, 21), (34, 35)]
START_FFN0 = (52 + SELF_START, 0)
START_HIDDEN = (4 * 2 * ITEMS + SELF_START, 0)
START_HIDDEN1 = (CROSS1_START + 4 * ITEMS, 0)
START_CROSS1, START_FFN1 = (CROSS1_START - 3, 0), (CROSS1_START + 19, 0)

LEAD = (7, 6, 7)
S_ORDER = (0, 3, 2, 1)

T_SLOT = {}
for _n in range(ITEMS):
    T_SLOT[_n] = 4 * _n
    T_SLOT[_n + ITEMS] = 4 * (_n + ITEMS) + SELF_START
    T_SLOT[_n + 2 * ITEMS] = CROSS1_START + 4 * _n


def lead(N):
    return LEAD[N // ITEMS]


def v_slots(N):
    after = range(4) if N // ITEMS == SELF else (0, 1) if N % ITEMS == ITEMS - 1 else (1, 2)
    return [T_SLOT[N] + 4 + i for i in after]


T_IN = {T_SLOT[n] + hh: (n, hh) for n in T_SLOT for hh in range(4)}
S_IN = {T_SLOT[n] - lead(n) + hh: (n, hh) for n in T_SLOT for hh in range(4)}
MAX_IN = {T_SLOT[n] - lead(n) + 4: n for n in T_SLOT}
V_IN = {slot: (n, j) for n in T_SLOT for j, slot in enumerate(v_slots(n))}
OUT_IN = {v_slots(n)[-1] + 1: n for n in T_SLOT}
FIRST_SLOTS = range(-LEAD[CROSS0], max(k for k in OUT_IN if k < CROSS1_START) + 1)
LAST_SLOTS = range(CROSS1_START - LEAD[CROSS1], max(OUT_IN) + 1)


def run_slots(slots, attention_slot, between):
    for slot in slots:
        attention_slot(slot)
        for (first, twice), work in between:
            if slot >= first:
                next(work, None)
                if slot < twice:
                    next(work, None)


def run_all(work):
    for _ in work:
        pass


def build(nc, early, late, consts, vecs, bs1, ws2, b2, bs2, bv, rscale, pad_mask, sub_mask, x, out):
    with ExitStack() as ctx:
        def sb(name, shape, dt=F32):
            return ctx.enter_context(nc.sbuf_tensor(name, shape, dt))

        def sem(name):
            return ctx.enter_context(nc.semaphore(name))

        def sems(name, n):
            return [sem(f"{name}_{i}") for i in range(n)]

        we = sb("we", [P, N_EARLY])
        wl = sb("wl", [P, N_LATE])
        cst = sb("cst", [P, N_CONST])
        vec = sb("vec", [P, len(VECS)])
        bs1_c = sb("bs1_c", [HE, 1])
        w_tail = sb("w_tail", [P, D])
        bv_b = sb("bv_b", [P, D])
        rs_b = sb("rs_b", [P, 1])
        eps_ln = sb("eps_ln", [P, 1])
        eps_rms = sb("eps_rms", [P, 1])
        msk = sb("msk", [P, B, TB, SC], BF16)
        msk_t = sb("msk_t", [KT, B, 2 * S], BF16)
        ident_b = sb("ident_b", [P, P], BF16)
        causal_b = sb("causal_b", [P, P], BF16)
        causal_tb = sb("causal_tb", [P, P], BF16)
        spread_b = sb("spread_b", [3 * E1, 4 * P], BF16)
        ones_b = sb("ones_b", [P, 512], BF16)
        X = sb("X", [P, NT, D])
        Y = sb("Y", [P, NT, D])
        U = sb("U", [P, NT, D])
        yT = sb("yT", [P, B * S])
        f32T = sb("f32T", [P, 2, S])
        sq = sb("sq", [P, 2, S])
        res = sb("res", [P, S])
        parts = sb("parts", [P, 4, 3, S], BF16)
        QA = sb("QA", [P, B * H * S], BF16)
        KS = sb("KS", [P, B * H * S], BF16)
        K1 = sb("K1", [P, KV, B * SC], BF16)
        VS = sb("VS", [P, NT, H, HD + 1])
        V0 = sb("V0", [KT, B, 2, H, HD + 1])
        V1 = sb("V1", [KT, B, 2, KV, HD + 1])
        PR = sb("PR", [P, 2 * 4 * 1280])
        O = sb("O", [P, 2, S])
        tail = sb("tail", [P, S])
        stats = sb("stats", [P, NT, 6])
        mv = sb("mv", [P, NT, 2])
        sm = sb("sm", [P, 6, NT])
        RSTD, VAR2, RMS, LOGV, GSUM, GINV = range(6)
        rden = sb("rden", [P, 2, TB, 4])
        nmax = sb("nmax", [P, 2, 16])
        nres = sb("nres", [P, 2, 16])
        nparts = sb("nparts", [P, 2, 48], BF16)
        nrows = sb("nrows", [48, 2, P], BF16)
        G = sb("G", [P, B, 6, TB, E1])
        gnum = sb("gnum", [P, TB, E1], I32)
        GG = sb("GG", [P, 2, TB, E1, E1])
        gparts = sb("gparts", [P, B, TB, 3, E1], BF16)
        gT = sb("gT", [3 * E1, S], BF16)
        PS = ctx.enter_context(nc.psum_tensor("PS", [P, 8, 512], F32))

        QAv = QA[:, :].rearrange("p (b h s) -> p b h s", b=B, h=H)
        KSv = KS[:, :].rearrange("p (b h s) -> p b h s", b=B, h=H)
        K0_AT, K0_N = H * S, H * B * SC
        K0 = KS[:, K0_AT:K0_AT + K0_N].rearrange("p (h s) -> p h s", h=H)
        K1f = K1[:, :, :].rearrange("p h s -> p (h s)")
        PRv = PR[:, :].rearrange("p (i h s) -> p i h s", i=2, h=4)
        HB = PR[:, 0:16 * S].rearrange("p (c s) -> p c s", s=S)
        sub_z = PR[:, 0:TB * SC].rearrange("p (t k) -> p t k", t=TB)
        sub_i = PR[:, 2 * S:2 * S + TB * SC].bitcast(I32).rearrange("p (t k) -> p t k", t=TB)
        pad_i = PR[:, 4 * S:4 * S + B * SC].bitcast(I32)
        pad_z = PR[:, 5 * S:5 * S + B * SC].rearrange("p (b k) -> p b k", b=B)

        def bank(b, rows=P, n=512, at=0):
            return PS[0:rows, b, at:at + n]

        def bank16(b):
            return PS[:, b, :].bitcast(BF16)

        def W(name, chunk=0, n=D):
            src, (at, size) = (we, EARLY[name]) if name in EARLY else (wl, LATE[name])
            n = min(n, size)
            return src[:, at + chunk * n:at + chunk * n + n]

        def C(name):
            at, n = CONST[name]
            return cst[:, at:at + n]

        def V(name):
            i = VECS.index(name)
            return vec[:, i:i + 1]

        def tokens(b):
            return slice(S * b, S * b + S)

        def tiles(b):
            return slice(TB * b, TB * b + TB)

        ident = C("ident")
        ctxT = we[:, 0:B * SC]
        T_BANKS, S_BANKS, PV_BANK = (0, 1), (3, 4, 7), 5
        SIDE = (2, 6)
        OUT_BANKS = (PV_BANK, SIDE[0])
        CTX_BANK = S_BANKS[2]

        in_x, in_early, in_const, in_vec, in_bv = sems("in_x", B), sem("in_early"), sem("in_const"), sem("in_vec"), sem("in_bv")
        in_mask, in_late, in_tail = sem("in_mask"), sem("in_late"), sem("in_tail")
        eps_set, consts_cast, pv_cleared = sem("eps_set"), sem("consts_cast"), sem("pv_cleared")
        vec_scaled = sem("vec_scaled")
        pool_fills = sem("pool_fills")
        ones_ready = sem("ones_ready")
        stack_fill = sem("stack_fill")
        ctx_mm, ctx_v = sem("ctx_mm"), sem("ctx_v")
        mask_ready, maskt_mm, maskt_ready = sem("mask_ready"), sem("maskt_mm"), sem("maskt_ready")
        stacked = sems("stacked", N_SPLITS)
        stacked3 = sems("stacked3", N_SPLITS)
        var_ready = sems("var_ready", 6)
        rstd_ready = sems("rstd_ready", 6)
        y_normed = sem("y_normed")
        rows_ready = sems("rows_ready", 5)
        rowsT_mm = sems("rowsT_mm", 5)
        rowsT_ready = sems("rowsT_ready", 5)
        proj_mm = sem("proj_mm")
        f32_ready = sem("f32_ready")
        hi_ready = sem("hi_ready")
        split_ready = sem("split_ready")
        sq_ready, ms_mm, rms_ready = sem("sq_ready"), sem("ms_mm"), sem("rms_ready")
        v_mm, v_ready = sem("v_mm"), sem("v_ready")
        s_mm, s_max = sem("s_mm"), sem("s_max")
        nparts_ready, nrows_mm, nrows_ready = sem("nparts_ready"), sem("nrows_mm"), sem("nrows_ready")
        max_rows = sems("max_rows", 2)
        t_mm, probs = sem("t_mm"), sem("probs")
        pv_mm, o_ready = sem("pv_mm"), sem("o_ready")
        oT_mm, ao_ready = sem("oT_mm"), sem("ao_ready")
        aoT_mm, aoT_ready, wo_mm, wo_used = sem("aoT_mm"), sem("aoT_ready"), sem("wo_mm"), sem("wo_used")
        gate_mm, gate_in, gate_exp, gates = sem("gate_mm"), sem("gate_in"), sem("gate_exp"), sem("gates")
        base_ready = sem("base_ready")
        h_mm, h_act, h_times = sem("h_mm"), sem("h_act"), sem("h_times")
        y_mm, y_used = sem("y_mm"), sem("y_used")
        h1_mm, h1_act, h1_gated = sem("h1_mm"), sem("h1_act"), sem("h1_gated")
        gT_mm, gT_ready, spread_mm, tail_gates = sem("gT_mm"), sem("gT_ready"), sem("spread_mm"), sem("tail_gates")
        tail_mm, tail_ready = sem("tail_mm"), sem("tail_ready")
        y1_mm, x_final = sem("y1_mm"), sem("x_final")
        dve_step, act_step = sem("dve_step"), sem("act_step")
        written = sem("written")

        block = ctx.enter_context(nc.Block())

        def s_jobs(layer):
            if layer == SELF:
                return [((t,), P * (t + 1)) for t in S_ORDER]
            return [((0, 1), SC), ((2, 3), SC)]

        def t_jobs(layer):
            if layer == SELF:
                return [(j, P, P * j, sum(S - P * i for i in range(j))) for j in range(TB)]
            return [(j, KT, 0, S * j) for j in range(2)]

        S_PER = [4 * len(s_jobs(l)) for l in range(3)]
        T_PER = [4 * len(t_jobs(l)) for l in range(3)]
        S_BEFORE = [ITEMS * sum(S_PER[:l]) for l in range(4)]
        T_BEFORE = [ITEMS * sum(T_PER[:l]) for l in range(4)]

        def place(N):
            layer, n = divmod(N, ITEMS)
            return (layer,) + divmod(n, QUADS)

        def s_index(N, hh=0, k=0):
            layer, n = divmod(N, ITEMS)
            return S_BEFORE[layer] + n * S_PER[layer] + hh * S_PER[layer] // 4 + k

        def t_index(N, hh=0, k=0):
            layer, n = divmod(N, ITEMS)
            return T_BEFORE[layer] + n * T_PER[layer] + hh * T_PER[layer] // 4 + k

        def q_split(layer, b):
            return (SP_Q0[b], SP_SELF + 2 * b, SP_Q1 + b)[layer]

        def wait_stacked(e, k):
            e.wait_ge(stacked[k], 16 * 6)
            e.wait_ge(stacked3[k], 16 * 3)

        def stack_dmas(e, k, which):
            if k == SP_K0:
                dst, src, q_side = lambda at: K0[at:at + HD, :, :], lambda i: parts[:, k % 4, i, 0:B * SC], False
            elif k == SP_K1:
                dst, src, q_side = lambda at: K1[at:at + HD, :, :], lambda i: parts[0:KV * HD, k % 4, i, 0:B * SC], False
            else:
                q_side = k < SP_SELF or k >= SP_Q1 or k % 2 == 0
                b = SP_Q0.index(k) if k < SP_SELF else k - SP_Q1 if k >= SP_Q1 else (k - SP_SELF) // 2
                stack = QAv if q_side else KSv
                dst, src = lambda at: stack[at:at + HD, b, :, :], lambda i: parts[:, k % 4, i, :]
            for part in which:
                e.wait_ge(hi_ready if part == 0 else split_ready, k + 1)
                for other in range(3):
                    at = part * 24 + other * HD if q_side else other * 24 + part * HD
                    e.dma_start(dst(at), src(part)).then_inc((stacked if part < 2 else stacked3)[k], 16)

        def run_ffn0(hidden, outputs, attention_slot, gate_work, query_work, ahead=0):
            next(gate_work)
            next(gate_work)
            for k in range(2):
                if k >= ahead:
                    hidden(0, k)
            next(gate_work)
            for k in range(2, N_HIDDEN):
                if k >= ahead:
                    hidden(0, k)
                if k in GATE_STAGES:
                    next(gate_work)
            if outputs:
                for t in range(TB):
                    outputs(0, t)
            for k in range(N_HIDDEN):
                if k == SWITCH:
                    next(query_work)
                    next(gate_work)
                    next(query_work)
                    run_all(gate_work)
                hidden(1, k)
                if k in QUERY_STAGES:
                    next(query_work)
            run_all(query_work)
            for t in range(TB):
                if outputs:
                    outputs(1, t)
                attention_slot(LAST_SLOTS[t])

        GATE_STAGES, QUERY_STAGES = (5, 8), (4, 7, 9, 10)

        def run_ffn1(gate_work, shared=None, hidden=None, gate_rows=None, spread=None, outputs=None, finish=None):
            def do(part, *args):
                if part:
                    part(*args)

            next(gate_work)
            do(shared, 0)
            do(gate_rows, 0)
            next(gate_work)
            do(spread, 0, (0, 1))
            next(gate_work)
            next(gate_work)
            do(spread, 0, (2, 3))
            next(gate_work)
            do(outputs, 0, (0, 1))
            next(gate_work)
            do(outputs, 0, (2, 3))
            next(gate_work)
            do(gate_rows, 1)
            do(finish, 0)
            do(hidden, 1, 0)
            for c in range(1, 4):
                do(hidden, 1, c)
                do(spread, 1, (c - 1,))
            do(shared, 1)
            do(spread, 1, (3,))
            do(outputs, 1, range(4))
            do(finish, 1)

        TAIL_BANK, GT_BANK = 5, 7

        FILL_K0, FILL_QA0, FILL_QA1, FILL_V, FILL_K1, FILL_KS0, FILL_KS1, FILL_W_TAIL, FILL_TAIL, FILL_VS, FILL_ALL = range(1, 12)

        @block.sync
        def _(sp):
            x_v = x.rearrange("b (t p) d -> b p t d", p=P)
            sp.dma_start(X[:, tiles(0), :], x_v[0]).then_inc(in_x[0], 16)
            sp.dma_start(we[:, :], early).then_inc(in_early, 16)
            sp.dma_start(vec[:, :], vecs).then_inc(in_vec, 16)
            sp.dma_start(cst[:, :], consts).then_inc(in_const, 16)
            sp.dma_start(sub_i, sub_mask.rearrange("(t p) k -> p t k", p=P)).then_inc(in_mask, 16)
            sp.dma_start(pad_i, pad_mask.partition_broadcast(P)).then_inc(in_mask, 16)
            sp.dma_start(X[:, tiles(1), :], x_v[1]).then_inc(in_x[1], 16)
            sp.dma_start(bv_b[:, :], bv.partition_broadcast(P)).then_inc(in_bv, 16)

            sp.wait_ge(pool_fills, FILL_K0)
            stack_dmas(sp, SP_K0, (0, 1))
            sp.wait_ge(pool_fills, FILL_QA0)
            stack_dmas(sp, SP_Q0[0], (0, 1))
            sp.wait_ge(ones_ready, 1)
            rest = (B * H * S - K0_AT - K0_N) // 8
            for stack, n, w in ((KS[STACK:TOP, K0_AT:K0_AT + K0_N], H, B * SC), (KS[STACK:TOP, 0:K0_AT], H, S),
                                (KS[STACK:TOP, K0_AT + K0_N:], 8, rest), (K1f[STACK:TOP, :], KV, B * SC)):
                sp.dma_start(stack.rearrange("p (a w) -> p a w", w=w),
                             ones_b[STACK:TOP, 0:w].unsqueeze(1).to_broadcast([3, n, w])).then_inc(stack_fill, 16)
            sp.wait_ge(pool_fills, FILL_QA1)
            stack_dmas(sp, SP_Q0[1], (0, 1))

            def keys1():
                yield
                sp.wait_ge(pool_fills, FILL_K1)
                for part in range(2):
                    stack_dmas(sp, SP_K1, (part,))
                    yield

            def load_weights():
                for piece in range(LATE_PIECES):
                    lo, hi = (N_LATE * (piece + i) // LATE_PIECES for i in range(2))
                    sp.dma_start(wl[:, lo:hi], late[:, lo:hi]).then_inc(in_late, 16)
                    for _ in range(4):
                        yield
                sp.wait_ge(pool_fills, FILL_W_TAIL)
                sp.dma_start(w_tail[0:HE, :], ws2).then_inc(in_tail, 16)
                sp.dma_start(w_tail[HE:HE + E1, :], b2).then_inc(in_tail, 16)
                sp.dma_start(w_tail[96:97, :], bs2).then_inc(in_tail, 16)
                sp.dma_start(bs1_c[:, :], bs1).then_inc(in_tail, 16)
                sp.dma_start(rs_b[:, :], rscale.partition_broadcast(P)).then_inc(in_tail, 16)
                yield

            def prep_self(b):
                for _ in range(8):
                    yield
                sp.wait_ge(pool_fills, FILL_KS1)
                stack_dmas(sp, SP_SELF + 2 * b, (0,))
                yield
                stack_dmas(sp, SP_SELF + 2 * b, (1,))
                stack_dmas(sp, SP_SELF + 2 * b + 1, (0,))
                yield
                stack_dmas(sp, SP_SELF + 2 * b + 1, (1,))
                yield

            def prep_cross1(b):
                for _ in range(5):
                    yield
                stack_dmas(sp, SP_Q1 + b, (0, 1))
                yield

            def attention_slot(slot):
                if slot not in MAX_IN:
                    return
                N = MAX_IN[slot]
                _, b, g = place(N)
                sp.wait_ge(nrows_ready, N + 1)
                sp.dma_start(QAv[STACK:TOP, b, 4 * g:4 * g + 4, :].rearrange("p h (t c) -> p (h t) c", c=P),
                             nrows[:, N % 2, :]).then_inc(max_rows[N % 2], 16)

            run_slots(FIRST_SLOTS, attention_slot, [(START_KEYS1, keys1()), (START_WEIGHTS, load_weights()), (START_SELF[0], prep_self(0)),
                                              (START_SELF[1], prep_self(1))])
            run_all(prep_cross1(0))
            for slot in LAST_SLOTS[:TB]:
                attention_slot(slot)
            run_slots(LAST_SLOTS[TB:], attention_slot, [(START_CROSS1, prep_cross1(1))])
            out_v = out.rearrange("b (t p) d -> b p t d", p=P)
            for b in range(B):
                sp.wait_ge(x_final, b + 1)
                sp.dma_start(out_v[b], X[:, tiles(b), :]).then_inc(written, 16)
            sp.wait_ge(written, 16 * B)

        @block.gpsimd
        def _(pool):
            fills = [0]

            def fill(view, value, last=True):
                ins = nc.gpsimd.memset(view, value)
                if last:
                    fills[0] += 1
                    ins.then_inc(pool_fills, 1)

            def zero_rows(stack):
                fill(stack.bitcast(F32), 0.0)

            zero_rows(KS[64:STACK, K0_AT:K0_AT + K0_N])
            zero_rows(QA[64:STACK, 0:H * S])
            zero_rows(QA[64:STACK, H * S:])
            pool.wait_ge(pool_fills, fills[0])
            stack_dmas(pool, SP_K0, (2,))
            stack_dmas(pool, SP_Q0[0], (2,))
            pool.wait_ge(pool_fills, fills[0])
            fill(V0[:, :, :, :, HD], 1.0, last=False)
            fill(V1[:, :, :, :, HD], 1.0)
            pool.wait_ge(pool_fills, fills[0])
            zero_rows(K1f[64:STACK, :])
            pool.wait_ge(pool_fills, fills[0])
            stack_dmas(pool, SP_Q0[1], (2,))
            stack_dmas(pool, SP_K1, (2,))
            zero_rows(KS[64:STACK, 0:K0_AT])
            zero_rows(KS[64:STACK, K0_AT + K0_N:])
            pool.wait_ge(pool_fills, fills[0])
            fill(w_tail[:, :], 0.0)
            pool.wait_ge(pool_fills, fills[0])
            fill(tail[64:P, :], 0.0)
            pool.wait_ge(pool_fills, fills[0])
            fill(VS[:, :, :, HD], 1.0)
            pool.wait_ge(pool_fills, fills[0])
            fill(tail[96:97, :], 1.0)
            for k in range(SP_SELF, SP_SELF + 2 * B):
                stack_dmas(pool, k, (2,))
            for b in range(B):
                pool.wait_ge(wo_used, b + 1)
                nc.gpsimd.tensor_tensor(X[:, tiles(b), :], X[:, tiles(b), :], Y[:, tiles(b), :], ALU.add)\
                    .then_inc(base_ready, 1)
            for b in range(B):
                stack_dmas(pool, SP_Q1 + b, (2,))

        @block.scalar
        def _(act):
            steps = [0]

            def link(ins):
                steps[0] += 1
                ins.then_inc(act_step, 1)
                act.wait_ge(act_step, steps[0])

            def exp_table():
                nc.scalar.preload_act_table_set("natural_log_exp_and_others")

            def gelu_table():
                nc.scalar.preload_act_table_set("gelu_and_others")

            def inv_sqrt(stage, b, src, to, eps):
                ts = tiles(b)
                act.wait_ge(var_ready[stage], b + 1)
                link(nc.scalar.activation(sm[:, LOGV, ts], src[:, ts], ACT.Ln, bias=eps[:, 0:1]))
                nc.scalar.activation(sm[:, to, ts], sm[:, LOGV, ts], ACT.Exp, scale=-0.5).then_inc(rstd_ready[stage], 1)

            def rms_rows(stage, b):
                ts = tiles(b)
                act.wait_ge(var_ready[stage], b + 1)
                link(nc.scalar.activation(sm[:, LOGV, ts], sm[:, VAR2, ts], ACT.Ln, bias=eps_rms[:, 0:1]))
                link(nc.scalar.activation(sm[:, RMS, ts], sm[:, LOGV, ts], ACT.Exp, scale=-0.5))
                for t in range(TB * b, TB * b + TB):
                    last = nc.scalar.activation(U[:, t, :], Y[:, t, :], ACT.Identity, scale=sm[:, RMS, t:t + 1])
                last.then_inc(rows_ready[T_SELF if stage == R_SELF else T_FFN0], 1)

            def rows_t(stage, b, scale=None):
                act.wait_ge(rowsT_mm[stage], b + 1)
                if scale is None:
                    ins = nc.scalar.activation(yT[:, tokens(b)], bank(SIDE[0]), ACT.Copy)
                else:
                    ins = nc.scalar.activation(yT[:, tokens(b)], bank(SIDE[0]), ACT.Identity, scale=scale)
                ins.then_inc(rowsT_ready[stage], 1)

            def f32_slot(k):
                if k >= 2:
                    act.wait_ge(split_ready, k - 1)
                return k % 2

            def hi_part(k, rows=P, n=S):
                act.wait_ge(f32_ready, k + 1)
                if k >= 4:
                    wait_stacked(act, k - 4)
                nc.scalar.activation(parts[0:rows, k % 4, 0, 0:n], f32T[0:rows, k % 2, 0:n], ACT.Copy).then_inc(hi_ready, 1)

            def ao_t(k):
                act.wait_ge(aoT_mm, k + 1)
                nc.scalar.activation(yT[:, tokens(k % B)], bank(SIDE[0]), ACT.Copy).then_inc(aoT_ready, 1)

            def attention_slot(slot):
                if slot in OUT_IN:
                    E = OUT_IN[slot]
                    act.wait_ge(pv_mm, E + 1)
                    if E >= 2:
                        act.wait_ge(oT_mm, E - 1)
                    nc.scalar.activation(O[:, E % 2, :], bank(PV_BANK), ACT.Copy).then_inc(o_ready, 1)
                if slot in T_IN:
                    N, hh = T_IN[slot]
                    if N >= 2 and hh == 0:
                        act.wait_ge(pv_mm, N - 1)
                    if N == 2 * ITEMS and hh == 0:
                        act.wait_ge(y_mm, NT)
                    for k, (j, rows, q0, at) in enumerate(t_jobs(N // ITEMS)):
                        tj = t_index(N, hh, k)
                        act.wait_ge(t_mm, tj + 1)
                        nc.scalar.activation(PRv[0:rows, N % 2, hh, at:at + S - q0],
                                             bank(T_BANKS[tj % 2], rows, S - q0, q0), ACT.Exp).then_inc(probs, 1)
                if slot in MAX_IN:
                    M = MAX_IN[slot]
                    act.wait_ge(nrows_mm, M + 1)
                    if M >= 2:
                        act.wait_ge(max_rows[M % 2], 16 * (M // 2))
                    nc.scalar.activation(nrows[:, M % 2, :], bank16(SIDE[1])[0:48, 0:P], ACT.Copy).then_inc(nrows_ready, 1)

            def keys_of_context(k, done, src, rows, bias):
                act.wait_ge(ctx_mm, done)
                dst = f32T[0:rows, f32_slot(k), 0:B * SC]
                if bias is None:
                    nc.scalar.activation(dst, src, ACT.Copy).then_inc(f32_ready, 1)
                else:
                    nc.scalar.activation(dst, src, ACT.Identity, bias=bias).then_inc(f32_ready, 1)
                hi_part(k, rows, B * SC)

            def prep_cross0(b):
                yield
                inv_sqrt(N_CROSS0, b, mv[:, :, 1], RSTD, eps_ln)
                yield
                yield
                rows_t(T_CROSS0, b)
                yield
                act.wait_ge(proj_mm, b + 1)
                nc.scalar.activation(f32T[:, f32_slot(SP_Q0[b]), :], bank(SIDE[1]), ACT.Identity, bias=V("x0_bq"),
                                     scale=HD ** -0.5).then_inc(f32_ready, 1)
                hi_part(SP_Q0[b])
                yield
                yield

            def prep_self(b):
                def raw(r):
                    k = 2 * b + r
                    act.wait_ge(proj_mm, 3 + k)
                    nc.scalar.activation(f32T[:, f32_slot(SP_SELF + k), :], bank(SIDE[1 - r]), ACT.Copy)
                    nc.scalar.activation(sq[:, r, :], bank(SIDE[1 - r]), ACT.Square).then_inc(sq_ready, 1)

                def inv_rms(r):
                    act.wait_ge(ms_mm, 2 * b + r + 1)
                    link(nc.scalar.activation(sq[:, r, :], bank(SIDE[1 - r]), ACT.Ln, bias=eps_rms[:, 0:1]))
                    nc.scalar.activation(sq[:, r, :], sq[:, r, :], ACT.Exp, scale=-0.5).then_inc(rms_ready, 1)

                yield
                inv_sqrt(N_SELF, b, mv[:, :, 1], RSTD, eps_ln)
                yield
                yield
                act.wait_ge(y_normed, b + 1)
                rms_rows(R_SELF, b)
                yield
                rows_t(T_SELF, b, V("n1"))
                yield
                raw(0)
                yield
                raw(1)
                inv_rms(0)
                yield
                inv_rms(1)
                yield
                hi_part(SP_SELF + 2 * b)
                act.wait_ge(v_mm, b + 1)
                nc.scalar.activation(VS[:, tiles(b), :, 0:HD],
                                     bank(SIDE[1]).rearrange("p (t h d) -> p t h d", t=TB, h=H), ACT.Copy).then_inc(v_ready, 1)
                yield
                hi_part(SP_SELF + 2 * b + 1)
                yield
                yield

            def ffn0_in(b):
                ao_t(b)
                yield
                yield
                if b:
                    exp_table()
                rms_rows(R_FFN0, b)
                yield
                rows_t(T_FFN0, b, V("n2"))
                yield
                yield
                if b:
                    exp_table()
                act.wait_ge(gate_in, b + 1)
                nc.scalar.activation(G[:, b, 1, :, 0:E0], G[:, b, 0, :, 0:E0], ACT.Exp).then_inc(gate_exp, 1)
                yield
                yield

            def prep_cross1(b):
                yield
                inv_sqrt(N_CROSS1, b, mv[:, :, 1], RSTD, eps_ln)
                yield
                yield
                rows_t(T_CROSS1, b)
                yield
                act.wait_ge(proj_mm, 7 + b)
                k = SP_Q1 + b
                nc.scalar.activation(f32T[:, f32_slot(k), :], bank(SIDE[1]), ACT.Copy, scale=HD ** -0.5).then_inc(f32_ready, 1)
                hi_part(k)
                yield
                yield

            def ffn1_in(b):
                ao_t(B + b)
                yield
                yield
                if b:
                    exp_table()
                inv_sqrt(N_FFN1, b, mv[:, :, 1], RSTD, eps_ln)
                yield
                yield
                rows_t(T_FFN1, b)
                yield
                yield
                act.wait_ge(gate_in, B + b + 1)
                nc.scalar.activation(G[:, b, 1, :, :], G[:, b, 0, :, :], ACT.Exp, scale=-1.0).then_inc(gate_exp, 1)
                if b:
                    gelu_table()
                yield
                yield

            def hidden(b, k):
                _, _, _, dst, func = HIDDEN[b][k]
                if func == "times":
                    return
                if b == 0 and (k == 0 or dst >= 10):
                    act.wait_ge(pv_mm, 2 * ITEMS - (dst < 10))
                if k == 0 and b == 1:
                    act.wait_ge(y_mm, TB * b)
                act.wait_ge(h_mm, b * N_HIDDEN + k + 1)
                nc.scalar.activation(HB[:, dst, :], bank(H_BANKS[(b * N_HIDDEN + k) % 4]), func).then_inc(h_act, 1)

            def hidden1(b, c):
                if b == c == 0:
                    act.wait_ge(pv_mm, 3 * ITEMS - 1)
                act.wait_ge(h1_mm, 4 * b + c + 1)
                nc.scalar.activation(HB[:, 4 * b + c, :], bank(H_BANKS[c]), ACT.Gelu, bias=V(f"b1_{c}")).then_inc(h1_act, 1)

            def shared(b):
                if b == 0:
                    act.wait_ge(in_tail, 16 * 5)
                    act.wait_ge(pool_fills, FILL_ALL)
                act.wait_ge(tail_mm, b + 1)
                if b:
                    act.wait_ge(y1_mm, b)
                nc.scalar.activation(tail[0:HE, :], bank(TAIL_BANK, HE), ACT.Gelu, bias=bs1_c[:, 0:1]).then_inc(tail_ready, 1)

            def gate_rows(b):
                act.wait_ge(gT_mm, b + 1)
                if b:
                    act.wait_ge(y1_mm, b)
                nc.scalar.activation(tail[HE:HE + E1, :], bank(SIDE[1], E1), ACT.Copy).then_inc(tail_gates, 1)

            exp_table()
            act.wait_ge(in_vec, 16)
            act.wait_ge(eps_set, 1)
            first, second = prep_cross0(0), prep_cross0(1)
            for _ in range(2):
                next(first)
            keys_of_context(SP_K0, 1, bank(0, P, B * SC), P, V("x0_bk"))
            act.wait_ge(vec_scaled, 1)
            for _ in range(3):
                next(first)
            run_all(second)
            keys_of_context(SP_K1, 2, bank(CTX_BANK, KV * HD, B * SC), KV * HD, None)
            for b in range(B):
                act.wait_ge(maskt_mm, b + 1)
                nc.scalar.activation(msk_t[:, b, :], bank16(T_BANKS[b])[0:KT, 0:2 * S], ACT.Copy).then_inc(maskt_ready, 1)
            run_slots(FIRST_SLOTS, attention_slot, [(START_SELF[0], prep_self(0)), (START_SELF[1], prep_self(1)),
                                              (START_FFN0, ffn0_in(0))])
            run_ffn0(hidden, None, attention_slot, ffn0_in(1), prep_cross1(0))
            exp_table()
            run_slots(LAST_SLOTS[TB:], attention_slot, [(START_CROSS1, prep_cross1(1)), (START_FFN1, ffn1_in(0))])
            gelu_table()
            gate_work = ffn1_in(1)
            hidden1(0, 0)
            next(gate_work)
            for c in range(1, 4):
                hidden1(0, c)
            run_ffn1(gate_work, shared=shared, hidden=hidden1, gate_rows=gate_rows)

        @block.tensor
        def _(pe):
            mm, tr = nc.tensor.matmul, nc.tensor.transpose
            reader = {}

            def side(i, sem, value):
                if i in reader:
                    pe.wait_ge(*reader[i])
                reader[i] = (sem, value)
                return SIDE[i]

            def transposes(src, bk, b, done):
                for t in range(TB):
                    last = tr(bank(bk, P, P, P * t), src[:, TB * b + t, :], ident)
                last.then_inc(done, 1)

            def rows_t(stage, b, src):
                pe.wait_ge(rows_ready[stage], b + 1)
                transposes(src, side(0, rowsT_ready[stage], b + 1), b, rowsT_mm[stage])

            def by_tile(bk, b, w, n):
                for t in range(TB):
                    last = mm(bank(bk, P, n, n * t), yT[:, S * b + P * t:S * b + P * t + P], w, start=True, stop=True)
                return last

            def s_job(N, hh, k):
                layer, b, g = place(N)
                h = 4 * g + hh
                if g == hh == k == 0:
                    wait_stacked(pe, q_split(layer, b))
                    if layer == SELF:
                        wait_stacked(pe, SP_SELF + 2 * b + 1)
                        pe.wait_ge(pool_fills, FILL_ALL)
                        pe.wait_ge(consts_cast, 2)
                    if layer == CROSS1:
                        wait_stacked(pe, SP_K1)
                ts, w = s_jobs(layer)[k]
                sj = s_index(N, hh, k)
                bk = S_BANKS[sj % 3]
                if S_BANKS[sj % 3] == CTX_BANK and sj < 3:
                    pe.wait_ge(f32_ready, SP_K1 + 1)
                if sj >= 3:
                    pe.wait_ge(s_max, sj - 2)
                for i, t in enumerate(ts):
                    q = QAv[0:STACK, b, h, P * t:P * t + P]
                    if layer == SELF:
                        keys = KSv[0:STACK, b, h, 0:w]
                    elif layer == CROSS0:
                        keys = K0[0:STACK, h, SC * b:SC * b + SC]
                    else:
                        keys = K1[0:STACK, g, SC * b:SC * b + SC]
                    last = mm(bank(bk, P, w, w * i), q, keys, start=True, stop=layer == CROSS1)
                    if layer == CROSS0:
                        last = mm(bank(bk, P, w, w * i), ident_b[:, :], msk[:, b, t, :], start=False, stop=True)
                    if layer == SELF:
                        last = mm(bank(bk, P, P, P * t), ident_b[:, :], causal_b[:, :], start=False, stop=True)
                last.then_inc(s_mm, 1)

            def maxima(N):
                pe.wait_ge(nparts_ready, N + 1)
                tr(bank16(side(1, nrows_ready, N + 1))[0:48, 0:P], nparts[:, N % 2, :], ident_b[:, :]).then_inc(nrows_mm, 1)

            def t_job(N, hh, k):
                layer, b, g = place(N)
                h = 4 * g + hh
                if hh == k == 0:
                    pe.wait_ge(max_rows[N % 2], 16 * (N // 2 + 1))
                    if N == 0:
                        pe.wait_ge(stack_fill, 16 * 4)
                        pe.wait_ge(maskt_ready, B)
                j, rows, q0, _ = t_jobs(layer)[k]
                tj = t_index(N, hh, k)
                bk = T_BANKS[tj % 2]
                if tj >= 2:
                    pe.wait_ge(probs, tj - 1)
                if layer == SELF:
                    keys = KSv[0:TOP, b, h, P * j:P * j + P]
                elif layer == CROSS0:
                    keys = K0[0:TOP, h, SC * b + CT[j]:SC * b + CT[j] + KT]
                else:
                    keys = K1[0:TOP, g, SC * b + CT[j]:SC * b + CT[j] + KT]
                last = mm(bank(bk, rows, S - q0, q0), keys, QAv[0:TOP, b, h, q0:S], start=True, stop=layer == CROSS1)
                if layer == CROSS0:
                    last = mm(bank(bk, rows), ident_b[0:KT, 0:KT], msk_t[:, b, S * j:S * j + S], start=False, stop=True)
                if layer == SELF:
                    last = mm(bank(bk, rows, P, q0), ident_b[:, :], causal_tb[:, :], start=False, stop=True)
                last.then_inc(t_mm, 1)

            def pass_v(N, tile):
                layer, b, g = place(N)
                jobs = t_jobs(layer)
                j, rows, q0, at = jobs[tile]
                if tile == 0:
                    pe.wait_ge(probs, t_index(N) + T_PER[layer])
                    if N >= 1:
                        pe.wait_ge(o_ready, N)
                for head in range(4):
                    if layer == SELF:
                        v = VS[:, TB * b + j, 4 * g + head, :]
                    elif layer == CROSS0:
                        v = V0[:, b, j, 4 * g + head, :]
                    else:
                        v = V1[:, b, j, g, :]
                    last = mm(PS[32 * head:32 * head + HD + 1, PV_BANK, q0:S], v,
                              PRv[0:rows, N % 2, head, at:at + S - q0], start=j == 0, stop=j == len(jobs) - 1)
                if j == len(jobs) - 1:
                    last.then_inc(pv_mm, 1)

            def heads_to_rows(N):
                pe.wait_ge(o_ready, N + 1)
                bk = side(0, ao_ready, N + 1)
                for t in range(TB):
                    last = tr(bank(bk, P, P, P * t), O[:, N % 2, P * t:P * t + P], ident)
                last.then_inc(oT_mm, 1)

            def attention_slot(slot):
                n_s = len(s_jobs(S_IN[slot][0] // ITEMS)) if slot in S_IN else 0
                n_t = len(t_jobs(T_IN[slot][0] // ITEMS)) if slot in T_IN else 0
                for k in range(max(n_s, n_t, 2)):
                    if k < n_s:
                        s_job(*S_IN[slot], k)
                    if k < n_t:
                        t_job(*T_IN[slot], k)
                    if k == 1 and slot in V_IN:
                        pass_v(*V_IN[slot])
                if slot in MAX_IN:
                    maxima(MAX_IN[slot])
                if slot in OUT_IN:
                    heads_to_rows(OUT_IN[slot])

            def prep_cross0(b):
                yield
                yield
                yield
                rows_t(T_CROSS0, b, Y)
                yield
                pe.wait_ge(rowsT_ready[T_CROSS0], b + 1)
                bk = side(1, f32_ready, SP_Q0[b] + 1)
                mm(bank(bk), W("x0_q"), yT[:, tokens(b)], start=True, stop=True).then_inc(proj_mm, 1)
                yield
                yield

            def prep_self(b):
                for _ in range(4):
                    yield
                rows_t(T_SELF, b, U)
                yield
                pe.wait_ge(in_late, 16 * LATE_PIECES)
                pe.wait_ge(rowsT_ready[T_SELF], b + 1)
                for r, w in enumerate(("wq", "wk")):
                    bk = side(1 - r, sq_ready, 2 * b + r + 1)
                    mm(bank(bk), W(w), yT[:, tokens(b)], start=True, stop=True).then_inc(proj_mm, 1)
                yield
                for r in range(2):
                    k = 2 * b + r
                    bk = side(1 - r, rms_ready, k + 1)
                    pe.wait_ge(sq_ready, k + 1)
                    mm(bank(bk), C("head_mean"), sq[:, r, :], start=True, stop=True).then_inc(ms_mm, 1)
                    yield
                by_tile(side(1, v_ready, b + 1), b, W("wv"), D).then_inc(v_mm, 1)
                yield
                yield
                yield

            def ffn0_in(b):
                pe.wait_ge(ao_ready, ITEMS + QUADS * (b + 1))
                transposes(U, side(0, aoT_ready, b + 1), b, aoT_mm)
                yield
                pe.wait_ge(aoT_ready, b + 1)
                at = LATE["wo"][0]
                by_tile(side(1, wo_used, b + 1), b, wl[:, at + KEEP:at + D], OC).then_inc(wo_mm, 1)
                yield
                yield
                rows_t(T_FFN0, b, U)
                yield
                pe.wait_ge(rowsT_ready[T_FFN0], b + 1)
                by_tile(side(1, gate_in, b + 1), b, W("gate0"), E0).then_inc(gate_mm, 1)
                yield
                yield
                yield

            def prep_cross1(b):
                yield
                yield
                yield
                rows_t(T_CROSS1, b, Y)
                yield
                pe.wait_ge(rowsT_ready[T_CROSS1], b + 1)
                bk = side(1, f32_ready, SP_Q1 + b + 1)
                mm(bank(bk), W("x1_q"), yT[:, tokens(b)], start=True, stop=True).then_inc(proj_mm, 1)
                yield
                yield

            def ffn1_in(b):
                pe.wait_ge(ao_ready, 2 * ITEMS + QUADS * (b + 1))
                transposes(U, side(0, aoT_ready, B + b + 1), b, aoT_mm)
                yield
                pe.wait_ge(aoT_ready, B + b + 1)
                by_tile(side(1, wo_used, B + b + 1), b, W("x1_o"), D).then_inc(wo_mm, 1)
                yield
                yield
                yield
                rows_t(T_FFN1, b, Y)
                yield
                pe.wait_ge(rowsT_ready[T_FFN1], b + 1)
                by_tile(side(1, gate_in, B + b + 1), b, W("gate1"), E1).then_inc(gate_mm, 1)
                yield
                yield
                yield

            def hidden(b, k):
                w, chunks, srcs, _, _ = HIDDEN[b][k]
                job = b * N_HIDDEN + k
                if job == 0:
                    pe.wait_ge(probs, T_BEFORE[CROSS1])
                    pe.wait_ge(s_max, S_BEFORE[CROSS1])
                if job >= 4:
                    fb, fk = divmod(job - 4, N_HIDDEN)
                    if HIDDEN[fb][fk][4] == "times":
                        pe.wait_ge(h_times, by_dve(fb, fk))
                    else:
                        pe.wait_ge(h_act, by_act(fb, fk))
                bk = H_BANKS[job % 4]
                if srcs is None:
                    last = mm(bank(bk), W(w, chunks[0]), yT[:, tokens(b)], start=True, stop=True)
                else:
                    pe.wait_ge(h_act, by_act(b, max(i for i, h in enumerate(HIDDEN[b]) if h[3] in srcs)))
                    for i, s in enumerate(srcs):
                        last = mm(bank(bk), W(w, chunks[i]), HB[:, s, :], start=i == 0, stop=i == len(srcs) - 1)
                last.then_inc(h_mm, 1)

            def outputs(b, t):
                if t == 0:
                    pe.wait_ge(h_act, by_act(b, N_HIDDEN - 1))
                    pe.wait_ge(h_times, by_dve(b, N_HIDDEN - 1))
                    if b == 0:
                        pe.wait_ge(o_ready, 2 * ITEMS)
                k = TB * b + t
                if t % 2:
                    side(0, y_used, k + 1)
                elif k >= 2:
                    pe.wait_ge(y_used, k - 1)
                for e, (w, srcs) in enumerate(OUTPUTS):
                    at = LATE[w][0]
                    for i, c in enumerate(srcs):
                        last = mm(bank(OUT_BANKS[t % 2], P, OC, OC * e), HB[:, c, P * t:P * t + P],
                                  wl[:, at + D * i + KEEP:at + D * i + D], start=i == 0, stop=i == 1)
                last.then_inc(y_mm, 1)

            def hidden1(b, c):
                if b == c == 0:
                    pe.wait_ge(probs, T_BEFORE[3])
                    pe.wait_ge(s_max, S_BEFORE[3])
                if b:
                    pe.wait_ge(h1_gated, 4 * (b - 1) + c + 1)
                mm(bank(H_BANKS[c]), W("w1", c), yT[:, tokens(b)], start=True, stop=True).then_inc(h1_mm, 1)

            def first_hidden1():
                for c in range(4):
                    hidden1(0, c)
                    yield

            def shared(b):
                if b == 0:
                    pe.wait_ge(in_tail, 16 * 5)
                    pe.wait_ge(o_ready, 3 * ITEMS)
                else:
                    pe.wait_ge(x_final, b)
                mm(bank(TAIL_BANK, HE), W("ws1"), yT[:, tokens(b)], start=True, stop=True).then_inc(tail_mm, 1)

            def gate_rows(b):
                pe.wait_ge(gates, b + 1)
                if b == 0:
                    pe.wait_ge(s_max, S_BEFORE[3])
                else:
                    pe.wait_ge(gT_ready, b)
                for t in range(TB):
                    tr(bank16(GT_BANK)[0:3 * E1, P * t:P * t + P], gparts[:, b, t, :, :].rearrange("p a e -> p (a e)"), ident_b[:, :])
                bk = side(1, tail_gates, b + 1)
                for t in range(TB):
                    last = tr(bank(bk, E1, P, P * t), G[:, b, 5, t, :], ident)
                last.then_inc(gT_mm, 1)

            def spread(b, cs):
                pe.wait_ge(gT_ready, b + 1)
                for c in cs:
                    pe.wait_ge(h1_act, 4 * b + c + 1)
                    mm(bank(H_BANKS[c]), spread_b[:, P * c:P * c + P], gT[:, :], start=True, stop=True).then_inc(spread_mm, 1)

            def outputs1(b, ts):
                for t in ts:
                    cols = slice(P * t, P * t + P)
                    if t == 0:
                        pe.wait_ge(tail_ready, b + 1)
                    for c in range(4):
                        if t == 0:
                            pe.wait_ge(h1_gated, 4 * b + c + 1)
                        mm(bank(TAIL_BANK, P, D, D * t), HB[:, 4 * b + c, cols], W("w2", c), start=c == 0, stop=False)
                    if t == 0:
                        pe.wait_ge(tail_gates, b + 1)
                    last = mm(bank(TAIL_BANK, P, D, D * t), tail[0:97, cols], w_tail[0:97, :], start=False, stop=True)
                if ts[-1] == TB - 1:
                    last.then_inc(y1_mm, 1)

            pe.wait_ge(in_early, 16)
            mm(bank(0, P, B * SC), W("x0_k"), ctxT, start=True, stop=True).then_inc(ctx_mm, 1)
            mm(bank(CTX_BANK, KV * HD, B * SC), W("x1_k"), ctxT, start=True, stop=True).then_inc(ctx_mm, 1)
            pe.wait_ge(in_const, 16)
            first, second = prep_cross0(0), prep_cross0(1)
            for _ in range(5):
                next(first)
            pe.wait_ge(pv_cleared, 1)
            for b in range(B):
                for j in range(2):
                    keys = ctxT[:, SC * b + CT[j]:SC * b + CT[j] + KT]
                    mm(bank(PV_BANK, KT, D, D * (2 * b + j)), keys, W("x0_v"), start=True, stop=True)
                    last = mm(bank(T_BANKS[1], KT, KV * HD, KV * HD * (2 * b + j)), keys, W("x1_v"), start=True, stop=True)
            last.then_inc(ctx_mm, 1)
            run_all(second)
            pe.wait_ge(consts_cast, 1)
            pe.wait_ge(f32_ready, SP_K0 + 1)
            for b in range(B):
                pe.wait_ge(mask_ready, b + 1)
                if b == 1:
                    pe.wait_ge(ctx_v, 1)
                for j in range(2):
                    for t in range(TB):
                        last = tr(bank16(T_BANKS[b])[0:KT, S * j + P * t:S * j + P * t + P],
                                  msk[:, b, t, CT[j]:CT[j] + KT], ident_b[:, :])
                last.then_inc(maskt_mm, 1)
            wait_stacked(pe, SP_K0)

            def first_hidden():
                for k in range(len(H_BANKS)):
                    hidden(0, k)
                    yield

            run_slots(FIRST_SLOTS, attention_slot, [(START_SELF[0], prep_self(0)), (START_SELF[1], prep_self(1)),
                                                    (START_FFN0, ffn0_in(0)), (START_HIDDEN, first_hidden())])
            run_ffn0(hidden, outputs, attention_slot, ffn0_in(1), prep_cross1(0), ahead=len(H_BANKS))
            pe.wait_ge(y_used, NT)
            after = first_hidden1()
            run_slots(LAST_SLOTS[TB:], attention_slot, [(START_CROSS1, prep_cross1(1)), (START_FFN1, ffn1_in(0)),
                                                   (START_HIDDEN1, after)])
            gate_work = ffn1_in(1)
            next(gate_work)
            run_all(after)
            run_ffn1(gate_work, shared=shared, hidden=hidden1, gate_rows=gate_rows, spread=spread, outputs=outputs1)

        @block.vector
        def _(dve):
            steps = [0]

            def link(ins):
                steps[0] += 1
                ins.then_inc(dve_step, 1)
                dve.wait_ge(dve_step, steps[0])

            def statistics(src, b):
                for t in range(TB * b, TB * b + TB):
                    last = nc.vector.bn_stats(stats[:, t, :], src[:, t, :])
                link(last)
                for t in range(TB * b, TB * b + TB):
                    last = nc.vector.bn_aggr(mv[:, t, :], stats[:, t, :])
                return last

            def normalise(stage, b):
                dve.wait_ge(rstd_ready[stage], b + 1)
                for t in range(TB * b, TB * b + TB):
                    last = nc.vector.tensor_scalar(Y[:, t, :], X[:, t, :], mv[:, t, 0:1], sm[:, RSTD, t:t + 1],
                                                   ALU.subtract, ALU.mult)
                return last

            def split(k, rows=P, n=S):
                p = [parts[0:rows, k % 4, i, 0:n] for i in range(3)]
                r = res[0:rows, 0:n]
                dve.wait_ge(hi_ready, k + 1)
                dve.wait_ge(split_ready, k)
                link(nc.vector.tensor_tensor(r, f32T[0:rows, k % 2, 0:n], p[0], ALU.subtract))
                link(nc.vector.tensor_copy(p[1], r))
                nc.vector.tensor_tensor(p[2], r, p[1], ALU.subtract).then_inc(split_ready, 1)

            def reduce(N, hh):
                for k, (ts, w) in enumerate(s_jobs(N // ITEMS)):
                    sj = s_index(N, hh, k)
                    dve.wait_ge(s_mm, sj + 1)
                    at = 4 * hh + ts[0]
                    nc.vector.tensor_reduce(nmax[:, N % 2, at:at + len(ts)],
                                            PS[:, S_BANKS[sj % 3], 0:w * len(ts)].rearrange("p (t k) -> p t k", k=w),
                                            AX.X, ALU.max, negate=True).then_inc(s_max, 1)

            def split_max(N):
                src, r = nmax[:, N % 2, :], nres[:, N % 2, :]
                p = [nparts[:, N % 2, 16 * i:16 * i + 16] for i in range(3)]
                dve.wait_ge(s_max, s_index(N) + S_PER[N // ITEMS])
                if N >= 2:
                    dve.wait_ge(nrows_mm, N - 1)
                link(nc.vector.tensor_copy(p[0], src))
                link(nc.vector.tensor_tensor(r, src, p[0], ALU.subtract))
                link(nc.vector.tensor_copy(p[1], r))
                nc.vector.tensor_tensor(p[2], r, p[1], ALU.subtract).then_inc(nparts_ready, 1)

            def rows_of_heads(N):
                _, b, g = place(N)
                dve.wait_ge(oT_mm, N + 1)
                v = PS[:, SIDE[0], :].rearrange("p (t h c) -> p t h c", t=TB, c=32)
                r = rden[:, N % 2, :, :]
                link(nc.vector.reciprocal(r, v[:, :, :, HD]))
                nc.vector.tensor_tensor(U[:, tiles(b), 4 * HD * g:4 * HD * g + 4 * HD].rearrange("p t (h d) -> p t h d", d=HD),
                                        v[:, :, :, 0:HD], r.unsqueeze(3).to_broadcast([P, TB, 4, HD]), ALU.mult)\
                    .then_inc(ao_ready, 1)

            def attention_slot(slot):
                if slot in S_IN:
                    N, hh = S_IN[slot]
                    reduce(N, hh)
                    if hh == 3:
                        split_max(N)
                if slot in OUT_IN:
                    rows_of_heads(OUT_IN[slot])

            def top2(b, prob, E, before, guard):
                g, q = GG[:, 0, :, 0:E, 0:E], GG[:, 1, :, 0:E, 0:E]
                pj = prob.unsqueeze(2).to_broadcast([P, TB, E, E])
                pi = prob.unsqueeze(3).to_broadcast([P, TB, E, E])
                lt = before.rearrange("p (i j) -> p i j", j=E).unsqueeze(1).to_broadcast([P, TB, E, E])
                nc.vector.tensor_tensor(g, pj, pi, ALU.is_gt)
                link(nc.vector.tensor_tensor(q, pj, pi, ALU.is_equal))
                link(nc.vector.tensor_tensor(q, q, lt, ALU.mult))
                link(nc.vector.tensor_tensor(g, g, q, ALU.add))
                link(nc.vector.tensor_reduce(G[:, b, 2, :, 0:E], g, AX.X, ALU.add))
                link(nc.vector.scalar_tensor_tensor(out=G[:, b, 3, :, 0:E], in0=G[:, b, 2, :, 0:E], scalar=2.0, in1=prob,
                                                    op0=ALU.is_lt, op1=ALU.mult))
                link(nc.vector.tensor_reduce(sm[:, GSUM, 0:TB], G[:, b, 3, :, 0:E], AX.X, ALU.add))
                if guard:
                    link(nc.vector.tensor_scalar(sm[:, GSUM, 0:TB], sm[:, GSUM, 0:TB], guard, None, ALU.add))
                link(nc.vector.reciprocal(sm[:, GINV, 0:TB], sm[:, GSUM, 0:TB]))
                link(nc.vector.tensor_tensor(G[:, b, 5, :, 0:E], G[:, b, 3, :, 0:E],
                                             sm[:, GINV, 0:TB].unsqueeze(2).to_broadcast([P, TB, E]), ALU.mult))

            def prep_cross0(b):
                dve.wait_ge(in_x[b], 16)
                statistics(X, b).then_inc(var_ready[N_CROSS0], 1)
                yield
                yield
                normalise(N_CROSS0, b).then_inc(rows_ready[T_CROSS0], 1)
                yield
                yield
                yield
                split(SP_Q0[b])
                yield

            def prep_self(b):
                ts = tiles(b)
                dve.wait_ge(ao_ready, QUADS * (b + 1))
                link(nc.vector.tensor_tensor(X[:, ts, :], X[:, ts, :], U[:, ts, :], ALU.add))
                statistics(X, b).then_inc(var_ready[N_SELF], 1)
                yield
                yield
                dve.wait_ge(rstd_ready[N_SELF], b + 1)
                link(nc.vector.tensor_tensor(sm[:, VAR2, ts], mv[:, ts, 1], sm[:, RSTD, ts], ALU.mult))
                nc.vector.tensor_tensor(sm[:, VAR2, ts], sm[:, VAR2, ts], sm[:, RSTD, ts], ALU.mult)\
                    .then_inc(var_ready[R_SELF], 1)
                normalise(N_SELF, b).then_inc(y_normed, 1)
                yield
                yield
                yield
                yield
                yield

                def norm(r, w):
                    k = 2 * b + r
                    dve.wait_ge(rms_ready, k + 1)
                    f = f32T[:, (SP_SELF + k) % 2, :]
                    nc.vector.scalar_tensor_tensor(out=f, in0=f, scalar=V(w), in1=sq[:, r, :],
                                                   op0=ALU.mult, op1=ALU.mult).then_inc(f32_ready, 1)

                norm(0, "qn")
                yield
                norm(1, "kn")
                yield
                split(SP_SELF + 2 * b)
                yield
                split(SP_SELF + 2 * b + 1)
                yield

            def ffn0_in(b):
                ts = tiles(b)
                yield
                dve.wait_ge(wo_mm, b + 1)
                nc.vector.tensor_tensor(Y[:, ts, KEEP:D], Y[:, ts, KEEP:D],
                                        bank(SIDE[1], P, TB * OC).rearrange("p (t d) -> p t d", t=TB), ALU.add)\
                    .then_inc(wo_used, 1)
                dve.wait_ge(wo_used, b + 1)
                link(statistics(Y, b))
                link(nc.vector.tensor_tensor(sm[:, VAR2, ts], mv[:, ts, 0], mv[:, ts, 0], ALU.mult))
                nc.vector.tensor_tensor(sm[:, VAR2, ts], sm[:, VAR2, ts], mv[:, ts, 1], ALU.add).then_inc(var_ready[R_FFN0], 1)
                yield
                yield
                yield
                dve.wait_ge(gate_mm, b + 1)
                logits = bank(SIDE[1], P, TB * E0).rearrange("p (t e) -> p t e", e=E0)
                z, raw, num = G[:, b, 0, :, 0:E0], G[:, b, 4, :, 0:E0], gnum[:, :, 0:E0]
                nc.vector.memset(z, 0.0)
                link(nc.vector.tensor_copy(raw, logits))
                link(nc.vector.tensor_tensor(num, raw, raw, ALU.is_equal))
                link(nc.vector.copy_predicated(z, num, raw))
                link(nc.vector.tensor_scalar(z, z, -FLT_MAX, FLT_MAX, ALU.max, ALU.min))
                link(nc.vector.tensor_reduce(sm[:, GSUM, 0:TB], z, AX.X, ALU.max))
                nc.vector.tensor_tensor(z, z, sm[:, GSUM, 0:TB].unsqueeze(2).to_broadcast([P, TB, E0]), ALU.subtract)\
                    .then_inc(gate_in, 1)
                yield
                yield
                dve.wait_ge(gate_exp, b + 1)
                e = G[:, b, 1, :, 0:E0]
                link(nc.vector.tensor_reduce(sm[:, GSUM, 0:TB], e, AX.X, ALU.add))
                link(nc.vector.reciprocal(sm[:, GINV, 0:TB], sm[:, GSUM, 0:TB]))
                link(nc.vector.tensor_tensor(raw, e, sm[:, GINV, 0:TB].unsqueeze(2).to_broadcast([P, TB, E0]), ALU.mult))
                top2(b, raw, E0, C("before0"), 1e-8)
                yield

            def prep_cross1(b):
                dve.wait_ge(y_used, TB * (b + 1))
                statistics(X, b).then_inc(var_ready[N_CROSS1], 1)
                yield
                yield
                normalise(N_CROSS1, b).then_inc(rows_ready[T_CROSS1], 1)
                yield
                yield
                yield
                split(SP_Q1 + b)
                yield

            def ffn1_in(b):
                ts = tiles(b)
                yield
                dve.wait_ge(wo_mm, B + b + 1)
                nc.vector.tensor_tensor(X[:, ts, :], X[:, ts, :], bank(SIDE[1]).rearrange("p (t d) -> p t d", t=TB), ALU.add)\
                    .then_inc(wo_used, 1)
                dve.wait_ge(wo_used, B + b + 1)
                statistics(X, b).then_inc(var_ready[N_FFN1], 1)
                yield
                yield
                normalise(N_FFN1, b).then_inc(rows_ready[T_FFN1], 1)
                yield
                yield
                dve.wait_ge(gate_mm, B + b + 1)
                nc.vector.tensor_copy(G[:, b, 0, :, :], bank(SIDE[1], P, TB * E1).rearrange("p (t e) -> p t e", e=E1))\
                    .then_inc(gate_in, 1)
                yield
                yield
                dve.wait_ge(in_tail, 16 * 5)
                dve.wait_ge(gate_exp, B + b + 1)
                g4, g5, gp = G[:, b, 4, :, :], G[:, b, 5, :, :], gparts[:, b]
                link(nc.vector.tensor_scalar(G[:, b, 1, :, :], G[:, b, 1, :, :], 1.0, None, ALU.add))
                link(nc.vector.reciprocal(g4, G[:, b, 1, :, :]))
                link(nc.vector.tensor_scalar(g4, g4, rs_b[:, 0:1], None, ALU.mult))
                top2(b, g4, E1, C("before1"), None)
                link(nc.vector.tensor_copy(gp[:, :, 0, :], g5))
                link(nc.vector.tensor_tensor(g4, g5, gp[:, :, 0, :], ALU.subtract))
                link(nc.vector.tensor_copy(gp[:, :, 1, :], g4))
                nc.vector.tensor_tensor(gp[:, :, 2, :], g4, gp[:, :, 1, :], ALU.subtract).then_inc(gates, 1)
                yield

            def hidden(b, k):
                _, _, _, dst, func = HIDDEN[b][k]
                if func == "times":
                    dve.wait_ge(h_act, by_act(b, k))
                    dve.wait_ge(h_mm, b * N_HIDDEN + k + 1)
                    nc.vector.tensor_tensor(HB[:, dst, :], HB[:, dst, :], bank(H_BANKS[(b * N_HIDDEN + k) % 4]), ALU.mult)\
                        .then_inc(h_times, 1)

            def outputs(b, t):
                if t == 0:
                    dve.wait_ge(base_ready, b + 1)
                dve.wait_ge(y_mm, TB * b + t + 1)
                xt = X[:, TB * b + t, KEEP:D]
                for e in range(E0):
                    ins = nc.vector.scalar_tensor_tensor(out=xt, in0=bank(OUT_BANKS[t % 2], P, OC, OC * e),
                                                         scalar=G[:, b, 5, t, e:e + 1], in1=xt,
                                                         op0=ALU.mult, op1=ALU.add)
                    if e < E0 - 1:
                        link(ins)
                    else:
                        ins.then_inc(y_used, 1)

            def gate_rows(b):
                dve.wait_ge(gT_mm, b + 1)
                if b:
                    dve.wait_ge(spread_mm, 4 * b)
                nc.vector.tensor_copy(gT[:, :], bank16(GT_BANK)[0:3 * E1, 0:S]).then_inc(gT_ready, 1)

            def spread(b, cs):
                for c in cs:
                    dve.wait_ge(h1_act, 4 * b + c + 1)
                    dve.wait_ge(spread_mm, 4 * b + c + 1)
                    hc = HB[:, 4 * b + c, :]
                    nc.vector.tensor_tensor(hc, hc, bank(H_BANKS[c]), ALU.mult).then_inc(h1_gated, 1)

            def finish(b):
                dve.wait_ge(y1_mm, b + 1)
                ts = tiles(b)
                nc.vector.tensor_tensor(X[:, ts, :], X[:, ts, :], bank(TAIL_BANK).rearrange("p (t d) -> p t d", t=TB), ALU.add)\
                    .then_inc(x_final, 1)

            nc.vector.memset(eps_ln[:, :], LN_EPS)
            nc.vector.memset(eps_rms[:, :], RMS_EPS).then_inc(eps_set, 1)
            nc.vector.memset(ones_b[:, :], 1.0).then_inc(ones_ready, 1)
            nc.vector.memset(PS[:, PV_BANK:PV_BANK + 1, :], 0.0).then_inc(pv_cleared, 1)
            first, second = prep_cross0(0), prep_cross0(1)
            next(first)
            for _ in range(2):
                next(first)
            dve.wait_ge(in_vec, 16)
            nc.vector.tensor_scalar(V("x0_bq"), V("x0_bq"), HD ** -0.5, None, ALU.mult)
            nc.vector.tensor_scalar(V("qn"), V("qn"), HD ** -0.5, None, ALU.mult).then_inc(vec_scaled, 1)
            split(SP_K0, P, B * SC)
            dve.wait_ge(in_const, 16)
            nc.vector.tensor_copy(ident_b[:, :], ident).then_inc(consts_cast, 1)
            next(second)
            dve.wait_ge(in_mask, 32)
            nc.vector.tensor_scalar(sub_z, sub_i, 0.0, NEG, ALU.is_equal, ALU.mult)
            link(nc.vector.tensor_scalar(pad_z, pad_i.rearrange("p (b k) -> p b k", b=B), 0.0, NEG, ALU.is_equal, ALU.mult))
            nc.vector.tensor_tensor(msk[:, 0, :, :], sub_z, pad_z[:, 0, :].unsqueeze(1).to_broadcast([P, TB, SC]), ALU.min)\
                .then_inc(mask_ready, 1)
            run_all(first)
            for _ in range(2):
                next(second)
            nc.vector.tensor_tensor(msk[:, 1, :, :], sub_z, pad_z[:, 1, :].unsqueeze(1).to_broadcast([P, TB, SC]), ALU.min)\
                .then_inc(mask_ready, 1)
            dve.wait_ge(ctx_mm, 3)
            dve.wait_ge(in_bv, 16)
            dve.wait_ge(pool_fills, FILL_V)
            bias = bv_b[0:KT, :].rearrange("p (h d) -> p h d", d=HD)
            for b in range(B):
                for j in range(2):
                    nc.vector.tensor_copy(V1[:, b, j, :, 0:HD],
                                          bank(T_BANKS[1], KT, KV * HD, KV * HD * (2 * b + j)).rearrange("p (h d) -> p h d", d=HD))
                    last = nc.vector.tensor_tensor(V0[:, b, j, :, 0:HD],
                                                   bank(PV_BANK, KT, D, D * (2 * b + j)).rearrange("p (h d) -> p h d", d=HD), bias, ALU.add)
            link(last)
            for b in range(B):
                nc.vector.memset(V0[0:OVER, b, 1, :, :], 0.0)
                last = nc.vector.memset(V1[0:OVER, b, 1, :, :], 0.0)
            last.then_inc(ctx_v, 1)

            def keys1():
                split(SP_K1, KV * HD, B * SC)
                yield
                nc.vector.tensor_copy(causal_b[:, :], C("causal"))
                nc.vector.tensor_copy(causal_tb[:, :], C("causal_t"))
                nc.vector.tensor_copy(spread_b[:, :], C("spread")[0:3 * E1, :]).then_inc(consts_cast, 1)
                yield

            run_slots(FIRST_SLOTS, attention_slot, [(START_QUERIES1, second), (START_KEYS1, keys1()), (START_SELF[0], prep_self(0)), (START_SELF[1], prep_self(1)),
                                              (START_FFN0, ffn0_in(0))])
            run_ffn0(hidden, outputs, attention_slot, ffn0_in(1), prep_cross1(0))
            run_slots(LAST_SLOTS[TB:], attention_slot, [(START_CROSS1, prep_cross1(1)), (START_FFN1, ffn1_in(0))])
            gate_work = ffn1_in(1)
            next(gate_work)
            run_ffn1(gate_work, gate_rows=gate_rows, spread=spread, finish=finish)


def shape_constants():
    c = np.zeros((P, N_CONST), np.float32)

    def put(name, a):
        at, n = CONST[name]
        c[:a.shape[0], at:at + n] = a

    i = np.arange(P)
    put("ident", np.eye(P))
    put("head_mean", (i[:, None] % H == i[None, :] % H) / HD)
    put("causal", np.where(i[None, :] > i[:, None], NEG, 0.0))
    put("causal_t", np.where(i[:, None] > i[None, :], NEG, 0.0))
    for name, E in (("before0", E0), ("before1", E1)):
        e = np.arange(E)
        put(name, np.tile((e[None, :] < e[:, None]).reshape(1, -1), (P, 1)))
    r, col = np.arange(3 * E1), np.arange(4 * P)
    put("spread", r[:, None] % E1 == col[None, :] // HE)
    return c


def kernel(**inputs):
    import concourse.bacc as bacc
    from concourse.bass_utils import run_bass_kernel_spmd

    a = {k: np.asarray(v) for k, v in inputs.items()}

    def chunks(w):
        return np.concatenate([w[P * i:P * i + P] for i in range(w.shape[0] // P)], axis=1)

    def by_feature(w, heads=H):
        return w.reshape(w.shape[0], heads, HD).transpose(0, 2, 1).reshape(w.shape[0], heads * HD)

    def vector_by_feature(v):
        return v.reshape(H, HD).T.reshape(-1)

    f0, f1 = "L0_ffn_", "L1_ffn_"
    packed = {
        "ctx": a["ctx_1024"].transpose(2, 0, 1).reshape(D, B * SC),
        "x0_k": by_feature(a["L0_xattn_Wk"].T), "x0_v": a["L0_xattn_Wv"].T, "x0_q": by_feature(a["L0_xattn_Wq"].T),
        "x1_k": by_feature(a["L1_xattn_W_k"], KV), "x1_v": a["L1_xattn_W_v"],
        "wq": by_feature(a[f0 + "wq"].T), "wk": by_feature(a[f0 + "wk"].T), "wv": a[f0 + "wv"].T, "wo": a[f0 + "wo"].T,
        "gate0": a[f0 + "gate_w"].T,
        "e1_w1": a[f0 + "e1_w1"].T, "e1_w2": a[f0 + "e1_w2"].T, "e0_up": a[f0 + "e0_up"].T,
        "e3_down": a[f0 + "e3_down"].T, "e2_l1": a[f0 + "e2_l1"].T, "e3_up": a[f0 + "e3_up"].T,
        "e2_l2": chunks(a[f0 + "e2_l2"].T), "e2_l3": chunks(a[f0 + "e2_l3"].T),
        "e0_down": chunks(a[f0 + "e0_down"].T), "e1_down": chunks(a[f0 + "e1_down"].T),
        "e2_l4": chunks(a[f0 + "e2_l4"].T), "e3_out": chunks(a[f0 + "e3_out"].T),
        "x1_q": by_feature(a["L1_xattn_W_q"]), "x1_o": a["L1_xattn_W_o"],
        "gate1": a[f1 + "gate_W"],
        "w1": a[f1 + "W1"].transpose(1, 0, 2).reshape(D, E1 * HE),
        "w2": chunks(a[f1 + "W2"].reshape(E1 * HE, D)),
        "ws1": a[f1 + "Ws1"],
    }
    vectors = {
        "x0_bq": vector_by_feature(a["L0_xattn_bq"]), "x0_bk": vector_by_feature(a["L0_xattn_bk"]),
        "n1": a[f0 + "n1_w"], "n2": a[f0 + "n2_w"],
        "qn": np.repeat(a[f0 + "qn_w"], H), "kn": np.repeat(a[f0 + "kn_w"], H),
        **{f"b1_{c}": a[f1 + "b1"].reshape(-1)[P * c:P * c + P] for c in range(4)},
    }
    arrays = {
        "early": np.concatenate([packed[n] for n in EARLY], axis=1),
        "late": np.concatenate([packed[n] for n in LATE], axis=1),
        "consts": shape_constants(),
        "vecs": np.stack([vectors[n] for n in VECS], axis=1),
        "bs1": a[f1 + "bs1"].reshape(HE, 1), "ws2": a[f1 + "Ws2"], "b2": a[f1 + "b2"],
        "bs2": a[f1 + "bs2"].reshape(1, D), "bv": a["L0_xattn_bv"],
        "rscale": a[f1 + "route_scale"].reshape(1),
        "pad_mask": a["mask_Bx1x1xS2_ik0"].reshape(B * SC),
        "sub_mask": a["mask_1x1xSxS2_ik0"].reshape(S, SC),
        "x": a["x"],
    }
    nc = bacc.Bacc("TRN2", target_bir_lowering=False, num_devices=1)
    arrays = {f"in_{k}": np.ascontiguousarray(v) for k, v in arrays.items()}
    args = [nc.dram_tensor(k, v.shape, mybir.dt.from_np(v.dtype), kind="ExternalInput").ap() for k, v in arrays.items()]
    out = nc.dram_tensor("out_x", (B, S, D), F32, kind="ExternalOutput").ap()
    build(nc, *args, out)
    r = run_bass_kernel_spmd(nc, [arrays], core_ids=[0])
    return r.results[0]["out_x"]
```
